# Optimizing a Trainium2 kernel written in Bass

```python
import numpy as np
import jax
import jax.numpy as jnp

def _softmax(x, axis=-1):
    return jax.nn.softmax(x, axis=axis)

def _gelu(x):
    return jax.nn.gelu(x, approximate=True)

def _silu(x):
    return jax.nn.silu(x)

def _sigmoid(x):
    return jax.nn.sigmoid(x)

def _layernorm(x, axis=-1, eps=1e-05):
    m = jnp.mean(x, axis=axis, keepdims=True)
    v = jnp.var(x, axis=axis, keepdims=True)
    return (x - m) / jnp.sqrt(v + eps)

def _scatter_add(tgt, idx, src, axis=0):
    return tgt.at[idx].add(src)

def _segment_sum(src, seg, n):
    return jax.ops.segment_sum(src, seg, n)
kernel_name = 'mk_lm_tower_d2_tok_ids512_r4_344c06'

def setup_inputs(seed: int=0):
    np.random.seed(seed)
    _w = jnp.asarray

    def _rec_inputs():
        import jax
        import jax.numpy as jnp
        _rk = jax.random.key(seed)
        x = jax.random.randint(jax.random.fold_in(_rk, 1), (32, 256), 0, 32001, jnp.int32)
        return x
    x = _rec_inputs()

    def _L0_tok_setup():
        import math
        import jax, jax.numpy as jnp
        import numpy as np
        B, T, C, DEPTH = (16, 512, 128, 4)
        VOCAB = 8000
        MAX_DURATION = 1024

        def _sinusoidal_position_embedding(length, dim):
            pos = np.arange(length, dtype=np.float64)[:, None]
            freqs = np.exp(-math.log(10000.0) * np.arange(0, dim, 2, dtype=np.float64) / dim)
            ang = pos * freqs
            pe = np.stack([np.sin(ang), np.cos(ang)], axis=-1).reshape(length, dim)
            return pe

        def _build_pos_embedding(embedding_dim):
            pe = _sinusoidal_position_embedding(MAX_DURATION, embedding_dim + 2)
            d = (embedding_dim + 2) // 2
            pe = pe.reshape(MAX_DURATION, d, 2).transpose(0, 2, 1)
            pe = pe[:, ::-1]
            pe = pe[..., :-1]
            pe = pe.reshape(MAX_DURATION, -1)
            return jnp.asarray(pe, dtype=jnp.float32)

        def _layernorm(x, g, b, eps=1e-06):
            mu = jnp.mean(x, axis=-1, keepdims=True)
            var = jnp.mean(jnp.square(x - mu), axis=-1, keepdims=True)
            return (x - mu) * jax.lax.rsqrt(var + eps) * g + b

        def _grn(x, w, b):
            g = jnp.sqrt(jnp.sum(x * x, axis=1, keepdims=True))
            norm = g / (jnp.mean(g, axis=-1, keepdims=True) + 1e-06)
            return w * (x * norm) + b + x

        def _block(x, cw, cb, lg, lb, W1, B1, gw, gb, W2, B2):
            identity = x
            h = jnp.transpose(x, (0, 2, 1))
            h = jax.lax.conv_general_dilated(h, cw, window_strides=(1,), padding=[(3, 3)], feature_group_count=C, dimension_numbers=('NCH', 'OIH', 'NCH'))
            h = h + cb[None, :, None]
            h = jnp.transpose(h, (0, 2, 1))
            h = _layernorm(h, lg, lb)
            h = jnp.einsum('btc,cd->btd', h, W1) + B1
            h = jax.nn.gelu(h, approximate=False)
            h = _grn(h, gw, gb)
            h = jnp.einsum('btd,dc->btc', h, W2) + B2
            return identity + h
        key = jax.random.key(seed)
        ks = jax.random.split(key, 12)
        s = 0.02
        inp = {'tokens': jax.random.randint(ks[0], (B, T), 0, VOCAB + 1), 'emb_table': jax.random.normal(ks[1], (VOCAB + 1, C), jnp.float32) * s, 'pos_emb': _build_pos_embedding(C), 'conv_w': jax.random.normal(ks[2], (DEPTH, C, 1, 7), jnp.float32) * s, 'conv_b': jnp.zeros((DEPTH, C), jnp.float32), 'ln_g': jnp.ones((DEPTH, C), jnp.float32), 'ln_b': jnp.zeros((DEPTH, C), jnp.float32), 'w1': jax.random.normal(ks[3], (DEPTH, C, 2 * C), jnp.float32) * s, 'b1': jnp.zeros((DEPTH, 2 * C), jnp.float32), 'grn_w': jnp.ones((DEPTH, 2 * C), jnp.float32), 'grn_b': jnp.zeros((DEPTH, 2 * C), jnp.float32), 'w2': jax.random.normal(ks[4], (DEPTH, 2 * C, C), jnp.float32) * s, 'b2': jnp.zeros((DEPTH, C), jnp.float32)}
        return inp
    _L0_tok_all = _L0_tok_setup()
    _L0_tok_in = {k: v for k, v in _L0_tok_all.items() if k in ('emb_table', 'pos_emb', 'conv_w', 'conv_b', 'ln_g', 'ln_b', 'w1', 'b1', 'grn_w', 'grn_b', 'w2', 'b2')}
    del _L0_tok_all

    def _L0_attn_setup():
        import jax, jax.numpy as jnp
        import numpy as np
        import math
        B_, T_, D_, S_, K_ = (4, 2048, 128, 64, 5)
        R_MIN, R_MAX, PHASE_MAX = (0.8, 0.99, 2.0 * math.pi)

        def _layernorm(x, w, b, eps=1e-05):
            mu = jnp.mean(x, axis=-1, keepdims=True)
            var = jnp.mean(jnp.square(x - mu), axis=-1, keepdims=True)
            return (x - mu) * jax.lax.rsqrt(var + eps) * w + b

        def _binop_diag(a, b):
            a_l, a_s = a
            b_l, b_s = b
            return (a_l * b_l, b_l * a_s + b_s)
        key = jax.random.key(seed)
        ks = jax.random.split(key, 12)
        x = jax.random.normal(ks[0], (B_, T_, D_), dtype=jnp.float32)
        ln_w = jnp.ones((D_,), jnp.float32)
        ln_b = jnp.zeros((D_,), jnp.float32)
        W_in = jax.random.normal(ks[1], (2 * S_, D_), jnp.float32) / math.sqrt(D_)
        conv_w = jax.random.normal(ks[2], (S_, S_, K_), jnp.float32) / math.sqrt(S_ * K_)
        conv_b = jnp.zeros((S_,), jnp.float32)
        u1 = jax.random.uniform(ks[3], (S_,), jnp.float32)
        nu_log = jnp.log(-0.5 * jnp.log(u1 * (R_MAX + R_MIN) * (R_MAX - R_MIN) + R_MIN ** 2))
        u2 = jax.random.uniform(ks[4], (S_,), jnp.float32)
        theta_log = jnp.log(PHASE_MAX * u2)
        L_mod = jnp.exp(-jnp.exp(nu_log))
        gamma_log = jnp.log(jnp.sqrt(1.0 - jnp.square(L_mod)))
        B_re = jax.random.normal(ks[5], (S_, S_), jnp.float32) / math.sqrt(2 * S_)
        B_im = jax.random.normal(ks[6], (S_, S_), jnp.float32) / math.sqrt(2 * S_)
        C_re = jax.random.normal(ks[7], (S_, S_), jnp.float32) / math.sqrt(S_)
        C_im = jax.random.normal(ks[8], (S_, S_), jnp.float32) / math.sqrt(S_)
        W_out = jax.random.normal(ks[9], (D_, S_), jnp.float32) / math.sqrt(S_)
        b_out = jnp.zeros((D_,), jnp.float32)
        return dict(x=x, ln_w=ln_w, ln_b=ln_b, W_in=W_in, conv_w=conv_w, conv_b=conv_b, nu_log=nu_log, theta_log=theta_log, gamma_log=gamma_log, B_re=B_re, B_im=B_im, C_re=C_re, C_im=C_im, W_out=W_out, b_out=b_out)
    _L0_attn_all = _L0_attn_setup()
    _L0_attn_in = {k: v for k, v in _L0_attn_all.items() if k in ('ln_w', 'ln_b', 'W_in', 'conv_w', 'conv_b', 'nu_log', 'theta_log', 'gamma_log', 'B_re', 'B_im', 'C_re', 'C_im', 'W_out', 'b_out')}
    del _L0_attn_all

    def _L0_ffn_setup():
        import jax, jax.numpy as jnp
        import numpy as np
        D, H, E, B, S = (128, 512, 16, 8, 2048)
        MAX_GROUP_SIZE = 1024
        MIN_CAPACITY = 8
        CAPACITY_FACTOR = 1.0

        def _group_dims(num_tokens, num_experts):
            num_groups = -(-num_tokens // MAX_GROUP_SIZE)
            while num_tokens % num_groups != 0 or num_groups % num_experts != 0:
                num_groups += 1
            return (num_tokens // num_groups, num_groups)
        key = jax.random.key(seed)
        ks = jax.random.split(key, 6)
        s = 0.02
        return {'x': jax.random.normal(ks[0], (B, S, D), jnp.float32), 'gate_w': jax.random.normal(ks[1], (D, E), jnp.float32) * s, 'w1': jax.random.normal(ks[2], (E, D, H), jnp.float32) * s, 'b1': jnp.zeros((E, H), jnp.float32), 'w2': jax.random.normal(ks[3], (E, H, D), jnp.float32) * s, 'b2': jnp.zeros((E, D), jnp.float32), 'sw1': jax.random.normal(ks[4], (D, H), jnp.float32) * s, 'sb1': jnp.zeros((H,), jnp.float32), 'sw2': jax.random.normal(ks[5], (H, D), jnp.float32) * s, 'sb2': jnp.zeros((D,), jnp.float32)}
    _L0_ffn_all = _L0_ffn_setup()
    _L0_ffn_in = {k: v for k, v in _L0_ffn_all.items() if k in ('gate_w', 'w1', 'b1', 'w2', 'b2', 'sw1', 'sb1', 'sw2', 'sb2')}
    del _L0_ffn_all

    def _L1_attn_setup():
        import jax, jax.numpy as jnp
        import numpy as np
        N, L, C = (4, 1024, 128)
        H = 8
        D = C // H
        KS = 9
        INV_PI = 1.0 / np.pi
        SCALE = H ** (-0.5)

        def _l2norm(t):
            return t / jnp.linalg.norm(t, axis=-1, keepdims=True)
        key = jax.random.key(seed)
        ks = jax.random.split(key, 6)
        s = 0.02
        return {'x': jax.random.normal(ks[0], (N, L, C), dtype=jnp.float32), 'w_qkv': jax.random.normal(ks[1], (C, 3 * C), dtype=jnp.float32) * s, 'b_qkv': jax.random.normal(ks[2], (3 * C,), dtype=jnp.float32) * s, 'w_dconv': jax.random.normal(ks[3], (H, 1, KS, 1), dtype=jnp.float32) * s, 'w_proj': jax.random.normal(ks[4], (C, C), dtype=jnp.float32) * s, 'b_proj': jax.random.normal(ks[5], (C,), dtype=jnp.float32) * s}
    _L1_attn_all = _L1_attn_setup()
    _L1_attn_in = {k: v for k, v in _L1_attn_all.items() if k in ('w_qkv', 'b_qkv', 'w_dconv', 'w_proj', 'b_proj')}
    del _L1_attn_all

    def _L1_ffn_setup():
        import jax, jax.numpy as jnp
        import numpy as np
        import math
        E, K, CAPF = (8, 2, 1.25)
        D, DFF = (128, 512)

        def _moe(x, Wr, br, W1, b1, W2, b2):
            orig = x.shape
            d = orig[-1]
            xf = x.reshape(-1, d)
            N = xf.shape[0]
            logits = xf @ Wr + br
            probs = jax.nn.softmax(logits, axis=-1)
            topk_p, topk_i = jax.lax.top_k(probs, K)
            topk_w = topk_p / (jnp.sum(topk_p, axis=-1, keepdims=True) + 1e-09)
            cap = max(1, int(math.ceil(CAPF * float(N * K) / float(E))))
            flat_e = topk_i.reshape(-1)
            flat_w = topk_w.reshape(-1)
            tok = jnp.repeat(jnp.arange(N), K)
            one_hot = jax.nn.one_hot(flat_e, E, dtype=xf.dtype)
            pos = (jnp.cumsum(one_hot, axis=0) - one_hot)[jnp.arange(N * K), flat_e]
            pos = pos.astype(jnp.int32)
            keep = pos < cap
            w_k = jnp.where(keep, flat_w, 0.0)
            sum_w = jnp.zeros((N,), xf.dtype).at[tok].add(w_k)
            w_norm = w_k / (sum_w[tok] + 1e-09)
            slot = flat_e * cap + pos
            slot_safe = jnp.where(keep, slot, E * cap)
            expert_in = jnp.zeros((E * cap, d), xf.dtype).at[slot_safe].set(xf[tok], mode='drop').reshape(E, cap, d)
            h = jax.nn.gelu(jnp.einsum('ecd,edf->ecf', expert_in, W1) + b1[:, None, :], approximate=False)
            expert_out = (jnp.einsum('ecf,efd->ecd', h, W2) + b2[:, None, :]).reshape(E * cap, d)
            contrib = expert_out[jnp.where(keep, slot, 0)]
            y = jnp.zeros((N, d), xf.dtype).at[tok].add(contrib * w_norm[:, None])
            return y.reshape(orig)
        key = jax.random.key(seed)
        ks = jax.random.split(key, 5)
        s = lambda k, sh, sc: jax.random.normal(k, sh, jnp.float32) * sc
        return {'x': jax.random.normal(ks[0], (8, 1024, D), jnp.float32), 'Wr': s(ks[1], (D, E), 1.0 / math.sqrt(D)), 'br': jnp.zeros((E,), jnp.float32), 'W1': s(ks[2], (E, D, DFF), 1.0 / math.sqrt(D)), 'b1': jnp.zeros((E, DFF), jnp.float32), 'W2': s(ks[3], (E, DFF, D), 1.0 / math.sqrt(DFF)), 'b2': jnp.zeros((E, D), jnp.float32)}
    _L1_ffn_all = _L1_ffn_setup()
    _L1_ffn_in = {k: v for k, v in _L1_ffn_all.items() if k in ('Wr', 'br', 'W1', 'b1', 'W2', 'b2')}
    del _L1_ffn_all
    return {'x': x, 'L0_tok_emb_table': _L0_tok_in['emb_table'], 'L0_tok_pos_emb': _L0_tok_in['pos_emb'], 'L0_tok_conv_w': _L0_tok_in['conv_w'], 'L0_tok_conv_b': _L0_tok_in['conv_b'], 'L0_tok_ln_g': _L0_tok_in['ln_g'], 'L0_tok_ln_b': _L0_tok_in['ln_b'], 'L0_tok_w1': _L0_tok_in['w1'], 'L0_tok_b1': _L0_tok_in['b1'], 'L0_tok_grn_w': _L0_tok_in['grn_w'], 'L0_tok_grn_b': _L0_tok_in['grn_b'], 'L0_tok_w2': _L0_tok_in['w2'], 'L0_tok_b2': _L0_tok_in['b2'], 'L0_attn_ln_w': _L0_attn_in['ln_w'], 'L0_attn_ln_b': _L0_attn_in['ln_b'], 'L0_attn_W_in': _L0_attn_in['W_in'], 'L0_attn_conv_w': _L0_attn_in['conv_w'], 'L0_attn_conv_b': _L0_attn_in['conv_b'], 'L0_attn_nu_log': _L0_attn_in['nu_log'], 'L0_attn_theta_log': _L0_attn_in['theta_log'], 'L0_attn_gamma_log': _L0_attn_in['gamma_log'], 'L0_attn_B_re': _L0_attn_in['B_re'], 'L0_attn_B_im': _L0_attn_in['B_im'], 'L0_attn_C_re': _L0_attn_in['C_re'], 'L0_attn_C_im': _L0_attn_in['C_im'], 'L0_attn_W_out': _L0_attn_in['W_out'], 'L0_attn_b_out': _L0_attn_in['b_out'], 'L0_ffn_gate_w': _L0_ffn_in['gate_w'], 'L0_ffn_w1': _L0_ffn_in['w1'], 'L0_ffn_b1': _L0_ffn_in['b1'], 'L0_ffn_w2': _L0_ffn_in['w2'], 'L0_ffn_b2': _L0_ffn_in['b2'], 'L0_ffn_sw1': _L0_ffn_in['sw1'], 'L0_ffn_sb1': _L0_ffn_in['sb1'], 'L0_ffn_sw2': _L0_ffn_in['sw2'], 'L0_ffn_sb2': _L0_ffn_in['sb2'], 'L1_attn_w_qkv': _L1_attn_in['w_qkv'], 'L1_attn_b_qkv': _L1_attn_in['b_qkv'], 'L1_attn_w_dconv': _L1_attn_in['w_dconv'], 'L1_attn_w_proj': _L1_attn_in['w_proj'], 'L1_attn_b_proj': _L1_attn_in['b_proj'], 'L1_ffn_Wr': _L1_ffn_in['Wr'], 'L1_ffn_br': _L1_ffn_in['br'], 'L1_ffn_W1': _L1_ffn_in['W1'], 'L1_ffn_b1': _L1_ffn_in['b1'], 'L1_ffn_W2': _L1_ffn_in['W2'], 'L1_ffn_b2': _L1_ffn_in['b2']}

def reference(x, L0_tok_emb_table, L0_tok_pos_emb, L0_tok_conv_w, L0_tok_conv_b, L0_tok_ln_g, L0_tok_ln_b, L0_tok_w1, L0_tok_b1, L0_tok_grn_w, L0_tok_grn_b, L0_tok_w2, L0_tok_b2, L0_attn_ln_w, L0_attn_ln_b, L0_attn_W_in, L0_attn_conv_w, L0_attn_conv_b, L0_attn_nu_log, L0_attn_theta_log, L0_attn_gamma_log, L0_attn_B_re, L0_attn_B_im, L0_attn_C_re, L0_attn_C_im, L0_attn_W_out, L0_attn_b_out, L0_ffn_gate_w, L0_ffn_w1, L0_ffn_b1, L0_ffn_w2, L0_ffn_b2, L0_ffn_sw1, L0_ffn_sb1, L0_ffn_sw2, L0_ffn_sb2, L1_attn_w_qkv, L1_attn_b_qkv, L1_attn_w_dconv, L1_attn_w_proj, L1_attn_b_proj, L1_ffn_Wr, L1_ffn_br, L1_ffn_W1, L1_ffn_b1, L1_ffn_W2, L1_ffn_b2):
    import jax
    import jax.numpy as jnp

    def _L0_tok_ref(tokens, emb_table, pos_emb, conv_w, conv_b, ln_g, ln_b, w1, b1, grn_w, grn_b, w2, b2):
        import math
        import jax, jax.numpy as jnp
        import numpy as np
        B, T, C, DEPTH = (16, 512, 128, 4)
        VOCAB = 8000
        MAX_DURATION = 1024

        def _sinusoidal_position_embedding(length, dim):
            pos = np.arange(length, dtype=np.float64)[:, None]
            freqs = np.exp(-math.log(10000.0) * np.arange(0, dim, 2, dtype=np.float64) / dim)
            ang = pos * freqs
            pe = np.stack([np.sin(ang), np.cos(ang)], axis=-1).reshape(length, dim)
            return pe

        def _build_pos_embedding(embedding_dim):
            pe = _sinusoidal_position_embedding(MAX_DURATION, embedding_dim + 2)
            d = (embedding_dim + 2) // 2
            pe = pe.reshape(MAX_DURATION, d, 2).transpose(0, 2, 1)
            pe = pe[:, ::-1]
            pe = pe[..., :-1]
            pe = pe.reshape(MAX_DURATION, -1)
            return jnp.asarray(pe, dtype=jnp.float32)

        def _layernorm(x, g, b, eps=1e-06):
            mu = jnp.mean(x, axis=-1, keepdims=True)
            var = jnp.mean(jnp.square(x - mu), axis=-1, keepdims=True)
            return (x - mu) * jax.lax.rsqrt(var + eps) * g + b

        def _grn(x, w, b):
            g = jnp.sqrt(jnp.sum(x * x, axis=1, keepdims=True))
            norm = g / (jnp.mean(g, axis=-1, keepdims=True) + 1e-06)
            return w * (x * norm) + b + x

        def _block(x, cw, cb, lg, lb, W1, B1, gw, gb, W2, B2):
            identity = x
            h = jnp.transpose(x, (0, 2, 1))
            h = jax.lax.conv_general_dilated(h, cw, window_strides=(1,), padding=[(3, 3)], feature_group_count=C, dimension_numbers=('NCH', 'OIH', 'NCH'))
            h = h + cb[None, :, None]
            h = jnp.transpose(h, (0, 2, 1))
            h = _layernorm(h, lg, lb)
            h = jnp.einsum('btc,cd->btd', h, W1) + B1
            h = jax.nn.gelu(h, approximate=False)
            h = _grn(h, gw, gb)
            h = jnp.einsum('btd,dc->btc', h, W2) + B2
            return identity + h
        t = tokens.shape[1]
        x = emb_table[tokens] + pos_emb[:t][None]
        for i in range(DEPTH):
            x = _block(x, conv_w[i], conv_b[i], ln_g[i], ln_b[i], w1[i], b1[i], grn_w[i], grn_b[i], w2[i], b2[i])
        return x

    def _L0_attn_ref(x, ln_w, ln_b, W_in, conv_w, conv_b, nu_log, theta_log, gamma_log, B_re, B_im, C_re, C_im, W_out, b_out):
        import jax, jax.numpy as jnp
        import numpy as np
        import math
        B_, T_, D_, S_, K_ = (4, 2048, 128, 64, 5)
        R_MIN, R_MAX, PHASE_MAX = (0.8, 0.99, 2.0 * math.pi)

        def _layernorm(x, w, b, eps=1e-05):
            mu = jnp.mean(x, axis=-1, keepdims=True)
            var = jnp.mean(jnp.square(x - mu), axis=-1, keepdims=True)
            return (x - mu) * jax.lax.rsqrt(var + eps) * w + b

        def _binop_diag(a, b):
            a_l, a_s = a
            b_l, b_s = b
            return (a_l * b_l, b_l * a_s + b_s)
        r = x
        h = _layernorm(x, ln_w, ln_b)
        h = h @ W_in.T
        xg, v = jnp.split(h, 2, axis=-1)
        pad = (K_ - 1) // 2
        vc = jax.lax.conv_general_dilated(v.transpose(0, 2, 1), conv_w, window_strides=(1,), padding=[(pad, pad)], dimension_numbers=('NCH', 'OIH', 'NCH'))
        v = vc.transpose(0, 2, 1) + conv_b
        L_mod = jnp.exp(-jnp.exp(nu_log))
        theta = jnp.exp(theta_log)
        Lam = (L_mod * jnp.cos(theta) + 1j * (L_mod * jnp.sin(theta))).astype(jnp.complex64)
        Bn = (B_re + 1j * B_im).astype(jnp.complex64) * jnp.exp(gamma_log)[:, None]
        Be = v.astype(jnp.complex64) @ Bn.T
        L_el = jnp.broadcast_to(Lam, Be.shape)
        _, states = jax.lax.associative_scan(_binop_diag, (L_el, Be), axis=1)
        Cc = (C_re + 1j * C_im).astype(jnp.complex64)
        y = (states @ Cc.T).real
        out = jax.nn.gelu(xg, approximate=False) * y
        return out @ W_out.T + b_out + r

    def _L0_ffn_ref(x, gate_w, w1, b1, w2, b2, sw1, sb1, sw2, sb2):
        import jax, jax.numpy as jnp
        import numpy as np
        D, H, E, B, S = (128, 512, 16, 8, 2048)
        MAX_GROUP_SIZE = 1024
        MIN_CAPACITY = 8
        CAPACITY_FACTOR = 1.0

        def _group_dims(num_tokens, num_experts):
            num_groups = -(-num_tokens // MAX_GROUP_SIZE)
            while num_tokens % num_groups != 0 or num_groups % num_experts != 0:
                num_groups += 1
            return (num_tokens // num_groups, num_groups)
        Bn, Sn, Dn = x.shape
        En = gate_w.shape[1]
        T = Bn * Sn
        group_size, num_groups = _group_dims(T, En)
        cap = max(int(round(CAPACITY_FACTOR * group_size * num_groups / En)), MIN_CAPACITY)
        xg = x.reshape(num_groups, group_size, Dn)
        logits = jnp.einsum('gsd,de->gse', xg, gate_w)
        probs = jax.nn.softmax(logits, axis=-1)
        flat_probs = probs.transpose(2, 0, 1).reshape(En, T)
        scores, tok_idx = jax.lax.top_k(flat_probs, cap)
        xf = x.reshape(T, Dn)
        toks = xf[tok_idx]
        h = jax.nn.gelu(jnp.einsum('ecd,edh->ech', toks, w1) + b1[:, None, :])
        y = jnp.einsum('ech,ehd->ecd', h, w2) + b2[:, None, :]
        y = y * scores[..., None]
        routed = jnp.zeros_like(xf).at[tok_idx.reshape(-1)].add(y.reshape(-1, Dn))
        shared = jax.nn.gelu(xf @ sw1 + sb1) @ sw2 + sb2
        out = (routed + shared).reshape(Bn, Sn, Dn)
        return out

    def _L1_attn_ref(x, w_qkv, b_qkv, w_dconv, w_proj, b_proj):
        import jax, jax.numpy as jnp
        import numpy as np
        N, L, C = (4, 1024, 128)
        H = 8
        D = C // H
        KS = 9
        INV_PI = 1.0 / np.pi
        SCALE = H ** (-0.5)

        def _l2norm(t):
            return t / jnp.linalg.norm(t, axis=-1, keepdims=True)
        n, l, c = x.shape
        qkv = x @ w_qkv + b_qkv
        qkv = qkv.reshape(n, l, 3, H, D).transpose(2, 0, 3, 1, 4)
        q, k, v = (qkv[0], qkv[1], qkv[2])
        q = _l2norm(q)
        k = _l2norm(k)
        pad = KS // 2
        dconv_v = jax.lax.conv_general_dilated(v, w_dconv, window_strides=(1, 1), padding=((pad, pad), (0, 0)), dimension_numbers=('NCHW', 'OIHW', 'NCHW'), feature_group_count=H)
        attn = jnp.einsum('nhld,nhle->nhde', k, v)
        out = 0.5 * v + INV_PI * jnp.einsum('nhld,nhde->nhle', q, attn)
        out = _l2norm(out)
        out = out + dconv_v
        out = out.transpose(0, 2, 1, 3).reshape(n, l, H * D)
        out = out @ w_proj + b_proj
        return out

    def _L1_ffn_ref(x, Wr, br, W1, b1, W2, b2):
        import jax, jax.numpy as jnp
        import numpy as np
        import math
        E, K, CAPF = (8, 2, 1.25)
        D, DFF = (128, 512)

        def _moe(x, Wr, br, W1, b1, W2, b2):
            orig = x.shape
            d = orig[-1]
            xf = x.reshape(-1, d)
            N = xf.shape[0]
            logits = xf @ Wr + br
            probs = jax.nn.softmax(logits, axis=-1)
            topk_p, topk_i = jax.lax.top_k(probs, K)
            topk_w = topk_p / (jnp.sum(topk_p, axis=-1, keepdims=True) + 1e-09)
            cap = max(1, int(math.ceil(CAPF * float(N * K) / float(E))))
            flat_e = topk_i.reshape(-1)
            flat_w = topk_w.reshape(-1)
            tok = jnp.repeat(jnp.arange(N), K)
            one_hot = jax.nn.one_hot(flat_e, E, dtype=xf.dtype)
            pos = (jnp.cumsum(one_hot, axis=0) - one_hot)[jnp.arange(N * K), flat_e]
            pos = pos.astype(jnp.int32)
            keep = pos < cap
            w_k = jnp.where(keep, flat_w, 0.0)
            sum_w = jnp.zeros((N,), xf.dtype).at[tok].add(w_k)
            w_norm = w_k / (sum_w[tok] + 1e-09)
            slot = flat_e * cap + pos
            slot_safe = jnp.where(keep, slot, E * cap)
            expert_in = jnp.zeros((E * cap, d), xf.dtype).at[slot_safe].set(xf[tok], mode='drop').reshape(E, cap, d)
            h = jax.nn.gelu(jnp.einsum('ecd,edf->ecf', expert_in, W1) + b1[:, None, :], approximate=False)
            expert_out = (jnp.einsum('ecf,efd->ecd', h, W2) + b2[:, None, :]).reshape(E * cap, d)
            contrib = expert_out[jnp.where(keep, slot, 0)]
            y = jnp.zeros((N, d), xf.dtype).at[tok].add(contrib * w_norm[:, None])
            return y.reshape(orig)
        return _moe(x, Wr, br, W1, b1, W2, b2)
    h = _L0_tok_ref(x, L0_tok_emb_table, L0_tok_pos_emb, L0_tok_conv_w, L0_tok_conv_b, L0_tok_ln_g, L0_tok_ln_b, L0_tok_w1, L0_tok_b1, L0_tok_grn_w, L0_tok_grn_b, L0_tok_w2, L0_tok_b2)
    h = h + _L0_attn_ref(_layernorm(h, axis=-1), L0_attn_ln_w, L0_attn_ln_b, L0_attn_W_in, L0_attn_conv_w, L0_attn_conv_b, L0_attn_nu_log, L0_attn_theta_log, L0_attn_gamma_log, L0_attn_B_re, L0_attn_B_im, L0_attn_C_re, L0_attn_C_im, L0_attn_W_out, L0_attn_b_out)
    h = h + _L0_ffn_ref(_layernorm(h, axis=-1), L0_ffn_gate_w, L0_ffn_w1, L0_ffn_b1, L0_ffn_w2, L0_ffn_b2, L0_ffn_sw1, L0_ffn_sb1, L0_ffn_sw2, L0_ffn_sb2)
    h = h + _L1_attn_ref(_layernorm(h, axis=-1), L1_attn_w_qkv, L1_attn_b_qkv, L1_attn_w_dconv, L1_attn_w_proj, L1_attn_b_proj)
    h = h + _L1_ffn_ref(_layernorm(h, axis=-1), L1_ffn_Wr, L1_ffn_br, L1_ffn_W1, L1_ffn_b1, L1_ffn_W2, L1_ffn_b2)
    return h

_drawn_inputs = setup_inputs


def setup_inputs(seed=0):
    import zlib

    import numpy as np

    out = dict(_drawn_inputs(seed))
    spreads = {'L0_tok_conv_b': (0.0, 0.1),
     'L0_tok_ln_g': (1.0, 0.2),
     'L0_tok_ln_b': (0.0, 0.1),
     'L0_tok_b1': (0.0, 0.1),
     'L0_tok_grn_w': (1.0, 0.2),
     'L0_tok_grn_b': (0.0, 0.1),
     'L0_tok_b2': (0.0, 0.1),
     'L0_attn_ln_w': (1.0, 0.2),
     'L0_attn_ln_b': (0.0, 0.1),
     'L0_attn_conv_b': (0.0, 0.1),
     'L0_attn_b_out': (0.0, 0.1),
     'L0_ffn_b1': (0.0, 0.771),
     'L0_ffn_b2': (0.0, 0.294),
     'L0_ffn_sb1': (0.0, 0.308),
     'L0_ffn_sb2': (0.0, 0.1),
     'L1_ffn_br': (0.0, 0.1),
     'L1_ffn_b1': (0.0, 0.282),
     'L1_ffn_b2': (0.0, 0.1)}
    factors = {'L0_ffn_w1': 4.875, 'L0_ffn_w2': 4.977, 'L1_attn_w_dconv': 16.854}
    for name, (base, spread) in spreads.items():
        noise = np.random.default_rng([zlib.crc32(name.encode()), seed]).standard_normal(out[name].shape)
        drawn = base * np.exp(spread * noise) if base else spread * noise
        out[name] = jnp.asarray(drawn.astype(out[name].dtype))
    for name, factor in factors.items():
        out[name] = (out[name] * factor).astype(out[name].dtype)
    return out
```

```python
from contextlib import ExitStack

import concourse.bass as bass
from concourse import mybir

F32 = mybir.dt.float32
BF16 = mybir.dt.bfloat16
I32 = mybir.dt.int32
ALU = mybir.AluOpType
ACT = mybir.ActivationFunctionType
AX = mybir.AxisListType.X

P = 128
C = 128
T = 8192
SEQ = 256
UNIT = 1024
NU = T // UNIT
UB = UNIT // SEQ
UT = UNIT // P
NT = T // P
L = 4
KC = 7
VOCAB_ROWS = 8001


class Stage:

    def __init__(self, nc, tag):
        self.nc, self.tag, self.ctx, self.sems = nc, tag, ExitStack(), []

    def __enter__(self):
        self.ctx.__enter__()
        return self

    def __exit__(self, *a):
        self.ctx.__exit__(*a)
        if self.sems and a[0] is None:
            self.nc.clear_and_free_semaphores(self.sems)
            self.nc.all_engine_barrier()

    def sb(self, name, shape, dt=F32):
        return self.ctx.enter_context(self.nc.sbuf_tensor(f"{self.tag}_{name}", shape, dt))

    def pb(self, name, shape, dt=F32):
        return self.ctx.enter_context(self.nc.psum_tensor(f"{self.tag}_{name}", shape, dt))

    def sem(self, name):
        self.sems.append(self.nc.alloc_semaphore(f"{self.tag}_{name}"))
        return self.sems[-1]

    def sem2(self, name):
        return [self.sem(f"{name}{u}") for u in range(2)]

    def block(self):
        return self.ctx.enter_context(self.nc.Block())


def bc(ap, at, n):
    pat = [list(x) for x in ap.ap]
    pat.insert(at, [0, n])
    return bass.AP(tensor=ap.tensor, offset=ap.offset, ap=pat)


def wait_alone(eng, sem, value, tick):
    eng.wait_ge(sem, value)
    eng.sem_inc(tick, 1)


def constants(nc, k):
    with Stage(nc, "cst") as s:
        s_m, s_i, s_d = s.sem("memset"), s.sem("ident"), s.sem("done")
        block = s.block()

        @block.gpsimd
        def _(pool):
            pool.memset(k["ident"][:, :], 0.0)
            pool.memset(k["mean"][:, :], 1.0 / C)
            pool.memset(k["ones"][:, :], 1.0)
            pool.memset(k["nhalf"][:, :], -0.5)
            pool.memset(k["half"][:, :], 0.5)
            pool.memset(k["half_mean"][:, :], 0.5 / C)
            pool.drain()
            pool.affine_select(out=k["ident"][:, :], in_=k["ident"][:, :], compare_op=ALU.not_equal, fill=1.0,
                               base=0, pattern=[[-1, P]], channel_multiplier=1)
            pool.drain()
            pool.tensor_tensor(k["cent"][:, :], k["ident"][:, :], k["mean"][:, :], ALU.subtract)


def token_embedding(nc, k, x, emb, pos, hT):
    with Stage(nc, "emb") as s:
        ids = s.sb("ids", [NT, P], I32)
        idf = s.sb("idf", [NT, P])
        idx = s.sb("idx", [P, NT], I32)
        idc = s.sb("idc", [P, 2, UT], I32)
        rows = s.sb("rows", [P, 2, UT, C])
        posr = s.sb("posr", [P, 2, C])
        posT = s.sb("posT", [P, SEQ])
        ps = s.pb("ps", [P, 2, UNIT])
        ps_pos = s.pb("pspos", [P, SEQ])
        ps_ids = s.pb("psids", [P, NT])
        s_in, s_idf, s_tr, s_idx = s.sem("in"), s.sem("idf"), s.sem("tr"), s.sem("idx")
        s_rows, s_free, s_hT, s_ps = s.sem2("rows"), s.sem2("free"), s.sem2("hT"), s.sem2("ps")
        s_hold = s.sem("hold")
        block = s.block()

        @block.sync
        def _(sp):
            sp.dma_start(ids[:, :], x.rearrange("a (b p) -> (a b) p", p=P)).then_inc(s_in, 16)
            sp.dma_start(posr[:, :, :], pos[0:SEQ, :].rearrange("(a p) c -> p a c", p=P)).then_inc(s_in, 16)

        @block.vector
        def _(dve):
            dve.wait_ge(s_in, 32)
            dve.tensor_scalar(idf[:, :], ids[:, :], float(VOCAB_ROWS - 1), None, ALU.min).then_inc(s_idf, 1)
            dve.wait_ge(s_tr, 1)
            dve.tensor_copy(idx[:, :], ps_ids[:, :])
            dve.tensor_copy(posT[:, :], ps_pos[:, :]).then_inc(s_idx, 1)
            dve.drain()
            with dve.Fori(0, NU // 2) as j:
                for u in range(2):
                    dve.wait_ge(s_ps[u], j + 1)
                    dst = hT[:, bass.ds(j * 2 * UNIT + u * UNIT, UNIT)].rearrange("p (b t) -> p b t", t=SEQ)
                    dve.tensor_tensor(dst, ps[:, u, :].rearrange("p (b t) -> p b t", t=SEQ),
                                      bc(posT[:, :], 1, UB), ALU.add).then_inc(s_hT[u], 1)

        @block.gpsimd
        def _(pool):
            pool.wait_ge(s_idx, 1)
            with pool.Fori(0, NU // 2) as j:
                for u in range(2):
                    pool.wait_ge(s_free[u], j + 1)
                    pool.tensor_copy(idc[:, u, :], idx[:, bass.ds(j * 2 * UT + u * UT, UT)])
                    pool.drain()
                    for t in range(UT):
                        pool.indirect_dma_start(rows[:, u, t, :], None, emb,
                                                bass.IndirectOffsetOnAxis(ap=idc[:, u, t:t + 1], axis=0))\
                            .then_inc(s_rows[u], 16)

        @block.tensor
        def _(pe):
            pe.sem_inc(s_free[0], 1)
            pe.sem_inc(s_free[1], 1)
            pe.wait_ge(s_idf, 1)
            pe.transpose(ps_ids[:, :], idf[:, :], k["ident"][0:NT, 0:NT])
            pe.transpose(ps_pos[:, 0:P], posr[:, 0, :], k["ident"][:, :])
            pe.transpose(ps_pos[:, P:SEQ], posr[:, 1, :], k["ident"][:, :]).then_inc(s_tr, 1)
            with pe.Fori(0, NU // 2) as j:
                for u in range(2):
                    pe.wait_ge(s_rows[u], j * 16 * UT + 16 * UT)
                    for t in range(UT):
                        last = pe.transpose(ps[:, u, t * P:(t + 1) * P], rows[:, u, t, :], k["ident"][:, :])
                        if t == UT - 1:
                            last.then_inc(s_ps[u], 1)
                    pe.wait_ge(s_hT[u], j + 1)
                    pe.sem_inc(s_free[u], 1)


def block_weights(nc, k, w, d):
    with Stage(nc, "bwt") as s:
        w1r = s.sb("w1r", [P, L, 2 * C])
        w1g = s.sb("w1g", [P, L, 2 * C])
        b1 = s.sb("b1", [P, L, 2])
        b2 = s.sb("b2", [P, L])
        lg = s.sb("lg", [P, L])
        lb = s.sb("lb", [P, L])
        gb = s.sb("gb", [P, L, 2])
        ps_w = s.pb("psw", [P, L, 2 * C])
        ps_b = s.pb("psb", [P, 32])
        s_in, s_g, s_mm = s.sem("in"), s.sem("g"), s.sem("mm")
        block = s.block()
        NIN = 10

        @block.sync
        def _(sp):
            for dst, src in (
                (w1r[:, :, :], d["w1"].rearrange("l c n -> c l n")),
                (w["w2"][:, :, :, :], d["w2"].rearrange("l (h p) c -> p l h c", p=P)),
                (w["cw"][:, 0:L, :], d["conv_w"].rearrange("l c o k -> c l (o k)")),
                (w["cb"][:, 0:L], d["conv_b"].rearrange("l c -> c l")),
                (lg[:, :], d["ln_g"].rearrange("l c -> c l")),
                (lb[:, :], d["ln_b"].rearrange("l c -> c l")),
                (b1[:, :, :], d["b1"].rearrange("l (h p) -> p l h", p=P)),
                (w["gw"][:, :, :], d["grn_w"].rearrange("l (h p) -> p l h", p=P)),
                (gb[:, :, :], d["grn_b"].rearrange("l (h p) -> p l h", p=P)),
                (b2[:, :], d["b2"].rearrange("l c -> c l")),
            ):
                sp.dma_start(dst, src, allow_slow_non_contiguous=True).then_inc(s_in, 16)

        @block.vector
        def _(dve):
            dve.wait_ge(s_in, 16 * NIN)
            dve.memset(w["cw"][:, L, :], 0.0)
            dve.memset(w["cb"][:, L:L + 1], 0.0)
            dve.tensor_tensor(w1g[:, :, :], w1r[:, :, :], bc(lg[:, :], 2, 2 * C), ALU.mult).then_inc(s_g, 1)
            dve.wait_ge(s_mm, 1)
            dve.tensor_copy(w["w1"][:, :, :], ps_w[:, :, :])
            dve.tensor_tensor(w["b1"][:, :, :], b1[:, :, :],
                              ps_b[:, 0:2 * L].rearrange("p (l h) -> p l h", h=2), ALU.add)
            dve.tensor_tensor(w["b2"][:, :], b2[:, :], ps_b[:, 2 * L:3 * L], ALU.add)

        @block.tensor
        def _(pe):
            pe.wait_ge(s_in, 16 * NIN)
            pe.wait_ge(s_g, 1)
            for l in range(L):
                pe.matmul(ps_w[:, l, :], k["cent"][:, :], w1g[:, l, :], start=True, stop=True)
                for h in range(2):
                    pe.matmul(ps_b[:, 2 * l + h:2 * l + h + 1], w1r[:, l, h * C:(h + 1) * C], lb[:, l:l + 1],
                              start=True, stop=True)
                for h in range(2):
                    last = pe.matmul(ps_b[:, 2 * L + l:2 * L + l + 1], w["w2"][:, l, h, :], gb[:, l, h:h + 1],
                                     start=(h == 0), stop=(h == 1))
            last.then_inc(s_mm, 1)


def convnext_blocks(nc, k, w, hT, table, ybuf2):
    NALL = L * NU
    LAG = 3
    NP = NU // 2
    with Stage(nc, "cnx") as s:
        y = s.sb("y", [P, 2, UNIT])
        ysq = s.sb("ysq", [P, 2, UNIT])
        yn = s.sb("yn", [P, 2, UNIT])
        gl = s.sb("gl", [P, 2, 2, UNIT])
        junk = s.sb("junk", [P, 2, UB, SEQ], BF16)
        w1c = s.sb("w1c", [P, 2 * C])
        w2s = s.sb("w2s", [P, 2, 2, UB, C])
        out = s.sb("out", [P, 2, UNIT])
        st = s.sb("st", [P, 2, UT])
        rs = s.sb("rs", [P, 2, UT])
        ss = s.sb("ss", [P, 2, 2, UB])
        g = s.sb("g", [P, 2, 2, UB])
        gm = s.sb("gm", [P, 2, UB])
        gs = s.sb("gs", [P, 2, 2, UB])
        ps_wide = s.pb("pswide", [P, UNIT])
        ps_inv = s.pb("psinv", [P, UNIT])
        ps_out = s.pb("psout", [P, UNIT])
        ps_c = s.pb("psc", [P, UNIT])
        ps_gm = ps_out[:, 0:UB]
        S = {n: s.sem(n) for n in ("mid", "conv", "cent", "sq", "stat", "stc", "rs", "inv", "norm", "w1", "gelu", "ss", "g",
                                   "gm", "sc", "w2s", "w2", "out", "wl")}
        s_tick = s.sem("tick")
        CE = CAP1 // P
        empty = s.sb("empty", [P, CE, ROW1])
        num = s.sb("num", [P, CE], I32)
        s_empty, s_fill = s.sem("empty"), s.sem("fill")
        block = s.block()
        mid = KC // 2

        def seqs(ap):
            return ap.rearrange("p (b t) -> p b t", t=SEQ)

        class Item:

            def __init__(self, j, u, lag):
                self.v = (u - lag) & 1
                q = j + (u - lag) // 2
                self.n = q * 2 + self.v
                self.there = not isinstance(j, int) or 0 <= self.n < NALL
                if self.there:
                    self.l = q // NP
                    self.col = (q & (NP - 1)) * (2 * UNIT) + self.v * UNIT

            def unit(self):
                return hT[:, self.col:self.col + UNIT] if isinstance(self.col, int) else hT[:, bass.ds(self.col, UNIT)]

        def one(ap, i):
            return ap[:, i:i + 1] if isinstance(i, int) else ap[:, bass.ds(i, 1)]

        def steps(eng, step):
            fill = (LAG + 1) // 2
            for j in range(fill):
                step(j, 0)
                step(j, 1)
            with eng.Fori(fill, NALL // 2) as j:
                step(j, 0)
                step(j, 1)
            for n in range(NALL, NALL + LAG):
                step(n // 2, n % 2)

        @block.sync
        def _(sp):
            sp.wait_ge(s_empty, 1)
            for e in range(E1):
                sp.dma_start(table[e * CAP1:(e + 1) * CAP1, :].rearrange("(t p) c -> p t c", p=P), empty[:, :, :])\
                    .then_inc(s_fill, 16)
            sp.dma_start(ybuf2[T:T + CAP1, :].rearrange("(t p) c -> p t c", p=P), empty[:, :, 0:C]).then_inc(s_fill, 16)
            sp.wait_ge(s_fill, 16 * (E1 + 1))

        @block.vector
        def _(dve):
            def taps(i, some):
                src, dst = seqs(i.unit()), seqs(y[:, i.v, :])
                for t in some:
                    o = t - mid
                    a, b = max(0, -o), SEQ - max(0, o)
                    last = dve.scalar_tensor_tensor(dst[:, :, a:b], src[:, :, a + o:b + o],
                                                    w["cw"][:, i.l, t:t + 1], dst[:, :, a:b], ALU.mult, ALU.add)
                    if t < KC - 1:
                        dve.drain()
                return last

            def step(j, u):
                this, norm, last = Item(j, u, 0), Item(j, u, 1), Item(j, u, 3)
                if last.there:
                    v = last.v
                    dve.wait_ge(S["gm"], last.n + 1)
                    dve.tensor_scalar(gm[:, v, :], ps_gm, 1e-6, None, ALU.add)
                    dve.drain()
                    dve.reciprocal(gm[:, v, :], gm[:, v, :])
                    dve.drain()
                    dve.tensor_tensor(gs[:, v, :, :], g[:, v, :, :], bc(gm[:, v, :], 1, 2), ALU.mult)
                    dve.drain()
                    for h in range(2):
                        scaled = dve.tensor_scalar(gs[:, v, h, :], gs[:, v, h, :], w["gw"][:, last.l, h:h + 1], 1.0,
                                                   ALU.mult, ALU.add)
                    scaled.then_inc(S["sc"], 1)
                if this.there:
                    dve.wait_ge(S["mid"], this.n + 1)
                    taps(this, [t for t in range(KC) if t != mid]).then_inc(S["conv"], 1)
                if norm.there:
                    dve.wait_ge(S["inv"], norm.n + 1)
                    dve.tensor_tensor(yn[:, norm.v, :], y[:, norm.v, :], ps_inv[:, :], ALU.mult)\
                        .then_inc(S["norm"], 1)

            steps(dve, step)

        @block.scalar
        def _(act):
            def middle(i):
                act.activation(y[:, i.v, :], i.unit(), ACT.Identity, bias=one(w["cb"], i.l),
                               scale=w["cw"][:, i.l, mid:mid + 1]).then_inc(S["mid"], 1)

            def squares(i, h):
                for b in range(UB):
                    last = act.activation(junk[:, h, b, :], gl[:, i.v, h, b * SEQ:(b + 1) * SEQ], ACT.Square,
                                          accum_out=ss[:, i.v, h, b:b + 1])
                return last

            middle(Item(0, 0, 0))

            def step(j, u):
                this, after, wide, small = Item(j, u, 0), Item(j, u, -1), Item(j, u, 1), Item(j, u, 2)
                if after.there:
                    if wide.there:
                        wait_alone(act, S["norm"], wide.n + 1, s_tick)
                    middle(after)
                if this.there:
                    act.wait_ge(S["cent"], this.n + 1)
                    act.activation(ysq[:, this.v, :], ps_c[:, :], ACT.Square).then_inc(S["sq"], 1)
                if wide.there:
                    wait_alone(act, S["w1"], wide.n * 2 + 1, s_tick)
                    act.activation(gl[:, wide.v, 0, :], ps_wide[:, :], ACT.Gelu, bias=w["b1"][:, wide.l, 0:1])\
                        .then_inc(S["gelu"], 1)
                if this.there:
                    act.wait_ge(S["stat"], this.n + 1)
                    act.activation(st[:, this.v, :], ps_c[:, 0:UT], ACT.Copy)\
                        .then_inc(S["stc"], 1)
                if wide.there:
                    act.drain()
                    squares(wide, 0)
                    wait_alone(act, S["w1"], wide.n * 2 + 2, s_tick)
                    act.activation(gl[:, wide.v, 1, :], ps_wide[:, :], ACT.Gelu, bias=w["b1"][:, wide.l, 1:2])\
                        .then_inc(S["gelu"], 1)
                    act.drain()
                    squares(wide, 1).then_inc(S["ss"], 1)
                if small.there:
                    wait_alone(act, S["w2"], small.n + 1, s_tick)
                    act.activation(out[:, small.v, :], ps_out[:, :], ACT.Identity, bias=one(w["b2"], small.l))\
                        .then_inc(S["out"], 1)

            steps(act, step)

        @block.gpsimd
        def _(pool):
            pool.memset(empty[:, :, :], 0.0)
            pool.iota(num[:, :], pattern=[[P, CE]], base=T, channel_multiplier=1)
            pool.drain()
            pool.tensor_copy(empty[:, :, C], num[:, :]).then_inc(s_empty, 1)

            def step(j, u):
                i = Item(j, u, 2)
                if i.there:
                    wait_alone(pool, S["sc"], i.n + 1, s_tick)
                    for h in range(2):
                        last = pool.tensor_tensor(w2s[:, i.v, h, :, :], bc(w["w2"][:, i.l, h, :], 1, UB),
                                                  bc(gs[:, i.v, h, :], 2, C), ALU.mult)
                    last.then_inc(S["w2s"], 1)
                i = Item(j, u, 0)
                if i.there:
                    wait_alone(pool, S["stc"], i.n + 1, s_tick)
                    pool.tensor_scalar(rs[:, i.v, :], st[:, i.v, :], 1e-6, None, ALU.add)
                    pool.drain()
                    pool.tensor_tensor(rs[:, i.v, :], rs[:, i.v, :], k["nhalf"][:, 0:UT], ALU.pow)\
                        .then_inc(S["rs"], 1)
                    if u == 0:
                        if not isinstance(j, int) or j > 0:
                            wait_alone(pool, S["w1"], i.n * 2, s_tick)
                        pool.tensor_copy(w1c[:, :], w["w1"][:, i.l, :]).then_inc(S["wl"], 1)
                i = Item(j, u, 1)
                if i.there:
                    pool.wait_ge(S["ss"], i.n + 1)
                    pool.tensor_tensor(g[:, i.v, :, :], ss[:, i.v, :, :],
                                       k["half"][:, 0:2 * UB].rearrange("p (a b) -> p a b", a=2), ALU.pow)\
                        .then_inc(S["g"], 1)
                i = Item(j, u, 2)
                if i.there:
                    wait_alone(pool, S["out"], i.n + 1, s_tick)
                    pool.tensor_tensor(i.unit(), i.unit(), out[:, i.v, :], ALU.add)

            steps(pool, step)

        @block.tensor
        def _(pe):
            def widen(i, h):
                for c in range(2):
                    last = pe.matmul(ps_wide[:, c * 512:(c + 1) * 512], w1c[:, h * C:(h + 1) * C],
                                     yn[:, i.v, c * 512:(c + 1) * 512], start=True, stop=True)
                last.then_inc(S["w1"], 1)

            def narrow(i):
                for b in range(UB):
                    for h in range(2):
                        last = pe.matmul(ps_out[:, b * SEQ:(b + 1) * SEQ], w2s[:, i.v, h, b, :],
                                         gl[:, i.v, h, b * SEQ:(b + 1) * SEQ], start=(h == 0), stop=(h == 1))
                last.then_inc(S["w2"], 1)

            def step(j, u):
                this, wide, small = Item(j, u, 0), Item(j, u, 1), Item(j, u, 2)
                if this.there:
                    pe.wait_ge(S["conv"], this.n + 1)
                    for c in range(2):
                        last = pe.matmul(ps_c[:, c * 512:(c + 1) * 512], k["cent"][:, :],
                                         y[:, this.v, c * 512:(c + 1) * 512], start=True, stop=True)
                    last.then_inc(S["cent"], 1)
                if wide.there:
                    if u == 1:
                        pe.wait_ge(S["wl"], j + 1)
                    pe.wait_ge(S["norm"], wide.n + 1)
                    if small.there:
                        pe.wait_ge(S["gelu"], wide.n * 2)
                    widen(wide, 0)
                if this.there:
                    pe.wait_ge(S["sq"], this.n + 1)
                    for t in range(UT):
                        last = pe.matmul(ps_c[:, t:t + 1], ysq[:, this.v, t * P:(t + 1) * P], k["mean"][:, 0:1],
                                         start=True, stop=True)
                    last.then_inc(S["stat"], 1)
                if wide.there:
                    pe.wait_ge(S["gelu"], wide.n * 2 + 1)
                    widen(wide, 1)
                if small.there:
                    pe.wait_ge(S["w2s"], small.n + 1)
                    narrow(small)
                if this.there:
                    pe.wait_ge(S["rs"], this.n + 1)
                    for t in range(UT):
                        last = pe.matmul(ps_inv[:, t * P:(t + 1) * P], bc(rs[:, this.v, t:t + 1], 1, P)[:, :, 0],
                                         k["ident"][:, :], start=True, stop=True)
                    last.then_inc(S["inv"], 1)
                if wide.there:
                    pe.wait_ge(S["g"], wide.n + 1)
                    if small.there:
                        pe.wait_ge(S["out"], small.n + 1)
                    for h in range(2):
                        last = pe.matmul(ps_gm, k["half_mean"][:, :], g[:, wide.v, h, :], start=(h == 0), stop=(h == 1))
                    last.then_inc(S["gm"], 1)

            steps(pe, step)



S_ = 64
KA = 5
E0 = 16
ROW = C + E0
TWO_PI_HI, TWO_PI_LO = 6.28125, 0.0019353071795864769
PI = 3.14159265358979
ROUND = 12582912.0


def lru_weights(nc, k, w, d):
    with Stage(nc, "lwt") as s:
        wi = s.sb("wi", [P, C])
        wit = s.sb("wit", [P, C])
        lnw = s.sb("lnw", [P, 2])
        cw = s.sb("cw", [S_, S_, KA])
        cwt = s.sb("cwt", [S_, KA + 1, S_])
        cb = s.sb("cb", [S_, 1])
        par = s.sb("par", [P, 3])
        ex = s.sb("ex", [P, 3])
        lm = s.sb("lm", [P, 1])
        lam = s.sb("lam", [P, 1])
        ang = s.sb("ang", [P, 2])
        q = s.sb("q", [P, 2])
        tr = s.sb("tr", [P, 2])
        bn = s.sb("bn", [P, S_])
        bnT = s.sb("bnT", [S_, P])
        cc = s.sb("cc", [S_, 2, 2, S_])
        wo = s.sb("wo", [P, S_])
        em = s.sb("em", [P, 2])
        en = s.sb("en", [P, 2])
        mix = s.sb("mix", [P, 2, SEQ // 2])
        ps = s.pb("ps", [P, 8, 512])
        s_in, s_ex, s_lm, s_q, s_sin = s.sem("in"), s.sem("ex"), s.sem("lm"), s.sem("q"), s.sem("sin")
        s_bn, s_cc, s_t, s_bnT, s_m, s_cwt, s_wit = (s.sem(n) for n in ("bn", "cc", "t", "bnT", "m", "cwt", "wit"))
        block = s.block()
        NIN = 21

        @block.sync
        def _(sp):
            col = lambda a: a.rearrange("(p a) -> p a", a=1)
            for dst, src in (
                (wi[0:S_, :], d["W_in"][S_:2 * S_, :]), (wi[S_:P, :], d["W_in"][0:S_, :]),
                (lnw[:, 0:1], col(d["ln_w"])), (lnw[:, 1:2], col(d["ln_b"])),
                (cw[:, :, :], d["conv_w"]), (cb[:, :], col(d["conv_b"])),
                (par[0:S_, 0:1], col(d["nu_log"])), (par[S_:P, 0:1], col(d["nu_log"])),
                (par[0:S_, 1:2], col(d["theta_log"])), (par[S_:P, 1:2], col(d["theta_log"])),
                (par[0:S_, 2:3], col(d["gamma_log"])), (par[S_:P, 2:3], col(d["gamma_log"])),
                (bn[0:S_, :], d["B_re"]), (bn[S_:P, :], d["B_im"]),
                (cc[:, 0, 0, :], d["C_re"]), (cc[:, 0, 1, :], d["C_im"]),
                (cc[:, 1, 0, :], d["C_im"]), (cc[:, 1, 1, :], d["C_re"]),
                (wo[:, :], d["W_out"]), (w["gate"][:, :], d["gate_w"]), (w["wout"][S_:S_ + 1, :], d["b_out"].rearrange("(a n) -> a n", a=1)),
            ):
                sp.dma_start(dst, src, allow_slow_non_contiguous=True).then_inc(s_in, 16)

        @block.scalar
        def _(act):
            act.wait_ge(s_in, 16 * NIN)
            act.activation(ex[:, :], par[:, :], ACT.Exp).then_inc(s_ex, 1)
            act.drain()
            act.activation(lm[:, :], ex[:, 0:1], ACT.Exp, scale=-1.0).then_inc(s_lm, 1)
            act.wait_ge(s_q, 1)
            act.activation(tr[:, :], ang[:, :], ACT.Sin).then_inc(s_sin, 1)

        @block.vector
        def _(dve):
            dve.wait_ge(s_in, 16 * NIN)
            dve.wait_ge(s_ex, 1)
            dve.tensor_scalar(bn[:, :], bn[:, :], ex[:, 2:3], None, ALU.mult).then_inc(s_bn, 1)
            dve.tensor_scalar(cc[:, 0, 1, :], cc[:, 0, 1, :], -1.0, None, ALU.mult)
            dve.tensor_scalar(cc[:, 1, :, :], cc[:, 1, :, :], -1.0, None, ALU.mult).then_inc(s_cc, 1)
            dve.tensor_copy(cwt[:, 0:KA, :], cw[:, :, :].rearrange("i j k -> i k j"))
            dve.memset(cwt[:, KA, :], 0.0).then_inc(s_cwt, 1)
            dve.tensor_scalar(ang[:, 0:1], ex[:, 1:2], PI / 2, None, ALU.add)
            dve.tensor_copy(ang[:, 1:2], ex[:, 1:2])
            dve.drain()
            dve.tensor_scalar(q[:, :], ang[:, :], 1.0 / (2 * PI), ROUND, ALU.mult, ALU.add)
            dve.drain()
            dve.tensor_scalar(q[:, :], q[:, :], ROUND, None, ALU.subtract)
            dve.drain()
            for part in (TWO_PI_HI, TWO_PI_LO):
                dve.scalar_tensor_tensor(ang[:, :], q[:, :], -part, ang[:, :], ALU.mult, ALU.add)
                dve.drain()
            dve.tensor_scalar(ang[:, :], ang[:, :], PI, -PI, ALU.min, ALU.max).then_inc(s_q, 1)
            dve.wait_ge(s_lm, 1)
            dve.memset(w["decay"][:, :], 1.0)
            dve.drain()
            dve.tensor_scalar(w["decay"][:, :], w["decay"][:, :], lm[:, :], None, ALU.mult)
            dve.drain()
            dve.memset(w["decay"][:, :].rearrange("p (b t) -> p b t", t=SEQ)[:, :, 0:1], 0.0)
            dve.wait_ge(s_sin, 1)
            cs, sn = w["cos"], w["sin"]
            dve.memset(cs[:, 0:1], 1.0)
            dve.memset(sn[:, 0:1], 0.0)
            dve.tensor_copy(em[:, :], tr[:, :])
            dve.drain()
            m = 1
            while m < SEQ:
                dve.tensor_scalar(mix[:, 0, 0:m], sn[:, 0:m], em[:, 1:2], None, ALU.mult)
                dve.tensor_scalar(mix[:, 1, 0:m], cs[:, 0:m], em[:, 1:2], None, ALU.mult)
                dve.tensor_tensor(en[:, :], em[:, :], em[:, :], ALU.mult)
                dve.drain()
                dve.scalar_tensor_tensor(cs[:, m:2 * m], cs[:, 0:m], em[:, 0:1], mix[:, 0, 0:m], ALU.mult, ALU.subtract)
                dve.scalar_tensor_tensor(sn[:, m:2 * m], sn[:, 0:m], em[:, 0:1], mix[:, 1, 0:m], ALU.mult, ALU.add)
                dve.tensor_tensor(en[:, 0:1], en[:, 0:1], en[:, 1:2], ALU.subtract)
                dve.drain()
                dve.scalar_tensor_tensor(em[:, 1:2], em[:, 1:2], 2.0, em[:, 0:1], ALU.mult, ALU.mult)
                dve.drain()
                dve.tensor_copy(em[:, 0:1], en[:, 0:1])
                dve.drain()
                m *= 2
            dve.tensor_copy(w["sinr"][0:S_, :], sn[0:S_, :])
            dve.tensor_scalar(w["sinr"][S_:P, :], sn[S_:P, :], -1.0, None, ALU.mult)
            dve.wait_ge(s_t, 1)
            dve.tensor_copy(bnT[:, :], ps[0:S_, 0, 0:P]).then_inc(s_bnT, 1)
            dve.tensor_copy(w["cp"][:, :], ps[:, 1, 0:S_])
            dve.tensor_copy(w["cq"][:, :], ps[:, 1, S_:P])
            dve.tensor_copy(w["wout"][0:S_, :], ps[0:S_, 2, 0:C])
            dve.tensor_copy(wit[:, :], ps[:, 3, 0:C]).then_inc(s_wit, 1)
            dve.drain()
            dve.tensor_scalar(w["win"][:, :], wit[:, :], lnw[:, 0:1], None, ALU.mult)
            dve.wait_ge(s_m, 1)
            for n in range(3):
                dve.tensor_copy(w["bc"][:, n, :], ps[:, 4, n * P:(n + 1) * P])
            dve.tensor_copy(w["bA"][:, :], ps[:, 5, 0:1])
            dve.tensor_copy(w["bsw"][0:S_, :], ps[S_:P, 5, 0:1])
            dve.tensor_copy(w["bsw"][S_:P, :], ps[0:S_, 5, 0:1])
            dve.tensor_copy(w["bin"][:, :], ps[:, 6, 0:1])

        @block.tensor
        def _(pe):
            pe.wait_ge(s_in, 16 * NIN)
            pe.wait_ge(s_bn, 1)
            pe.wait_ge(s_cc, 1)
            pe.transpose(ps[0:S_, 0, 0:P], bn[:, :], k["ident"][:, :])
            for n in range(2):
                pe.transpose(ps[:, 1, n * S_:(n + 1) * S_], cc[:, n, :, :].rearrange("o a s -> o (a s)"),
                             k["ident"][0:S_, 0:S_])
            pe.transpose(ps[0:S_, 2, 0:C], wo[:, :], k["ident"][:, :])
            pe.transpose(ps[:, 3, 0:C], wi[:, :], k["ident"][:, :]).then_inc(s_t, 1)
            pe.wait_ge(s_bnT, 1)
            pe.wait_ge(s_cwt, 1)
            for n in range(3):
                pe.matmul(ps[:, 4, n * P:(n + 1) * P], cwt[:, 2 * n:2 * n + 2, :].rearrange("i a j -> i (a j)"),
                          bnT[:, :], start=True, stop=True)
            pe.matmul(ps[:, 5, 0:1], bnT[:, :], cb[:, :], start=True, stop=True)
            pe.wait_ge(s_wit, 1)
            pe.matmul(ps[:, 6, 0:1], wit[:, :], lnw[:, 1:2], start=True, stop=True).then_inc(s_m, 1)


def lru_block(nc, k, w, hT, x2T, lg, xrows, ybuf):
    NP = NU // 2
    W = SEQ + 4
    with Stage(nc, "lru") as s:
        hx = s.sb("hx", [P, 2, UNIT])
        hsq = s.sb("hsq", [P, 2, UNIT])
        st = s.sb("st", [P, 2, 2 * UT])
        va = s.sb("va", [P, 2, UT])
        r1 = s.sb("r1", [P, 2, UT])
        rz = s.sb("rz", [P, 2, UT])
        htk = s.sb("htk", [P, 2, UT, C])
        x1 = s.sb("x1", [P, 2, UT, C])
        z = s.sb("z", [P, 2, UT, C])
        zT = hx
        V2 = s.sb("V2", [P, 2, UB, W])
        gx = s.sb("gx", [S_, 2, UNIT])
        ta = hsq
        tb = s.sb("tb", [P, 2, UNIT])
        uu = z
        o = s.sb("o", [S_ + 1, 2, UNIT])
        bs = s.sb("bs", [P, 2, UT, 6])
        ba = s.sb("ba", [P, 2, UT, 2])
        rb = s.sb("rb", [P, 2, UT])
        x2 = tb
        x2c = s.sb("x2c", [P, 2, UNIT])
        ps = s.pb("ps", [P, 2, 4, 512])
        names = ("hx", "sq", "T1", "htk", "rs", "x1", "z", "hx1", "Tz", "zT", "win", "V2", "gx", "A", "t", "u", "scan",
                 "q", "p", "y", "o", "wo", "h1", "bn", "rb", "x2", "T2", "x2T", "x2c", "lg", "lgc", "st", "sx", "sy")
        S = {n: s.sem2(n) for n in names}
        s_pad, s_tick = s.sem("pad"), s.sem("tick")
        block = s.block()
        flat = lambda ap: ap.rearrange("p a b -> p (a b)")
        seqs = lambda ap: ap.rearrange("p (b t) -> p b t", t=SEQ)

        def bank(u, n, rows=slice(0, P)):
            return ps[rows, u, n:n + 2, :].rearrange("p a b -> p (a b)")

        @block.sync
        def _(sp):
            with sp.Fori(0, NP) as j:
                for u in range(2):
                    rows = lambda t: t[bass.ds(j * 2 * UNIT + u * UNIT, UNIT), :].rearrange("(t p) c -> p t c", p=P)
                    sp.wait_ge(S["h1"][u], j + 1)
                    sp.dma_start(rows(ybuf), htk[:, u, :, :]).then_inc(S["sy"][u], 16)
                    sp.wait_ge(S["x2"][u], j + 1)
                    sp.dma_start(rows(xrows[:, 0:C]), x2[:, u, :].rearrange("p (t c) -> p t c", c=C))\
                        .then_inc(S["sx"][u], 16)
            for u in range(2):
                sp.wait_ge(S["sy"][u], 16 * NP)
                sp.wait_ge(S["sx"][u], 16 * NP)

        @block.scalar
        def _(act):
            with act.Fori(0, NP) as j:
                for u in range(2):
                    wait_alone(act, S["y"][u], j, s_tick)
                    act.activation(hx[:, u, :], hT[:, bass.ds(j * 2 * UNIT + u * UNIT, UNIT)], ACT.Copy)\
                        .then_inc(S["hx"][u], 1)
                    act.drain()
                    act.activation(hsq[:, u, :], hx[:, u, :], ACT.Square).then_inc(S["sq"][u], 1)
                for u in range(2):
                    act.wait_ge(S["T1"][u], j + 1)
                    act.wait_ge(S["sy"][u], j * 16)
                    act.activation(st[:, u, :], ps[:, u, 2, 0:2 * UT], ACT.Copy).then_inc(S["st"][u], 1)
                    act.activation(flat(htk[:, u, :, :]), bank(u, 0), ACT.Copy).then_inc(S["htk"][u], 1)
                for u in range(2):
                    act.wait_ge(S["Tz"][u], j + 1)
                    act.activation(zT[:, u, :], bank(u, 0), ACT.Copy).then_inc(S["zT"][u], 1)
                for u in range(2):
                    act.wait_ge(S["win"][u], j + 1)
                    if u == 0:
                        act.wait_ge(s_pad, 1)
                    act.activation(V2[0:S_, u, :, 2:2 + SEQ], seqs(bank(u, 2, slice(0, S_))), ACT.Identity,
                                   bias=w["bin"][0:S_, 0:1])
                    act.activation(V2[S_:P, u, :, 1:1 + SEQ], seqs(bank(u, 2, slice(0, S_))), ACT.Identity,
                                   bias=w["bin"][0:S_, 0:1]).then_inc(S["V2"][u], 1)
                    act.activation(gx[:, u, :], bank(u, 2, slice(S_, P)), ACT.Gelu,
                                   bias=w["bin"][S_:P, 0:1]).then_inc(S["gx"][u], 1)
                for u in range(2):
                    act.wait_ge(S["T2"][u], j + 1)
                    act.activation(x2c[:, u, :], bank(u, 2), ACT.Copy).then_inc(S["x2c"][u], 1)
                    act.activation(x2T[:, bass.ds(j * 2 * UNIT + u * UNIT, UNIT)], bank(u, 2), ACT.Copy)\
                        .then_inc(S["x2T"][u], 1)

        @block.gpsimd
        def _(pool):
            pool.memset(V2[:, :, :, :], 0.0).then_inc(s_pad, 1)
            pool.drain()
            pool.memset(o[S_:S_ + 1, :, :], 1.0).then_inc(s_pad, 1)
            pool.drain()
            nh = k["nhalf"][:, 0:UT]
            with pool.Fori(0, NP) as j:
                for u in range(2):
                    mean, sq = st[:, u, 0:UT], st[:, u, UT:2 * UT]
                    pool.wait_ge(S["st"][u], j + 1)
                    pool.tensor_tensor(va[:, u, :], mean, mean, ALU.mult)
                    pool.drain()
                    pool.tensor_tensor(va[:, u, :], sq, va[:, u, :], ALU.subtract)
                    pool.drain()
                    pool.tensor_scalar(va[:, u, :], va[:, u, :], 0.0, None, ALU.max)
                    pool.drain()
                    pool.tensor_scalar(r1[:, u, :], va[:, u, :], 1e-5, None, ALU.add)
                    pool.drain()
                    pool.tensor_tensor(r1[:, u, :], r1[:, u, :], nh, ALU.pow)
                    pool.drain()
                    pool.tensor_tensor(rz[:, u, :], r1[:, u, :], r1[:, u, :], ALU.mult)
                    pool.drain()
                    pool.tensor_tensor(rz[:, u, :], rz[:, u, :], va[:, u, :], ALU.mult)
                    pool.drain()
                    pool.tensor_scalar(rz[:, u, :], rz[:, u, :], 1e-5, None, ALU.add)
                    pool.drain()
                    pool.tensor_tensor(rz[:, u, :], rz[:, u, :], nh, ALU.pow)
                    pool.drain()
                    pool.tensor_tensor(rz[:, u, :], rz[:, u, :], r1[:, u, :], ALU.mult).then_inc(S["rs"][u], 1)
                for u in range(2):
                    pool.wait_ge(S["x1"][u], j + 1)
                    pool.tensor_tensor(x1[:, u, :, :], x1[:, u, :, :], htk[:, u, :, :], ALU.add)\
                        .then_inc(S["hx1"][u], 1)
                for u in range(2):
                    pool.wait_ge(S["t"][u], j + 1)
                    pool.tensor_tensor(flat(uu[:, u, :, :]), ta[:, u, :], tb[:, u, :], ALU.add).then_inc(S["u"][u], 1)
                for u in range(2):
                    pool.wait_ge(S["scan"][u], j + 1)
                    pool.tensor_tensor(seqs(tb[:, u, :]), seqs(flat(uu[:, u, :, :])), bc(w["sin"][:, :], 1, UB),
                                       ALU.mult).then_inc(S["q"][u], 1)
                for u in range(2):
                    wait_alone(pool, S["bn"][u], j + 1, s_tick)
                    pool.tensor_scalar(rb[:, u, :], ba[:, u, :, 1], 1e-5, None, ALU.add)
                    pool.drain()
                    pool.tensor_tensor(rb[:, u, :], rb[:, u, :], nh, ALU.pow).then_inc(S["rb"][u], 1)

        @block.vector
        def _(dve):
            with dve.Fori(0, NP) as j:
                for u in range(2):
                    dve.wait_ge(S["rs"][u], j + 1)
                    dve.wait_ge(S["htk"][u], j + 1)
                    for t in range(UT):
                        last = dve.tensor_scalar(x1[:, u, t, :], htk[:, u, t, :], st[:, u, t:t + 1],
                                                 r1[:, u, t:t + 1], ALU.subtract, ALU.mult)
                    last.then_inc(S["x1"][u], 1)
                    for t in range(UT):
                        last = dve.tensor_scalar(z[:, u, t, :], htk[:, u, t, :], st[:, u, t:t + 1],
                                                 rz[:, u, t:t + 1], ALU.subtract, ALU.mult)
                    last.then_inc(S["z"][u], 1)
                for u in range(2):
                    dve.wait_ge(S["A"][u], j + 1)
                    dve.wait_ge(S["sx"][u], j * 16)
                    dve.scalar_tensor_tensor(seqs(ta[:, u, :]), seqs(bank(u, 0)), w["bA"][:, 0:1],
                                             bc(w["cos"][:, :], 1, UB), ALU.add, ALU.mult)
                    dve.scalar_tensor_tensor(seqs(tb[0:S_, u, :]), seqs(bank(u, 0, slice(S_, P))), w["bsw"][0:S_, 0:1],
                                             bc(w["sinr"][0:S_, :], 1, UB), ALU.add, ALU.mult)
                    dve.scalar_tensor_tensor(seqs(tb[S_:P, u, :]), seqs(bank(u, 0, slice(0, S_))), w["bsw"][S_:P, 0:1],
                                             bc(w["sinr"][S_:P, :], 1, UB), ALU.add, ALU.mult).then_inc(S["t"][u], 1)
                for u in range(2):
                    dve.wait_ge(S["u"][u], j + 1)
                    dve.tensor_tensor_scan(flat(uu[:, u, :, :]), w["decay"][:, :], flat(uu[:, u, :, :]), 0.0,
                                           ALU.mult, ALU.add).then_inc(S["scan"][u], 1)
                    dve.drain()
                    dve.tensor_tensor(seqs(ta[:, u, :]), seqs(flat(uu[:, u, :, :])), bc(w["cos"][:, :], 1, UB),
                                      ALU.mult).then_inc(S["p"][u], 1)
                for u in range(2):
                    dve.wait_ge(S["y"][u], j + 1)
                    dve.wait_ge(S["gx"][u], j + 1)
                    dve.tensor_tensor(o[0:S_, u, :], bank(u, 2, slice(0, S_)), gx[:, u, :], ALU.mult)\
                        .then_inc(S["o"][u], 1)
                for u in range(2):
                    dve.wait_ge(S["wo"][u], j + 1)
                    dve.wait_ge(S["hx1"][u], j + 1)
                    dve.tensor_tensor(flat(htk[:, u, :, :]), bank(u, 0), flat(x1[:, u, :, :]), ALU.add)\
                        .then_inc(S["h1"][u], 1)
                    dve.drain()
                    for t in range(UT):
                        dve.bn_stats(bs[:, u, t, :], htk[:, u, t, :])
                    dve.drain()
                    for t in range(UT):
                        last = dve.bn_aggr(ba[:, u, t, :], bs[:, u, t, :])
                    last.then_inc(S["bn"][u], 1)
                for u in range(2):
                    dve.wait_ge(S["rb"][u], j + 1)
                    for t in range(UT):
                        last = dve.tensor_scalar(x2[:, u, t * C:(t + 1) * C], htk[:, u, t, :], ba[:, u, t, 0:1],
                                                 rb[:, u, t:t + 1], ALU.subtract, ALU.mult)
                    last.then_inc(S["x2"][u], 1)
                for u in range(2):
                    dve.wait_ge(S["lg"][u], j + 1)
                    dve.tensor_copy(lg[:, bass.ds(j * 2 * UT + u * UT, UT), :],
                                    ps[:, u, 0, 0:UT * E0].rearrange("p (t e) -> p t e", e=E0)).then_inc(S["lgc"][u], 1)

        @block.tensor
        def _(pe):
            pe.wait_ge(s_pad, 2)
            tiles = lambda ap, t: ap[:, t * P:(t + 1) * P]
            halves = lambda c: slice(c * 512, (c + 1) * 512)
            with pe.Fori(0, NP) as j:
                for u in range(2):
                    pe.wait_ge(S["sq"][u], j + 1)
                    pe.wait_ge(S["x2T"][u], j)
                    pe.wait_ge(S["lgc"][u], j)
                    for q, src in enumerate((hx, hsq)):
                        for t in range(UT):
                            pe.matmul(ps[:, u, 2, q * UT + t:q * UT + t + 1], tiles(src[:, u, :], t),
                                      k["mean"][:, 0:1], start=True, stop=True)
                    for t in range(UT):
                        last = pe.transpose(ps[:, u, t // 4, (t % 4) * P:(t % 4 + 1) * P], tiles(hx[:, u, :], t),
                                            k["ident"][:, :])
                    last.then_inc(S["T1"][u], 1)
                for u in range(2):
                    pe.wait_ge(S["z"][u], j + 1)
                    for t in range(UT):
                        last = pe.transpose(ps[:, u, t // 4, (t % 4) * P:(t % 4 + 1) * P], z[:, u, t, :],
                                            k["ident"][:, :])
                    last.then_inc(S["Tz"][u], 1)
                for u in range(2):
                    pe.wait_ge(S["zT"][u], j + 1)
                    for c in range(2):
                        last = pe.matmul(ps[:, u, 2 + c, :], w["win"][:, :], zT[:, u, halves(c)], start=True, stop=True)
                    last.then_inc(S["win"][u], 1)
                for u in range(2):
                    pe.wait_ge(S["V2"][u], j + 1)
                    for c in range(2):
                        for n in range(3):
                            rows = slice(0, P if n < 2 else S_)
                            last = pe.matmul(ps[:, u, c, :].rearrange("p (b t) -> p b t", t=SEQ), w["bc"][rows, n, :],
                                             V2[rows, u, 2 * c:2 * c + 2, 2 * n:2 * n + SEQ],
                                             start=(n == 0), stop=(n == 2))
                    last.then_inc(S["A"][u], 1)
                for u in range(2):
                    pe.wait_ge(S["gx"][u], j + 1)
                    pe.wait_ge(S["p"][u], j + 1)
                    pe.wait_ge(S["q"][u], j + 1)
                    for c in range(2):
                        pe.matmul(ps[0:S_, u, 2 + c, :], w["cp"][:, :], ta[:, u, halves(c)], start=True, stop=False)
                        last = pe.matmul(ps[0:S_, u, 2 + c, :], w["cq"][:, :], tb[:, u, halves(c)],
                                         start=False, stop=True)
                    last.then_inc(S["y"][u], 1)
                for u in range(2):
                    pe.wait_ge(S["o"][u], j + 1)
                    for t in range(UT):
                        last = pe.matmul(ps[:, u, t // 4, (t % 4) * P:(t % 4 + 1) * P], tiles(o[:, u, :], t),
                                         w["wout"][:, :], start=True, stop=True)
                    last.then_inc(S["wo"][u], 1)
                for u in range(2):
                    pe.wait_ge(S["x2"][u], j + 1)
                    for t in range(UT):
                        last = pe.transpose(ps[:, u, 2 + t // 4, (t % 4) * P:(t % 4 + 1) * P], tiles(x2[:, u, :], t),
                                            k["ident"][:, :])
                    last.then_inc(S["T2"][u], 1)
                for u in range(2):
                    pe.wait_ge(S["x2c"][u], j + 1)
                    for t in range(UT):
                        last = pe.matmul(ps[:, u, 0, t * E0:(t + 1) * E0], tiles(x2c[:, u, :], t), w["gate"][:, :],
                                         start=True, stop=True)
                    last.then_inc(S["lg"][u], 1)




CAP0 = T // E0
H = 512
HT = H // P
CH = 512
CT = CH // P
SEG = P // E0
ST = NT // SEG


def softmax_experts(nc, k, lg, pT, xrows):
    with Stage(nc, "smx") as s:
        mx = s.sb("mx", [P, NT])
        pr = s.sb("pr", [P, ST, SEG, E0])
        ps = s.pb("ps", [P, 2, 512])
        s_sub, s_exp, s_pr, s_pc, s_t, s_x = (s.sem(n) for n in ("sub", "exp", "pr", "pc", "t", "x"))
        block = s.block()

        @block.vector
        def _(dve):
            dve.tensor_reduce(mx[:, :], lg[:, :, :], AX, ALU.max)
            dve.drain()
            dve.tensor_tensor(lg[:, :, :], lg[:, :, :], bc(mx[:, :], 2, E0), ALU.subtract).then_inc(s_sub, 1)
            dve.wait_ge(s_exp, 1)
            dve.tensor_reduce(mx[:, :], lg[:, :, :], AX, ALU.add)
            dve.drain()
            dve.reciprocal(mx[:, :], mx[:, :])
            dve.drain()
            dve.tensor_tensor(lg[:, :, :], lg[:, :, :], bc(mx[:, :], 2, E0), ALU.mult).then_inc(s_pr, 1)
            dve.drain()
            dve.tensor_copy(pr[:, :, :, :], lg[:, :, :].rearrange("p (s t) e -> p t s e", s=SEG)).then_inc(s_pc, 1)
            dve.wait_ge(s_t, 1)
            dve.tensor_copy(pT[:, :], ps[:, :, :].rearrange("p a b -> p (a b)"))

        @block.scalar
        def _(act):
            act.wait_ge(s_sub, 1)
            act.activation(lg[:, :, :], lg[:, :, :], ACT.Exp).then_inc(s_exp, 1)

        @block.tensor
        def _(pe):
            pe.wait_ge(s_pc, 1)
            for t in range(ST):
                last = pe.transpose(ps[:, t // 4, (t % 4) * P:(t % 4 + 1) * P],
                                    pr[:, t, :, :].rearrange("p s e -> p (s e)"), k["ident"][:, :])
            last.then_inc(s_t, 1)

        @block.sync
        def _(sp):
            sp.wait_ge(s_pr, 1)
            sp.dma_start(xrows[:, C:ROW].rearrange("(t p) e -> p t e", p=P), lg[:, :, :],
                         allow_slow_non_contiguous=True).then_inc(s_x, 16)
            sp.wait_ge(s_x, 16)


def select_and_shared(nc, k, d, x2T, pT, idx, shared):
    with Stage(nc, "sel") as s:
        w1 = s.sb("w1", [P, H])
        w2 = s.sb("w2", [P, HT, C])
        b1 = s.sb("b1", [P, HT])
        b2 = s.sb("b2", [P, C])
        same = s.sb("same", [P, P])
        lower = s.sb("lower", [P, P])
        hs = s.sb("hs", [P, 2, HT, CH])
        thr = s.sb("thr", [P, 1], I32)
        cand = s.sb("cand", [P, 1], I32)
        bit = s.sb("bit", [P, 1], I32)
        keep = s.sb("keep", [P, 1], I32)
        cnt = s.sb("cnt", [P, 4])
        junk = s.sb("junk", [P, T // SEG], BF16)
        gt = s.sb("gt", [P, T // SEG])
        eq = s.sb("eq", [P, T // SEG])
        rk = s.sb("rk", [P, T // SEG])
        one = s.sb("one", [P, T // SEG])
        lim = s.sb("lim", [P, 2])
        sl = s.sb("sl", [P, SEG, ST, E0], I32)
        si = s.sb("si", [P, SEG, ST, E0], I32)
        lo = s.sb("lo", [P, NT, E0], BF16)
        hi = s.sb("hi", [P, NT, E0], BF16)
        io = s.sb("io", [P, 32, E0], I32)
        iob = s.sb("iob", [P, 32, E0], BF16)
        ioe = s.sb("ioe", [P, E0, 32], BF16)
        tok = s.sb("tok", [P, 1 + NT])
        toki = s.sb("toki", [P, 1 + NT], I32)
        oa = s.sb("oa", [P, 2, E0, 32], BF16)
        ob = s.sb("ob", [P, 2, 16, E0], BF16)
        ov = s.sb("ov", [P, 2, 2, 16, E0], BF16)
        zz = s.sb("zz", [P, P], BF16)
        ls = s.sb("ls", [P, 4, 2, 16, 4])
        psh = s.pb("psh", [P, 4, 512])
        pso = s.pb("pso", [P, 2, 512])
        psc = s.pb("psc", [P, 512])
        s_in, s_set, s_tick = s.sem("in"), s.sem("set"), s.sem("tick")
        s_hid = [s.sem(f"hid{n}") for n in range(HT)]
        s_gel = [s.sem(f"gel{n}") for n in range(HT)]
        s_out, s_ev = s.sem2("out"), s.sem2("ev")
        s_cnt, s_sum, s_thr = s.sem("cnt"), s.sem("sum"), s.sem("thr")
        s_ge, s_tot, s_cs, s_off, s_v, s_vt = (s.sem(n) for n in ("ge", "tot", "cs", "off", "v", "vt"))
        s_zz = s.sem("zz")
        s_oh, s_li = s.sem2("oh"), s.sem2("li")
        s_end = s.sem("end")
        block = s.block()
        NCH = T // CH

        @block.sync
        def _(sp):
            for dst, src in ((w1[:, :], d["sw1"]), (w2[:, :, :], d["sw2"].rearrange("(k p) c -> p k c", p=P)),
                             (b1[:, :], d["sb1"].rearrange("(k p) -> p k", p=P)), (b2[:, :], bc(d["sb2"], 0, P))):
                sp.dma_start(dst, src, allow_slow_non_contiguous=True).then_inc(s_in, 16)

        @block.gpsimd
        def _(pool):
            pool.memset(lower[:, :], 0.0)
            pool.memset(one[:, :], 1.0)
            pool.memset(zz[:, :], 0.0)
            pool.iota(toki[:, 0:1], pattern=[[0, 1]], base=0, channel_multiplier=1)
            pool.iota(toki[:, 1:1 + NT], pattern=[[1, NT]], base=0, channel_multiplier=0)
            pool.iota(io[:, :, :], pattern=[[1, 32], [0, E0]], base=0, channel_multiplier=0)
            pool.drain()
            pool.tensor_copy(tok[:, :], toki[:, :])
            pool.tensor_copy(iob[:, :, :], io[:, :, :])
            pool.tensor_copy(ioe[:, :, :], io[:, :, :].rearrange("p b e -> p e b"))
            for n in range(1, SEG):
                pool.affine_select(out=lower[:, :], in_=lower[:, :], compare_op=ALU.not_equal, fill=1.0,
                                   base=E0 * n, pattern=[[-1, P]], channel_multiplier=1)
                pool.drain()
            pool.tensor_tensor(same[:, :], lower[:, :], k["ident"][:, :], ALU.add)
            pool.drain()
            for n in range(1, SEG):
                last = pool.affine_select(out=same[:, :], in_=same[:, :], compare_op=ALU.not_equal, fill=1.0,
                                          base=-E0 * n, pattern=[[-1, P]], channel_multiplier=1)
                if n == SEG - 1:
                    last.then_inc(s_set, 1)
                else:
                    pool.drain()

        @block.scalar
        def _(act):
            act.wait_ge(s_in, 64)
            with act.Fori(0, NCH // 2) as j:
                for u in range(2):
                    for m in range(HT):
                        act.wait_ge(s_hid[m], 2 * j + u + 1)
                        act.activation(hs[:, u, m, :], psh[:, m, :], ACT.Gelu_apprx_tanh, bias=b1[:, m:m + 1])\
                            .then_inc(s_gel[m], 1)

        @block.vector
        def _(dve):
            dve.memset(thr[:, :], 0)
            dve.memset(bit[:, :], 1 << 29)
            dve.wait_ge(s_set, 1)
            dve.wait_ge(s_in, 64)
            dve.drain()
            with dve.Fori(0, NCH // 2) as j:
                for u in range(2):
                    for q in range(2):
                        n = 4 * j + 2 * u + q
                        dve.tensor_tensor(cand[:, :], thr[:, :], bit[:, :], ALU.bitwise_or)
                        dve.drain()
                        dve.tensor_scalar(junk[:, :], pT[:, :], cand[:, :].bitcast(F32), None, ALU.is_ge, ALU.add,
                                          accum_out=cnt[:, 0:1]).then_inc(s_cnt, 1)
                        dve.tensor_scalar(bit[:, :], bit[:, :], 1, None, ALU.logical_shift_right)
                        dve.wait_ge(s_sum, n + 1)
                        dve.tensor_scalar(keep[:, :], psc[:, 0:1], CAP0 - 0.5, None, ALU.is_ge)
                        dve.drain()
                        dve.copy_predicated(thr[:, :], keep[:, :], cand[:, :]).then_inc(s_thr, 1)
                        dve.drain()
                for u in range(2):
                    dve.wait_ge(s_out[u], j + 1)
                    dst = shared[:, bass.ds(j * 2 * CT + u * CT, CT), :]
                    dve.tensor_tensor(dst, pso[:, u, :].rearrange("p (t c) -> p t c", c=C),
                                      bc(b2[:, :], 1, CT), ALU.add).then_inc(s_ev[u], 1)
            thf = thr[:, :].bitcast(F32)
            dve.tensor_scalar(gt[:, :], pT[:, :], thf, None, ALU.is_gt, ALU.add, accum_out=cnt[:, 0:1])
            dve.tensor_scalar(eq[:, :], pT[:, :], thf, None, ALU.is_equal, ALU.add, accum_out=cnt[:, 1:2])\
                .then_inc(s_ge, 1)
            dve.drain()
            dve.tensor_tensor_scan(rk[:, :], one[:, :], eq[:, :], 0.0, ALU.mult, ALU.add)
            dve.wait_ge(s_tot, 1)
            dve.tensor_scalar(lim[:, 0:1], psc[:, 1:2], -1.0, float(CAP0), ALU.mult, ALU.add)
            dve.drain()
            dve.tensor_tensor(lim[:, 0:1], lim[:, 0:1], psc[:, 2:3], ALU.subtract)
            dve.drain()
            dve.scalar_tensor_tensor(eq[:, :], rk[:, :], lim[:, 0:1], eq[:, :], ALU.is_le, ALU.mult)
            dve.drain()
            dve.tensor_tensor(gt[:, :], gt[:, :], eq[:, :], ALU.add)
            dve.drain()
            dve.tensor_tensor_scan(rk[:, :], one[:, :], gt[:, :], 0.0, ALU.mult, ALU.add).then_inc(s_cs, 1)
            dve.wait_ge(s_off, 1)
            dve.tensor_copy(lim[:, 1:2], psc[:, 3:4])
            dve.drain()
            dve.scalar_tensor_tensor(rk[:, :], rk[:, :], lim[:, 1:2], gt[:, :], ALU.add, ALU.mult).then_inc(s_v, 1)
            dve.wait_ge(s_vt, 1)
            for q in range(2):
                dve.tensor_scalar(si[:, :, q * 4:(q + 1) * 4, :],
                                  psh[:, q, :].rearrange("p (t s e) -> p s t e", s=SEG, e=E0), -1.0, None, ALU.add)
            dve.drain()
            dve.tensor_scalar(sl[:, :, :, :], si[:, :, :, :], 31, None, ALU.bitwise_and)
            dve.tensor_scalar(si[:, :, :, :], si[:, :, :, :], 5, None, ALU.arith_shift_right)
            dve.drain()
            dve.tensor_copy(lo[:, :, :], sl[:, :, :, :].rearrange("p s t e -> p (s t) e"))
            dve.tensor_copy(hi[:, :, :], si[:, :, :, :].rearrange("p s t e -> p (s t) e"))
            dve.drain()
            with dve.Fori(0, NT // 2) as j:
                for u in range(2):
                    t = 2 * j + u
                    dve.wait_ge(s_li[u], j)
                    dve.tensor_tensor(oa[:, u, :, :], bc(lo[:, bass.ds(t, 1), :], 3, 32)[:, 0, :, :], ioe[:, :, :],
                                      ALU.is_equal)
                    dve.tensor_tensor(ob[:, u, :, :], bc(hi[:, bass.ds(t, 1), :], 1, 16)[:, :, 0, :], iob[:, 0:16, :],
                                      ALU.is_equal)
                    dve.drain()
                    dve.tensor_scalar(ov[:, u, 0, :, :], ob[:, u, :, :], tok[:, 0:1], None, ALU.mult)
                    dve.tensor_scalar(ov[:, u, 1, :, :], ob[:, u, :, :], tok[:, bass.ds(t + 1, 1)], None,
                                      ALU.mult).then_inc(s_oh[u], 1)
                    dve.drain()
            dve.wait_ge(s_end, 1)
            dve.tensor_copy(ls[:, :, :, :, :].rearrange("p g v a e -> p g (v a e)"), psh[:, :, 0:P])
            dve.drain()
            for e in range(4):
                for a in range(4):
                    src = ls[32 * e:32 * e + 32, :, :, a:16:4, e]
                    dst = idx[32 * a:32 * a + 32, :, :].rearrange("p (q e) g -> p q e g", e=4)[:, :, e, :]
                    dve.scalar_tensor_tensor(dst, src[:, :, 1, :], float(P), src[:, :, 0, :], ALU.mult, ALU.add)

        @block.tensor
        def _(pe):
            pe.wait_ge(s_in, 64)
            pe.wait_ge(s_set, 1)
            with pe.Fori(0, NCH // 2) as j:
                def count(n):
                    pe.wait_ge(s_cnt, n + 1)
                    pe.matmul(psc[:, 0:1], same[:, :], cnt[:, 0:1], start=True, stop=True).then_inc(s_sum, 1)

                for u in range(2):
                    for m in range(HT):
                        pe.wait_ge(s_gel[m], 2 * j + u)
                        pe.matmul(psh[:, m, :], w1[:, m * P:(m + 1) * P],
                                  x2T[:, bass.ds(j * 2 * CH + u * CH, CH)], start=True, stop=True).then_inc(s_hid[m], 1)
                        if m % 2:
                            count(4 * j + 2 * u + m // 2)
                for u in range(2):
                    pe.wait_ge(s_ev[u], j)
                    for m in range(HT):
                        pe.wait_ge(s_gel[m], 2 * j + u + 1)
                    for t in range(CT):
                        for m in range(HT):
                            last = pe.matmul(pso[:, u, t * P:(t + 1) * P], hs[:, u, m, t * P:(t + 1) * P],
                                             w2[:, m, :], start=(m == 0), stop=(m == HT - 1))
                    last.then_inc(s_out[u], 1)
            pe.wait_ge(s_ge, 1)
            pe.matmul(psc[:, 1:2], same[:, :], cnt[:, 0:1], start=True, stop=True)
            pe.matmul(psc[:, 2:3], lower[:, :], cnt[:, 1:2], start=True, stop=True).then_inc(s_tot, 1)
            pe.wait_ge(s_cs, 1)
            pe.matmul(psc[:, 3:4], lower[:, :], rk[:, T // SEG - 1:T // SEG], start=True, stop=True).then_inc(s_off, 1)
            pe.wait_ge(s_v, 1)
            for t in range(ST):
                last = pe.transpose(psh[:, t // 4, (t % 4) * P:(t % 4 + 1) * P], rk[:, t * P:(t + 1) * P],
                                    k["ident"][:, :])
            last.then_inc(s_vt, 1)
            pe.wait_ge(s_oh[0], 1)
            for g in range(4):
                pe.matmul(psh[:, g, 0:P], zz[:, :], zz[:, :], start=True, stop=False)
            with pe.Fori(0, NT // 2) as j:
                for u in range(2):
                    pe.wait_ge(s_oh[u], j + 1)
                    for g in range(4):
                        last = pe.matmul(psh[:, g, 0:P],
                                         oa[:, u, 4 * g:4 * g + 4, :].rearrange("p e b -> p (e b)"),
                                         ov[:, u, :, :, 4 * g:4 * g + 4].rearrange("p v a e -> p (v a) e"),
                                         start=False, stop=False)
                    last.then_inc(s_li[u], 1)
            for g in range(4):
                last = pe.matmul(psh[:, g, 0:P], zz[:, :], zz[:, :], start=False, stop=True)
            last.then_inc(s_end, 1)


def experts_choice(nc, k, d, idx, xrows, ybuf):
    with Stage(nc, "moe") as s:
        w1 = s.sb("w1", [P, 2, H])
        w2 = s.sb("w2", [P, 2, HT, C])
        b1 = s.sb("b1", [P, 2, HT])
        b2 = s.sb("b2", [P, 2, C])
        idc = s.sb("idc", [P, 2, CT], I32)
        xg = s.sb("xg", [P, 2, CT, ROW])
        xT = s.sb("xT", [P, 2, CH])
        hs = s.sb("hs", [P, 2, HT, CH])
        yo = s.sb("yo", [P, 2, CT, C])
        psx = s.pb("psx", [P, 2, 512])
        psh = s.pb("psh", [P, 4, 512])
        pso = s.pb("pso", [P, 2, 512])
        S = {n: s.sem2(n) for n in ("w", "x", "T", "xT", "out", "y", "add", "free")}
        s_hid = [s.sem(f"hid{n}") for n in range(HT)]
        s_gel = [s.sem(f"gel{n}") for n in range(HT)]
        s_tick = s.sem("tick")
        block = s.block()
        NE2 = E0 // 2
        NW = 4

        @block.sync
        def _(sp):
            def load(e, u):
                for dst, src in (
                    (w1[:, u, :], d["w1"][e, :, :].rearrange("a c h -> (a c) h")),
                    (w2[:, u, :, :], d["w2"][e, :, :].rearrange("a (k p) c -> p (a k) c", p=P)),
                    (b1[:, u, :], d["b1"][e, :].rearrange("a (k p) -> p (a k)", p=P)),
                    (b2[:, u, :], bc(d["b2"][e, :], 0, P).rearrange("q a c -> q (a c)")),
                ):
                    sp.dma_start(dst, src, allow_slow_non_contiguous=True).then_inc(S["w"][u], 16)

            for u in range(2):
                load(slice(u, u + 1), u)
            with sp.Fori(0, NE2 - 1) as j:
                for u in range(2):
                    sp.wait_ge(S["y"][u], j + 1)
                    load(bass.ds(2 * j + 2 + u, 1), u)

        @block.gpsimd
        def _(pool):
            def gather(u):
                pool.drain()
                for t in range(CT):
                    pool.indirect_dma_start(xg[:, u, t, :], None, xrows,
                                            bass.IndirectOffsetOnAxis(ap=idc[:, u, t:t + 1], axis=0))\
                        .then_inc(S["x"][u], 16)

            def scatter(u):
                for t in range(CT):
                    pool.indirect_dma_start(ybuf, bass.IndirectOffsetOnAxis(ap=idc[:, u, t:t + 1], axis=0),
                                            yo[:, u, t, :], None, compute_op=ALU.add).then_inc(S["add"][u], 16)

            for u in range(2):
                pool.tensor_copy(idc[:, u, :], idx[:, u, :])
                gather(u)
            with pool.Fori(0, NE2 - 1) as j:
                for u in range(2):
                    pool.wait_ge(S["y"][u], j + 1)
                    wait_alone(pool, S["add"][1 - u], (j + u) * 16 * CT, s_tick)
                    scatter(u)
                    wait_alone(pool, S["add"][u], (j + 1) * 16 * CT, s_tick)
                    pool.tensor_copy(idc[:, u, :], idx[:, bass.ds(2 * j + 2 + u, 1), :].rearrange("p a g -> p (a g)"))
                    gather(u)
            for u in range(2):
                pool.wait_ge(S["y"][u], NE2)
                pool.wait_ge(S["add"][1 - u], (NE2 - 1 + u) * 16 * CT)
                scatter(u)
            pool.wait_ge(S["add"][1], NE2 * 16 * CT)

        @block.scalar
        def _(act):
            with act.Fori(0, NE2) as j:
                for u in range(2):
                    act.wait_ge(S["w"][u], (j + 1) * 16 * NW)
                    for m in range(HT):
                        act.wait_ge(s_hid[m], 2 * j + u + 1)
                        act.activation(hs[:, u, m, :], psh[:, m, :], ACT.Gelu_apprx_tanh, bias=b1[:, u, m:m + 1])\
                            .then_inc(s_gel[m], 1)

        @block.vector
        def _(dve):
            with dve.Fori(0, NE2) as j:
                for u in range(2):
                    dve.wait_ge(S["T"][u], j + 1)
                    dve.tensor_copy(xT[:, u, :], psx[:, u, :]).then_inc(S["xT"][u], 1)
                for u in range(2):
                    dve.wait_ge(S["out"][u], j + 1)
                    dve.wait_ge(S["add"][u], j * 16 * CT)
                    dve.tensor_tensor(yo[:, u, :, :], pso[:, u, :].rearrange("p (t c) -> p t c", c=C),
                                      bc(b2[:, u, :], 1, CT), ALU.add)
                    dve.drain()
                    for t in range(CT):
                        last = dve.tensor_scalar(yo[:, u, t, :], yo[:, u, t, :],
                                                 xg[:, u, t, bass.ds(2 * j + u + C, 1)], None, ALU.mult)
                    last.then_inc(S["y"][u], 1)

        @block.tensor
        def _(pe):
            with pe.Fori(0, NE2) as j:
                for u in range(2):
                    pe.wait_ge(S["x"][u], (j + 1) * 16 * CT)
                    for t in range(CT):
                        last = pe.transpose(psx[:, u, t * P:(t + 1) * P], xg[:, u, t, 0:C], k["ident"][:, :])
                    last.then_inc(S["T"][u], 1)
                for u in range(2):
                    pe.wait_ge(S["w"][u], (j + 1) * 16 * NW)
                    pe.wait_ge(S["xT"][u], j + 1)
                    for m in range(HT):
                        pe.wait_ge(s_gel[m], 2 * j + u)
                        pe.matmul(psh[:, m, :], w1[:, u, m * P:(m + 1) * P], xT[:, u, :], start=True,
                                  stop=True).then_inc(s_hid[m], 1)
                for u in range(2):
                    pe.wait_ge(S["y"][u], j)
                    for m in range(HT):
                        pe.wait_ge(s_gel[m], 2 * j + u + 1)
                    for t in range(CT):
                        for m in range(HT):
                            last = pe.matmul(pso[:, u, t * P:(t + 1) * P], hs[:, u, m, t * P:(t + 1) * P],
                                             w2[:, u, m, :], start=(m == 0), stop=(m == HT - 1))
                    last.then_inc(S["out"][u], 1)




NH, HD = 8, C // 8
KD = 9
E1 = 8
CAP1 = 2560
ROW1 = C + 1 + E1
DUMP = E1 * CAP1


def attention_block(nc, k, d, shared, ybuf, x4, lg, ybuf2):
    NP = NU // 2
    W = SEQ + KD - 1
    with Stage(nc, "att") as s:
        wq = s.sb("wq", [P, 3 * C])
        bq = s.sb("bq", [P, 3 * C])
        bv = s.sb("bv", [P, 1])
        wd = s.sb("wd", [P, KD])
        wp = s.sb("wp", [P, C])
        bp = s.sb("bp", [P, C])
        wr = s.sb("wr", [P, E1])
        br = s.sb("br", [P, E1])
        mask = s.sb("mask", [P, P])
        ht = s.sb("ht", [P, 2, UT, C])
        xa = s.sb("xa", [P, 2, UT, C])
        xT = s.sb("xT", [P, 2, UNIT])
        qk = s.sb("qk", [P, 2, UT, 2 * C])
        sq = s.sb("sq", [P, 2, UT, 2 * C])
        rr = s.sb("rr", [P, 2, UT, 2 * NH])
        v = s.sb("v", [P, 2, UT, C])
        vp = s.sb("vp", [P, 2, UB, W])
        dc = s.sb("dc", [P, 2, UNIT])
        qT = s.sb("qT", [P, 2, UNIT])
        am = s.sb("am", [P, 2, UB, P])
        on = s.sb("on", [P, 2, UT, C])
        ro = s.sb("ro", [P, 2, UT, NH])
        bs = s.sb("bs", [P, 2, UT, 6])
        ba = s.sb("ba", [P, 2, UT, 2])
        rb = s.sb("rb", [P, 2, UT])
        cT, x4T = xT, qT
        ps = s.pb("ps", [P, 2, 4, 512])
        names = ("ld", "h3", "bn", "rb", "xn", "Tx", "xT", "QK", "qk", "sq", "ssq", "rr", "kn", "V", "v", "vT", "vp",
                 "Tq", "qT", "at", "am", "dc", "o", "o2", "osq", "oss", "ro", "on", "To", "cT", "pr", "h4", "hb", "bn2",
                 "rb2", "x4", "x4c", "T4", "x4T", "lg", "lgc", "sy")
        S = {n: s.sem2(n) for n in names}
        s_in, s_set, s_tick, s_mask = s.sem("in"), s.sem("set"), s.sem("tick"), s.sem("mask")
        block = s.block()
        flat = lambda ap: ap.rearrange("p a b -> p (a b)")
        seqs = lambda ap: ap.rearrange("p (b t) -> p b t", t=SEQ)
        bank = lambda u, n, m=2: ps[:, u, n:n + m, :].rearrange("p a b -> p (a b)")
        NIN = 9

        @block.sync
        def _(sp):
            one = lambda a: a.rearrange("(p a) -> p a", a=1)
            for dst, src in (
                (wq[:, :], d["w_qkv"]), (bq[:, :], bc(d["b_qkv"], 0, P)), (bv[:, :], one(d["b_qkv"][2 * C:3 * C])),
                (wd[:, :], bc(d["w_dconv"].rearrange("h a k b -> h (a k b)"), 1, HD)),
                (wp[:, :], d["w_proj"]), (bp[:, :], bc(d["b_proj"], 0, P)), (wr[:, :], d["Wr"]),
                (br[:, :], bc(d["br"], 0, P)),
            ):
                sp.dma_start(dst, src, allow_slow_non_contiguous=True).then_inc(s_in, 16)
            with sp.Fori(0, NP) as j:
                for u in range(2):
                    rows = lambda t: t[bass.ds(j * 2 * UNIT + u * UNIT, UNIT), :].rearrange("(t p) c -> p t c", p=P)
                    sp.wait_ge(S["sy"][u], j * 16)
                    sp.wait_ge(S["x4"][u], j)
                    sp.dma_start(ht[:, u, :, :], rows(ybuf)).then_inc(S["ld"][u], 16)
                for u in range(2):
                    rows = lambda t: t[bass.ds(j * 2 * UNIT + u * UNIT, UNIT), :].rearrange("(t p) c -> p t c", p=P)
                    sp.wait_ge(S["h4"][u], j + 1)
                    sp.dma_start(rows(ybuf2), ht[:, u, :, :]).then_inc(S["sy"][u], 16)
            for u in range(2):
                sp.wait_ge(S["sy"][u], 16 * NP)

        @block.scalar
        def _(act):
            act.wait_ge(s_in, 16 * (NIN - 1))
            with act.Fori(0, NP) as j:
                for u in range(2):
                    act.wait_ge(S["Tx"][u], j + 1)
                    act.activation(xT[:, u, :], bank(u, 0), ACT.Copy).then_inc(S["xT"][u], 1)
                for u in range(2):
                    act.wait_ge(S["qk"][u], j + 1)
                    act.activation(sq[:, u, :, :], qk[:, u, :, :], ACT.Square).then_inc(S["sq"][u], 1)
                for u in range(2):
                    act.wait_ge(S["vT"][u], j + 1)
                    if u == 0:
                        act.wait_ge(s_set, 1)
                    act.activation(vp[:, u, :, KD // 2:KD // 2 + SEQ], seqs(bank(u, 2)), ACT.Identity,
                                   bias=bv[:, 0:1]).then_inc(S["vp"][u], 1)
                for u in range(2):
                    act.wait_ge(S["Tq"][u], j + 1)
                    act.activation(qT[:, u, :], bank(u, 0), ACT.Copy).then_inc(S["qT"][u], 1)
                act.drain()
                for u in range(2):
                    act.wait_ge(S["o2"][u], j + 1)
                    act.activation(sq[:, u, :, 0:C], on[:, u, :, :], ACT.Square).then_inc(S["osq"][u], 1)
                for u in range(2):
                    act.wait_ge(S["T4"][u], j + 1)
                    act.activation(x4T[:, u, :], bank(u, 2), ACT.Copy).then_inc(S["x4T"][u], 1)
                act.drain()

        @block.gpsimd
        def _(pool):
            pool.memset(vp[:, :, :, :], 0.0).then_inc(s_set, 1)
            pool.memset(mask[:, :], 1.0)
            pool.drain()
            blocks = mask[:, :].rearrange("p (h e) -> p h e", e=HD)
            pool.affine_select(out=blocks, in_=blocks, compare_op=ALU.is_ge, fill=0.0, base=0,
                               pattern=[[-HD, NH], [0, HD]], channel_multiplier=1)
            pool.drain()
            pool.affine_select(out=blocks, in_=blocks, compare_op=ALU.is_ge, fill=0.0, base=HD - 1,
                               pattern=[[HD, NH], [0, HD]], channel_multiplier=-1).then_inc(s_mask, 1)
            pool.wait_ge(s_in, 16 * (NIN - 1))

            def rsqrt(dst, src, eps):
                if eps:
                    pool.tensor_scalar(dst, src, eps, None, ALU.add)
                    pool.drain()
                    src = dst
                return src

            nh = k["nhalf"]
            with pool.Fori(0, NP) as j:
                for u in range(2):
                    wait_alone(pool, S["ld"][u], (j + 1) * 16, s_tick)
                    pool.tensor_tensor(ht[:, u, :, :], ht[:, u, :, :],
                                       shared[:, bass.ds(j * 2 * UT + u * UT, UT), :], ALU.add).then_inc(S["h3"][u], 1)
                for u in range(2):
                    wait_alone(pool, S["bn"][u], j + 1, s_tick)
                    rsqrt(rb[:, u, :], ba[:, u, :, 1], 1e-5)
                    pool.tensor_tensor(rb[:, u, :], rb[:, u, :], nh[:, 0:UT], ALU.pow).then_inc(S["rb"][u], 1)
                for u in range(2):
                    pool.wait_ge(S["xn"][u], j + 1)
                    pool.tensor_tensor(ht[:, u, :, :], ht[:, u, :, :], bc(bp[:, :], 1, UT), ALU.add)\
                        .then_inc(S["hb"][u], 1)
                for u in range(2):
                    pool.wait_ge(S["ssq"][u], j + 1)
                    pool.tensor_tensor(rr[:, u, :, :], rr[:, u, :, :], bc(nh[:, 0:2 * NH], 1, UT), ALU.pow)
                    pool.drain()
                    pool.tensor_scalar(rr[:, u, :, 0:NH], rr[:, u, :, 0:NH], 1.0 / PI, None, ALU.mult)\
                        .then_inc(S["rr"][u], 1)
                for u in range(2):
                    pool.wait_ge(S["oss"][u], j + 1)
                    pool.tensor_tensor(ro[:, u, :, :], ro[:, u, :, :], bc(nh[:, 0:NH], 1, UT), ALU.pow)\
                        .then_inc(S["ro"][u], 1)
                for u in range(2):
                    wait_alone(pool, S["bn2"][u], j + 1, s_tick)
                    rsqrt(rb[:, u, :], ba[:, u, :, 1], 1e-5)
                    pool.tensor_tensor(rb[:, u, :], rb[:, u, :], nh[:, 0:UT], ALU.pow).then_inc(S["rb2"][u], 1)
                for u in range(2):
                    wait_alone(pool, S["x4"][u], j + 1, s_tick)
                    pool.tensor_copy(x4[:, bass.ds(j * 2 * UT + u * UT, UT), 0:C], xa[:, u, :, :])\
                        .then_inc(S["x4c"][u], 1)

        @block.vector
        def _(dve):
            def norm_stats(u, done):
                for t in range(UT):
                    dve.bn_stats(bs[:, u, t, :], ht[:, u, t, :])
                dve.drain()
                for t in range(UT):
                    last = dve.bn_aggr(ba[:, u, t, :], bs[:, u, t, :])
                last.then_inc(done, 1)

            def normalize(u, done):
                for t in range(UT):
                    last = dve.tensor_scalar(xa[:, u, t, :], ht[:, u, t, :], ba[:, u, t, 0:1], rb[:, u, t:t + 1],
                                             ALU.subtract, ALU.mult)
                last.then_inc(done, 1)

            heads = lambda ap: ap.rearrange("p t (h e) -> p (t h) e", e=HD)
            dve.wait_ge(s_in, 16 * (NIN - 1))
            dve.wait_ge(s_mask, 1)
            with dve.Fori(0, NP) as j:
                for u in range(2):
                    dve.wait_ge(S["h3"][u], j + 1)
                    norm_stats(u, S["bn"][u])
                for u in range(2):
                    dve.wait_ge(S["rb"][u], j + 1)
                    dve.wait_ge(S["x4c"][u], j)
                    normalize(u, S["xn"][u])
                for u in range(2):
                    dve.wait_ge(S["QK"][u], j + 1)
                    dve.tensor_tensor(qk[:, u, :, :], bank(u, 0, 4).rearrange("p (t n) -> p t n", n=2 * C),
                                      bc(bq[:, 0:2 * C], 1, UT), ALU.add).then_inc(S["qk"][u], 1)
                for u in range(2):
                    dve.wait_ge(S["V"][u], j + 1)
                    dve.tensor_tensor(v[:, u, :, :], bank(u, 0).rearrange("p (t n) -> p t n", n=C),
                                      bc(bq[:, 2 * C:3 * C], 1, UT), ALU.add).then_inc(S["v"][u], 1)
                    dve.wait_ge(S["sq"][u], j + 1)
                    dve.tensor_reduce(rr[:, u, :, :].rearrange("p t h -> p (t h)"), heads(sq[:, u, :, :]), AX,
                                      ALU.add).then_inc(S["ssq"][u], 1)
                for u in range(2):
                    dve.wait_ge(S["rr"][u], j + 1)
                    kk = qk[:, u, :, C:2 * C].rearrange("p t (h e) -> p t h e", e=HD)
                    dve.tensor_tensor(kk, kk, bc(rr[:, u, :, NH:2 * NH], 3, HD), ALU.mult).then_inc(S["kn"][u], 1)
                for u in range(2):
                    dve.wait_ge(S["at"][u], j + 1)
                    dve.tensor_tensor(am[:, u, :, :], bank(u, 2, 1).rearrange("p (b n) -> p b n", n=P),
                                      bc(mask[:, :], 1, UB), ALU.mult).then_inc(S["am"][u], 1)
                for u in range(2):
                    dve.wait_ge(S["vp"][u], j + 1)
                    dst = seqs(dc[:, u, :])
                    dve.tensor_scalar(dst, vp[:, u, :, 0:SEQ], wd[:, 0:1], None, ALU.mult)
                    for t in range(1, KD):
                        dve.drain()
                        last = dve.scalar_tensor_tensor(dst, vp[:, u, :, t:t + SEQ], wd[:, t:t + 1], dst, ALU.mult,
                                                        ALU.add)
                    last.then_inc(S["dc"][u], 1)
                for u in range(2):
                    dve.wait_ge(S["o"][u], j + 1)
                    oo = on[:, u, :, :].rearrange("p t (h e) -> p (t h) e", e=HD)
                    dve.tensor_tensor(on[:, u, :, :].rearrange("p t (h e) -> p t h e", e=HD),
                                      bank(u, 0).rearrange("p (t h e) -> p t h e", e=HD, h=NH),
                                      bc(rr[:, u, :, 0:NH], 3, HD), ALU.mult)
                    dve.drain()
                    dve.scalar_tensor_tensor(on[:, u, :, :], v[:, u, :, :], 0.5, on[:, u, :, :], ALU.mult,
                                             ALU.add).then_inc(S["o2"][u], 1)
                for u in range(2):
                    dve.wait_ge(S["osq"][u], j + 1)
                    dve.tensor_reduce(ro[:, u, :, :], sq[:, u, :, 0:C].rearrange("p t (h e) -> p t h e", e=HD), AX,
                                      ALU.add).then_inc(S["oss"][u], 1)
                for u in range(2):
                    dve.wait_ge(S["ro"][u], j + 1)
                    oo = on[:, u, :, :].rearrange("p t (h e) -> p (t h) e", e=HD)
                    dve.tensor_tensor(oo, oo, bc(ro[:, u, :, :].rearrange("p t h -> p (t h)"), 2, HD), ALU.mult)\
                        .then_inc(S["on"][u], 1)
                for u in range(2):
                    dve.wait_ge(S["To"][u], j + 1)
                    dve.tensor_tensor(cT[:, u, :], bank(u, 2), dc[:, u, :], ALU.add).then_inc(S["cT"][u], 1)
                for u in range(2):
                    dve.wait_ge(S["pr"][u], j + 1)
                    dve.wait_ge(S["hb"][u], j + 1)
                    dve.tensor_tensor(flat(ht[:, u, :, :]), bank(u, 0), flat(ht[:, u, :, :]), ALU.add)\
                        .then_inc(S["h4"][u], 1)
                    dve.drain()
                    norm_stats(u, S["bn2"][u])
                for u in range(2):
                    dve.wait_ge(S["rb2"][u], j + 1)
                    normalize(u, S["x4"][u])
                for u in range(2):
                    dve.wait_ge(S["lg"][u], j + 1)
                    dve.tensor_tensor(lg[:, bass.ds(j * 2 * UT + u * UT, UT), :],
                                      ps[:, u, 0, 0:UT * E1].rearrange("p (t e) -> p t e", e=E1),
                                      bc(br[:, :], 1, UT), ALU.add).then_inc(S["lgc"][u], 1)

        @block.tensor
        def _(pe):
            pe.wait_ge(s_in, 16 * (NIN - 1))
            tile = lambda u, n, t: ps[:, u, n + t // 4, (t % 4) * P:(t % 4 + 1) * P]
            cols = lambda ap, t: ap[:, t * P:(t + 1) * P]

            def transposes(u, n, src, done):
                for t in range(UT):
                    last = pe.transpose(tile(u, n, t), src(t), k["ident"][:, :])
                last.then_inc(done, 1)

            with pe.Fori(0, NP) as j:
                for u in range(2):
                    pe.wait_ge(S["xn"][u], j + 1)
                    pe.wait_ge(S["lgc"][u], j)
                    transposes(u, 0, lambda t: xa[:, u, t, :], S["Tx"][u])
                for u in range(2):
                    pe.wait_ge(S["xT"][u], j + 1)
                    for t in range(UT):
                        last = pe.matmul(ps[:, u, t // 2, (t % 2) * 2 * C:(t % 2 + 1) * 2 * C], cols(xT[:, u, :], t),
                                         wq[:, 0:2 * C], start=True, stop=True)
                    last.then_inc(S["QK"][u], 1)
                for u in range(2):
                    pe.wait_ge(S["qk"][u], j + 1)
                    for t in range(UT):
                        last = pe.matmul(tile(u, 0, t), cols(xT[:, u, :], t), wq[:, 2 * C:3 * C], start=True, stop=True)
                    last.then_inc(S["V"][u], 1)
                    for c in range(2):
                        last = pe.matmul(ps[:, u, 2 + c, :], wq[:, 2 * C:3 * C], xT[:, u, c * 512:(c + 1) * 512],
                                         start=True, stop=True)
                    last.then_inc(S["vT"][u], 1)
                for u in range(2):
                    pe.wait_ge(S["v"][u], j + 1)
                    transposes(u, 0, lambda t: qk[:, u, t, 0:C], S["Tq"][u])
                for u in range(2):
                    pe.wait_ge(S["kn"][u], j + 1)
                    pe.wait_ge(S["vp"][u], j + 1)
                    for b in range(UB):
                        for t in range(2):
                            last = pe.matmul(ps[:, u, 2, b * P:(b + 1) * P], qk[:, u, 2 * b + t, C:2 * C],
                                             v[:, u, 2 * b + t, :], start=(t == 0), stop=(t == 1))
                    last.then_inc(S["at"][u], 1)
                for u in range(2):
                    pe.wait_ge(S["am"][u], j + 1)
                    pe.wait_ge(S["qT"][u], j + 1)
                    for t in range(UT):
                        last = pe.matmul(tile(u, 0, t), cols(qT[:, u, :], t), am[:, u, t // 2, :], start=True, stop=True)
                    last.then_inc(S["o"][u], 1)
                for u in range(2):
                    pe.wait_ge(S["on"][u], j + 1)
                    transposes(u, 2, lambda t: on[:, u, t, :], S["To"][u])
                for u in range(2):
                    pe.wait_ge(S["cT"][u], j + 1)
                    for t in range(UT):
                        last = pe.matmul(tile(u, 0, t), cols(cT[:, u, :], t), wp[:, :], start=True, stop=True)
                    last.then_inc(S["pr"][u], 1)
                for u in range(2):
                    pe.wait_ge(S["x4"][u], j + 1)
                    transposes(u, 2, lambda t: xa[:, u, t, :], S["T4"][u])
                for u in range(2):
                    pe.wait_ge(S["x4T"][u], j + 1)
                    for t in range(UT):
                        last = pe.matmul(ps[:, u, 0, t * E1:(t + 1) * E1], cols(x4T[:, u, :], t), wr[:, :],
                                         start=True, stop=True)
                    last.then_inc(S["lg"][u], 1)


def route(nc, k, x4, lg, table):
    with Stage(nc, "rte") as s:
        A = lambda n, dt=F32: s.sb(n, [P, NT, E1], dt)
        pr, one1, one2, tmp = A("pr"), A("one1"), A("one2"), A("tmp")
        both, run, reset = (s.sb(n, [P, E1, NT]) for n in ("both", "run", "reset"))
        rank = s.sb("rank", [P, E1])
        ranki = s.sb("ranki", [P, E1], I32)
        base = s.sb("base", [P, E1])
        basei = s.sb("basei", [P, E1], I32)
        m = s.sb("m", [P, 2, NT])
        f = s.sb("f", [P, NT])
        kp = s.sb("kp", [P, 2, NT])
        slot = s.sb("slot", [P, 2, NT])
        dump = s.sb("dump", [P, 2, NT])
        numi = s.sb("numi", [P, 2, NT], I32)
        sloti = s.sb("sloti", [P, 2, NT], I32)
        before = s.sb("before", [P, P])
        rows = s.sb("rows", [P, 2, UT, ROW1])
        at = s.sb("at", [P, 2, 2, UT], I32)
        ps = s.pb("ps", [P, 512])
        s_set, s_sub, s_exp, s_run, s_pos, s_slot = (s.sem(n) for n in ("set", "sub", "exp", "run", "pos", "slot"))
        s_row, s_put, s_tick = s.sem2("row"), s.sem2("put"), s.sem("tick")
        block = s.block()
        te = lambda ap: ap.rearrange("p e t -> p t e")

        @block.gpsimd
        def _(pool):
            pool.memset(before[:, :], 1.0)
            pool.memset(reset[:, :, :], 1.0)
            pool.iota(ranki[:, :], pattern=[[-1, E1]], base=E1, channel_multiplier=0)
            pool.iota(basei[:, :], pattern=[[CAP1, E1]], base=0, channel_multiplier=0)
            pool.iota(numi[:, :, :], pattern=[[T, 2], [P, NT]], base=0, channel_multiplier=1)
            pool.drain()
            pool.memset(reset[:, :, 0:1], 0.0)
            pool.affine_select(out=before[:, :], in_=before[:, :], compare_op=ALU.is_gt, fill=0.0, base=0,
                               pattern=[[1, P]], channel_multiplier=-1)
            pool.tensor_copy(rank[:, :], ranki[:, :])
            pool.tensor_copy(base[:, :], basei[:, :])
            pool.tensor_copy(dump[:, :, :], numi[:, :, :]).then_inc(s_set, 1)
            pool.wait_ge(s_slot, 1)
            with pool.Fori(0, NU // 2) as j:
                for u in range(2):
                    wait_alone(pool, s_put[u], j * 16 * 2 * UT, s_tick)
                    pool.tensor_copy(at[:, u, :, :], sloti[:, :, bass.ds(j * 2 * UT + u * UT, UT)])
                    wait_alone(pool, s_row[u], j + 1, s_tick)
                    pool.drain()
                    for t in range(UT):
                        for q in range(2):
                            pool.indirect_dma_start(table,
                                                    bass.IndirectOffsetOnAxis(ap=at[:, u, q, t:t + 1], axis=0),
                                                    rows[:, u, t, :], None).then_inc(s_put[u], 16)
            for u in range(2):
                pool.wait_ge(s_put[u], NU // 2 * 16 * 2 * UT)

        @block.scalar
        def _(act):
            act.wait_ge(s_sub, 1)
            act.activation(pr[:, :, :], pr[:, :, :], ACT.Exp).then_inc(s_exp, 1)

        @block.vector
        def _(dve):
            dve.wait_ge(s_set, 1)
            dve.tensor_reduce(f[:, :], lg[:, :, :], AX, ALU.max)
            dve.drain()
            dve.tensor_tensor(pr[:, :, :], lg[:, :, :], bc(f[:, :], 2, E1), ALU.subtract).then_inc(s_sub, 1)
            dve.wait_ge(s_exp, 1)
            dve.tensor_reduce(f[:, :], pr[:, :, :], AX, ALU.add)
            dve.drain()
            dve.reciprocal(f[:, :], f[:, :])
            dve.drain()
            dve.tensor_tensor(pr[:, :, :], pr[:, :, :], bc(f[:, :], 2, E1), ALU.mult)
            dve.drain()
            for q, hot in enumerate((one1, one2)):
                dve.tensor_reduce(m[:, q, :], pr[:, :, :], AX, ALU.max)
                dve.drain()
                dve.tensor_tensor(tmp[:, :, :], pr[:, :, :], bc(m[:, q, :], 2, E1), ALU.is_equal)
                dve.drain()
                dve.tensor_tensor(tmp[:, :, :], tmp[:, :, :], bc(rank[:, :], 1, NT), ALU.mult)
                dve.drain()
                dve.tensor_reduce(f[:, :], tmp[:, :, :], AX, ALU.max)
                dve.drain()
                dve.tensor_tensor(hot[:, :, :], tmp[:, :, :], bc(f[:, :], 2, E1), ALU.is_equal)
                dve.drain()
                if q == 0:
                    dve.scalar_tensor_tensor(pr[:, :, :], hot[:, :, :], -2.0, pr[:, :, :], ALU.mult, ALU.add)
                    dve.drain()
            dve.tensor_tensor(te(both[:, :, :]), one1[:, :, :], one2[:, :, :], ALU.add)
            dve.drain()
            fl = lambda ap: ap.rearrange("p a b -> p (a b)")
            dve.tensor_tensor_scan(fl(run[:, :, :]), fl(reset[:, :, :]), fl(both[:, :, :]), 0.0, ALU.mult, ALU.add)
            dve.drain()
            dve.tensor_tensor(run[:, :, :], run[:, :, :], both[:, :, :], ALU.subtract).then_inc(s_run, 1)
            dve.drain()
            dve.wait_ge(s_pos, 1)
            dve.tensor_copy(run[:, :, :], ps[:, :].rearrange("p (e t) -> p e t", t=NT))
            dve.drain()
            dve.tensor_scalar(both[:, :, :], run[:, :, :], float(CAP1), None, ALU.is_lt)
            dve.tensor_tensor(run[:, :, :], run[:, :, :], bc(base[:, :], 2, NT), ALU.add)
            dve.tensor_tensor(f[:, :], m[:, 0, :], m[:, 1, :], ALU.add)
            dve.drain()
            dve.tensor_scalar(f[:, :], f[:, :], 1e-9, None, ALU.add)
            dve.drain()
            dve.reciprocal(f[:, :], f[:, :])
            dve.drain()
            dve.tensor_tensor(m[:, :, :], m[:, :, :], bc(f[:, :], 1, 2), ALU.mult)
            for q, hot in enumerate((one1, one2)):
                dve.tensor_tensor(tmp[:, :, :], hot[:, :, :], te(both[:, :, :]), ALU.mult)
                dve.drain()
                dve.tensor_reduce(kp[:, q, :], tmp[:, :, :], AX, ALU.add)
                dve.drain()
                dve.tensor_tensor(tmp[:, :, :], hot[:, :, :], te(run[:, :, :]), ALU.mult)
                dve.drain()
                dve.tensor_reduce(slot[:, q, :], tmp[:, :, :], AX, ALU.add)
                dve.drain()
            dve.tensor_tensor(m[:, :, :], m[:, :, :], kp[:, :, :], ALU.mult)
            dve.tensor_scalar(dump[:, :, :], dump[:, :, :], float(DUMP), None, ALU.add)
            dve.drain()
            dve.tensor_tensor(slot[:, :, :], slot[:, :, :], dump[:, :, :], ALU.subtract)
            dve.drain()
            dve.tensor_tensor(slot[:, :, :], slot[:, :, :], kp[:, :, :], ALU.mult)
            dve.drain()
            dve.tensor_tensor(slot[:, :, :], slot[:, :, :], dump[:, :, :], ALU.add)
            dve.tensor_tensor(f[:, :], m[:, 0, :], m[:, 1, :], ALU.add)
            dve.drain()
            dve.tensor_copy(sloti[:, :, :], slot[:, :, :]).then_inc(s_slot, 1)
            dve.tensor_scalar(f[:, :], f[:, :], 1e-9, None, ALU.add)
            dve.drain()
            dve.reciprocal(f[:, :], f[:, :])
            dve.drain()
            dve.tensor_tensor(m[:, :, :], m[:, :, :], bc(f[:, :], 1, 2), ALU.mult)
            dve.drain()
            for q, hot in enumerate((one1, one2)):
                dve.tensor_tensor(hot[:, :, :], hot[:, :, :], bc(m[:, q, :], 2, E1), ALU.mult)
            dve.drain()
            dve.tensor_tensor(x4[:, :, C + 1:ROW1], one1[:, :, :], one2[:, :, :], ALU.add)
            dve.tensor_scalar(x4[:, :, C], dump[:, 0, :], -float(DUMP), None, ALU.add)
            dve.drain()
            with dve.Fori(0, NU // 2) as j:
                for u in range(2):
                    dve.wait_ge(s_put[u], j * 16 * 2 * UT)
                    dve.tensor_copy(rows[:, u, :, :], x4[:, bass.ds(j * 2 * UT + u * UT, UT), :]).then_inc(s_row[u], 1)

        @block.tensor
        def _(pe):
            pe.wait_ge(s_set, 1)
            pe.wait_ge(s_run, 1)
            pe.matmul(ps[:, :], before[:, :], both[:, :, :].rearrange("p e t -> p (e t)"), start=True, stop=False)
            pe.matmul(ps[:, :], k["ones"][:, :], run[:, :, :].rearrange("p e t -> p (e t)"), start=False,
                      stop=True).then_inc(s_pos, 1)


def top2_experts(nc, k, d, table, ybuf2, out):
    NC1 = CAP1 // CH
    with Stage(nc, "mo2") as s:
        w1 = s.sb("w1", [P, 2, H])
        w2 = s.sb("w2", [P, 2, HT, C])
        b1 = s.sb("b1", [P, 2, HT])
        b2 = s.sb("b2", [P, 2, C])
        idc = s.sb("idc", [P, 2, CT], I32)
        xg = s.sb("xg", [P, 2, CT, ROW1])
        xT = s.sb("xT", [P, 2, CH])
        hs = s.sb("hs", [P, 2, HT, CH])
        yo = s.sb("yo", [P, 2, CT, C])
        psx = s.pb("psx", [P, 2, 512])
        psh = s.pb("psh", [P, 4, 512])
        pso = s.pb("pso", [P, 2, 512])
        S = {n: s.sem2(n) for n in ("w", "x", "T", "xT", "out", "y", "add", "wfree")}
        s_hid = [s.sem(f"hid{n}") for n in range(HT)]
        s_gel = [s.sem(f"gel{n}") for n in range(HT)]
        s_tick, s_o = s.sem("tick"), s.sem("o")
        block = s.block()
        NE2 = E1 // 2
        NW = 4
        BODY = 2 * NC1
        HALF = BODY // 2

        @block.sync
        def _(sp):
            def load(e, u):
                for dst, src in (
                    (w1[:, u, :], d["W1"][e, :, :].rearrange("a c h -> (a c) h")),
                    (w2[:, u, :, :], d["W2"][e, :, :].rearrange("a (k p) c -> p (a k) c", p=P)),
                    (b1[:, u, :], d["b1"][e, :].rearrange("a (k p) -> p (a k)", p=P)),
                    (b2[:, u, :], bc(d["b2"][e, :], 0, P).rearrange("q a c -> q (a c)")),
                ):
                    sp.dma_start(dst, src, allow_slow_non_contiguous=True).then_inc(S["w"][u], 16)

            with sp.Fori(0, NE2) as j:
                for i in range(BODY):
                    u = i % 2
                    if i % NC1 == 0:
                        sp.wait_ge(S["wfree"][i // NC1], j)
                        load(bass.ds(2 * j + i // NC1, 1), i // NC1)
                    sp.wait_ge(S["y"][u], j * HALF + i // 2)
                    sp.dma_start(xg[:, u, :, :], table[bass.ds(j * BODY * CH + i * CH, CH), :]
                                 .rearrange("(t p) c -> p t c", p=P)).then_inc(S["x"][u], 16)
            for u in range(2):
                sp.wait_ge(S["add"][u], NE2 * HALF * 16 * CT)
            sp.dma_start(out.rearrange("a b c -> (a b) c"), ybuf2[0:T, :]).then_inc(s_o, 16)
            sp.wait_ge(s_o, 16)

        @block.gpsimd
        def _(pool):
            with pool.Fori(0, NE2) as j:
                for i in range(BODY):
                    u = i % 2
                    wait_alone(pool, S["y"][u], j * HALF + i // 2 + 1, s_tick)
                    if i % NC1 == 0:
                        for q in range(2):
                            wait_alone(pool, S["add"][q], (j * HALF + (i + 1 - q) // 2) * 16 * CT, s_tick)
                    for t in range(CT):
                        pool.indirect_dma_start(ybuf2, bass.IndirectOffsetOnAxis(ap=idc[:, u, t:t + 1], axis=0),
                                                yo[:, u, t, :], None, compute_op=ALU.add).then_inc(S["add"][u], 16)

        @block.scalar
        def _(act):
            with act.Fori(0, NE2) as j:
                for i in range(BODY):
                    u, e = i % 2, i // NC1
                    if i % NC1 == 0:
                        act.wait_ge(S["w"][e], (j + 1) * 16 * NW)
                    for m in range(HT):
                        act.wait_ge(s_hid[m], j * BODY + i + 1)
                        act.activation(hs[:, u, m, :], psh[:, m, :], ACT.Gelu, bias=b1[:, e, m:m + 1])\
                            .then_inc(s_gel[m], 1)

        @block.vector
        def _(dve):
            with dve.Fori(0, NE2) as j:
                def evac(i):
                    u = i % 2
                    dve.wait_ge(S["T"][u], j * HALF + i // 2 + 1)
                    dve.tensor_copy(xT[:, u, :], psx[:, u, :]).then_inc(S["xT"][u], 1)

                def finish(i):
                    u, e = i % 2, i // NC1
                    dve.wait_ge(S["out"][u], j * HALF + i // 2 + 1)
                    dve.wait_ge(S["add"][u], (j * HALF + i // 2) * 16 * CT)
                    dve.tensor_copy(idc[:, u, :], xg[:, u, :, C])
                    dve.tensor_tensor(yo[:, u, :, :], pso[:, u, :].rearrange("p (t c) -> p t c", c=C),
                                      bc(b2[:, e, :], 1, CT), ALU.add)
                    dve.drain()
                    for t in range(CT):
                        last = dve.tensor_scalar(yo[:, u, t, :], yo[:, u, t, :],
                                                 xg[:, u, t, bass.ds(2 * j + e + C + 1, 1)], None, ALU.mult)
                    last.then_inc(S["y"][u], 1)
                    if i % NC1 == NC1 - 1:
                        dve.drain()
                        dve.sem_inc(S["wfree"][e], 1)

                for i in range(0, BODY, 2):
                    evac(i)
                    evac(i + 1)
                    finish(i)
                    finish(i + 1)

        @block.tensor
        def _(pe):
            with pe.Fori(0, NE2) as j:
                def gathered(i):
                    u = i % 2
                    pe.wait_ge(S["x"][u], (j * HALF + i // 2 + 1) * 16)
                    for t in range(CT):
                        last = pe.transpose(psx[:, u, t * P:(t + 1) * P], xg[:, u, t, 0:C], k["ident"][:, :])
                    last.then_inc(S["T"][u], 1)

                def up(i):
                    u, e = i % 2, i // NC1
                    if i % NC1 == 0:
                        pe.wait_ge(S["w"][e], (j + 1) * 16 * NW)
                    pe.wait_ge(S["xT"][u], j * HALF + i // 2 + 1)
                    for m in range(HT):
                        pe.wait_ge(s_gel[m], j * BODY + i)
                        pe.matmul(psh[:, m, :], w1[:, e, m * P:(m + 1) * P], xT[:, u, :], start=True,
                                  stop=True).then_inc(s_hid[m], 1)

                def down(i):
                    u, e = i % 2, i // NC1
                    pe.wait_ge(S["y"][u], j * HALF + i // 2)
                    for m in range(HT):
                        pe.wait_ge(s_gel[m], j * BODY + i + 1)
                    for t in range(CT):
                        for m in range(HT):
                            last = pe.matmul(pso[:, u, t * P:(t + 1) * P], hs[:, u, m, t * P:(t + 1) * P],
                                             w2[:, e, m, :], start=(m == 0), stop=(m == HT - 1))
                    last.then_inc(S["out"][u], 1)

                for i in range(0, BODY, 2):
                    for step in (gathered, up, down):
                        step(i)
                        step(i + 1)


def tower(nc, d, out):
    xrows = nc.dram_tensor("xrows", [T, ROW], F32, kind="Internal").ap()
    ybuf = nc.dram_tensor("ybuf", [T, C], F32, kind="Internal").ap()
    ybuf2 = nc.dram_tensor("ybuf2", [T + CAP1, C], F32, kind="Internal").ap()
    table = nc.dram_tensor("table", [DUMP + 2 * T, ROW1], F32, kind="Internal").ap()
    part = lambda tag: {n[len(tag):]: a for n, a in d.items() if n.startswith(tag)}
    with Stage(nc, "top") as s:
        k = {n: s.sb(n, [P, P]) for n in ("ident", "cent", "mean", "ones", "half_mean")}
        k["nhalf"] = s.sb("nhalf", [P, 64])
        k["half"] = s.sb("half", [P, 64])
        hT = s.sb("hT", [P, T])
        constants(nc, k)
        with Stage(nc, "tok") as st:
            w = {"w1": st.sb("w1", [P, L, 2 * C]), "w2": st.sb("w2", [P, L, 2, C]), "cw": st.sb("cw", [P, L + 1, KC]),
                 "cb": st.sb("cb", [P, L + 1]), "gw": st.sb("gw", [P, L, 2]), "b1": st.sb("b1", [P, L, 2]),
                 "b2": st.sb("b2", [P, L])}
            block_weights(nc, k, w, part("L0_tok_"))
            token_embedding(nc, k, d["x"], d["L0_tok_emb_table"], d["L0_tok_pos_emb"], hT)
            convnext_blocks(nc, k, w, hT, table, ybuf2)
        big = s.sb("big", [P, NT * ROW1])
        x2T = big[:, 0:T]
        x4 = big[:, :].rearrange("p (t c) -> p t c", c=ROW1)
        lg = s.sb("lg", [P, NT, E0])
        with Stage(nc, "rec") as st:
            w = {"win": st.sb("win", [P, C]), "bin": st.sb("bin", [P, 1]), "bc": st.sb("bcw", [P, 3, P]),
                 "bA": st.sb("bA", [P, 1]), "bsw": st.sb("bsw", [P, 1]), "decay": st.sb("decay", [P, UNIT]),
                 "cos": st.sb("cos", [P, SEQ]), "sin": st.sb("sin", [P, SEQ]), "sinr": st.sb("sinr", [P, SEQ]),
                 "cp": st.sb("cp", [P, S_]), "cq": st.sb("cq", [P, S_]), "wout": st.sb("wout", [S_ + 1, C]),
                 "gate": st.sb("gate", [P, E0])}
            lru_weights(nc, k, w, {**part("L0_attn_"), "gate_w": d["L0_ffn_gate_w"]})
            lru_block(nc, k, w, hT, x2T, lg, xrows, ybuf)
        shared = hT[:, :].rearrange("p (t c) -> p t c", c=C)
        idx = s.sb("idx", [P, E0, CAP0 // P], I32)
        with Stage(nc, "exp") as st:
            pT = st.sb("pT", [P, T // SEG])
            softmax_experts(nc, k, lg, pT, xrows)
            select_and_shared(nc, k, part("L0_ffn_"), x2T, pT, idx, shared)
        experts_choice(nc, k, part("L0_ffn_"), idx, xrows, ybuf)
        lg8 = lg[:, 0:NT // 2, :].rearrange("p t (a e) -> p (t a) e", e=E1)
        attention_block(nc, k, {**part("L1_attn_"), **part("L1_ffn_")}, shared, ybuf, x4, lg8, ybuf2)
        route(nc, k, x4, lg8, table)
        top2_experts(nc, k, part("L1_ffn_"), table, ybuf2, out)


_INS = ["x"] + ["L0_tok_" + n for n in ("emb_table", "pos_emb", "conv_w", "conv_b", "ln_g", "ln_b", "w1", "b1", "grn_w", "grn_b",
                                        "w2", "b2")] \
    + ["L0_attn_" + n for n in ("ln_w", "ln_b", "W_in", "conv_w", "conv_b", "nu_log", "theta_log", "gamma_log", "B_re",
                                "B_im", "C_re", "C_im", "W_out", "b_out")] \
    + ["L0_ffn_" + n for n in ("gate_w", "w1", "b1", "w2", "b2", "sw1", "sb1", "sw2", "sb2")] \
    + ["L1_attn_" + n for n in ("w_qkv", "b_qkv", "w_dconv", "w_proj", "b_proj")] \
    + ["L1_ffn_" + n for n in ("Wr", "br", "W1", "b1", "W2", "b2")]


def kernel(**inputs):
    import numpy as _np
    import concourse.bacc as _bacc
    from concourse import mybir as _mybir
    from concourse.bass_utils import run_bass_kernel_spmd as _run

    nc = _bacc.Bacc("TRN2", target_bir_lowering=False, num_devices=1)
    arrays, d = {}, {}
    for name in _INS:
        a = _np.ascontiguousarray(inputs[name])
        arrays[f"{name}_dram"] = a
        d[name] = nc.dram_tensor(f"{name}_dram", a.shape, _mybir.dt.from_np(a.dtype), kind="ExternalInput").ap()
    out = nc.dram_tensor("out_dram", (32, SEQ, C), _mybir.dt.from_np(_np.dtype("float32")), kind="ExternalOutput").ap()
    tower(nc, d, out)
    r = _run(nc, [arrays], core_ids=[0])
    return r.results[0]["out_dram"]
```

```python
from contextlib import ExitStack

import concourse.bass as bass
from concourse import mybir

F32 = mybir.dt.float32
BF16 = mybir.dt.bfloat16
I32 = mybir.dt.int32
ALU = mybir.AluOpType
ACT = mybir.ActivationFunctionType
AX = mybir.AxisListType.X

P = 128
C = 128
T = 8192
SEQ = 256
UNIT = 1024
NU = T // UNIT
UB = UNIT // SEQ
UT = UNIT // P
NT = T // P
L = 4
KC = 7
VOCAB_ROWS = 8001


class Stage:

    def __init__(self, nc, tag):
        self.nc, self.tag, self.ctx, self.sems = nc, tag, ExitStack(), []

    def __enter__(self):
        self.ctx.__enter__()
        return self

    def __exit__(self, *a):
        self.ctx.__exit__(*a)
        if self.sems and a[0] is None:
            self.nc.clear_and_free_semaphores(self.sems)
            self.nc.all_engine_barrier()

    def sb(self, name, shape, dt=F32):
        return self.ctx.enter_context(self.nc.sbuf_tensor(f"{self.tag}_{name}", shape, dt))

    def pb(self, name, shape, dt=F32):
        return self.ctx.enter_context(self.nc.psum_tensor(f"{self.tag}_{name}", shape, dt))

    def sem(self, name):
        self.sems.append(self.nc.alloc_semaphore(f"{self.tag}_{name}"))
        return self.sems[-1]

    def sem2(self, name):
        return [self.sem(f"{name}{u}") for u in range(2)]

    def block(self):
        return self.ctx.enter_context(self.nc.Block())


def bc(ap, at, n):
    pat = [list(x) for x in ap.ap]
    pat.insert(at, [0, n])
    return bass.AP(tensor=ap.tensor, offset=ap.offset, ap=pat)


def wait_alone(eng, sem, value, tick):
    eng.wait_ge(sem, value)
    eng.sem_inc(tick, 1)


def pairs(eng, step, n=NU // 2):
    step(0, True)
    with eng.Fori(1, n - 1) as j:
        step(j, True)
    step(n - 1, False)


def after_first(j):
    return not isinstance(j, int) or j > 0


def constants(nc, k):
    with Stage(nc, "cst") as s:
        s_m, s_i, s_d = s.sem("memset"), s.sem("ident"), s.sem("done")
        block = s.block()

        @block.gpsimd
        def _(pool):
            pool.memset(k["ident"][:, :], 0.0)
            pool.memset(k["mean"][:, :], 1.0 / C)
            pool.memset(k["ones"][:, :], 1.0)
            pool.memset(k["nhalf"][:, :], -0.5)
            pool.memset(k["half"][:, :], 0.5)
            pool.memset(k["half_mean"][:, :], 0.5 / C)
            pool.drain()
            pool.affine_select(out=k["ident"][:, :], in_=k["ident"][:, :], compare_op=ALU.not_equal, fill=1.0,
                               base=0, pattern=[[-1, P]], channel_multiplier=1)
            pool.drain()
            pool.tensor_tensor(k["cent"][:, :], k["ident"][:, :], k["mean"][:, :], ALU.subtract)


def token_embedding(nc, k, x, emb, pos, hT):
    with Stage(nc, "emb") as s:
        ids = s.sb("ids", [NT, P], I32)
        idf = s.sb("idf", [NT, P])
        idx = s.sb("idx", [P, NT], I32)
        idc = s.sb("idc", [P, 2, UT], I32)
        rows = s.sb("rows", [P, 2, UT, C])
        posr = s.sb("posr", [P, 2, C])
        posT = s.sb("posT", [P, SEQ])
        ps = s.pb("ps", [P, 2, UNIT])
        ps_pos = s.pb("pspos", [P, SEQ])
        ps_ids = s.pb("psids", [P, NT])
        s_in, s_idf, s_tr, s_idx = s.sem("in"), s.sem("idf"), s.sem("tr"), s.sem("idx")
        s_rows, s_free, s_hT, s_ps = s.sem2("rows"), s.sem2("free"), s.sem2("hT"), s.sem2("ps")
        s_hold = s.sem("hold")
        block = s.block()

        @block.sync
        def _(sp):
            sp.dma_start(ids[:, :], x.rearrange("a (b p) -> (a b) p", p=P)).then_inc(s_in, 16)
            sp.dma_start(posr[:, :, :], pos[0:SEQ, :].rearrange("(a p) c -> p a c", p=P)).then_inc(s_in, 16)

        @block.vector
        def _(dve):
            dve.wait_ge(s_in, 32)
            dve.tensor_scalar(idf[:, :], ids[:, :], float(VOCAB_ROWS - 1), None, ALU.min).then_inc(s_idf, 1)
            dve.wait_ge(s_tr, 1)
            dve.tensor_copy(idx[:, :], ps_ids[:, :])
            dve.tensor_copy(posT[:, :], ps_pos[:, :]).then_inc(s_idx, 1)
            dve.drain()
            with dve.Fori(0, NU // 2) as j:
                for u in range(2):
                    dve.wait_ge(s_ps[u], j + 1)
                    dst = hT[:, bass.ds(j * 2 * UNIT + u * UNIT, UNIT)].rearrange("p (b t) -> p b t", t=SEQ)
                    dve.tensor_tensor(dst, ps[:, u, :].rearrange("p (b t) -> p b t", t=SEQ),
                                      bc(posT[:, :], 1, UB), ALU.add).then_inc(s_hT[u], 1)

        @block.gpsimd
        def _(pool):
            pool.wait_ge(s_idx, 1)
            with pool.Fori(0, NU // 2) as j:
                for u in range(2):
                    pool.wait_ge(s_free[u], j + 1)
                    pool.tensor_copy(idc[:, u, :], idx[:, bass.ds(j * 2 * UT + u * UT, UT)])
                    pool.drain()
                    for t in range(UT):
                        pool.indirect_dma_start(rows[:, u, t, :], None, emb,
                                                bass.IndirectOffsetOnAxis(ap=idc[:, u, t:t + 1], axis=0))\
                            .then_inc(s_rows[u], 16)

        @block.tensor
        def _(pe):
            pe.sem_inc(s_free[0], 1)
            pe.sem_inc(s_free[1], 1)
            pe.wait_ge(s_idf, 1)
            pe.transpose(ps_ids[:, :], idf[:, :], k["ident"][0:NT, 0:NT])
            pe.transpose(ps_pos[:, 0:P], posr[:, 0, :], k["ident"][:, :])
            pe.transpose(ps_pos[:, P:SEQ], posr[:, 1, :], k["ident"][:, :]).then_inc(s_tr, 1)
            with pe.Fori(0, NU // 2) as j:
                for u in range(2):
                    pe.wait_ge(s_rows[u], j * 16 * UT + 16 * UT)
                    for t in range(UT):
                        last = pe.transpose(ps[:, u, t * P:(t + 1) * P], rows[:, u, t, :], k["ident"][:, :])
                        if t == UT - 1:
                            last.then_inc(s_ps[u], 1)
                    pe.wait_ge(s_hT[u], j + 1)
                    pe.sem_inc(s_free[u], 1)


def block_weights(nc, k, w, d):
    with Stage(nc, "bwt") as s:
        w1r = s.sb("w1r", [P, L, 2 * C])
        w1g = s.sb("w1g", [P, L, 2 * C])
        b1 = s.sb("b1", [P, L, 2])
        b2 = s.sb("b2", [P, L])
        lg = s.sb("lg", [P, L])
        lb = s.sb("lb", [P, L])
        gb = s.sb("gb", [P, L, 2])
        ps_w = s.pb("psw", [P, L, 2 * C])
        ps_b = s.pb("psb", [P, 32])
        s_in, s_g, s_mm = s.sem("in"), s.sem("g"), s.sem("mm")
        block = s.block()
        NIN = 10

        @block.sync
        def _(sp):
            for dst, src in (
                (w1r[:, :, :], d["w1"].rearrange("l c n -> c l n")),
                (w["w2"][:, :, :, :], d["w2"].rearrange("l (h p) c -> p l h c", p=P)),
                (w["cw"][:, 0:L, :], d["conv_w"].rearrange("l c o k -> c l (o k)")),
                (w["cb"][:, 0:L], d["conv_b"].rearrange("l c -> c l")),
                (lg[:, :], d["ln_g"].rearrange("l c -> c l")),
                (lb[:, :], d["ln_b"].rearrange("l c -> c l")),
                (b1[:, :, :], d["b1"].rearrange("l (h p) -> p l h", p=P)),
                (w["gw"][:, :, :], d["grn_w"].rearrange("l (h p) -> p l h", p=P)),
                (gb[:, :, :], d["grn_b"].rearrange("l (h p) -> p l h", p=P)),
                (b2[:, :], d["b2"].rearrange("l c -> c l")),
            ):
                sp.dma_start(dst, src, allow_slow_non_contiguous=True).then_inc(s_in, 16)

        @block.vector
        def _(dve):
            dve.wait_ge(s_in, 16 * NIN)
            dve.memset(w["cw"][:, L, :], 0.0)
            dve.memset(w["cb"][:, L:L + 1], 0.0)
            dve.tensor_tensor(w1g[:, :, :], w1r[:, :, :], bc(lg[:, :], 2, 2 * C), ALU.mult).then_inc(s_g, 1)
            dve.wait_ge(s_mm, 1)
            dve.tensor_copy(w["w1"][:, :, :], ps_w[:, :, :])
            dve.tensor_tensor(w["b1"][:, :, :], b1[:, :, :],
                              ps_b[:, 0:2 * L].rearrange("p (l h) -> p l h", h=2), ALU.add)
            dve.tensor_tensor(w["b2"][:, :], b2[:, :], ps_b[:, 2 * L:3 * L], ALU.add)

        @block.tensor
        def _(pe):
            pe.wait_ge(s_in, 16 * NIN)
            pe.wait_ge(s_g, 1)
            for l in range(L):
                pe.matmul(ps_w[:, l, :], k["cent"][:, :], w1g[:, l, :], start=True, stop=True)
                for h in range(2):
                    pe.matmul(ps_b[:, 2 * l + h:2 * l + h + 1], w1r[:, l, h * C:(h + 1) * C], lb[:, l:l + 1],
                              start=True, stop=True)
                for h in range(2):
                    last = pe.matmul(ps_b[:, 2 * L + l:2 * L + l + 1], w["w2"][:, l, h, :], gb[:, l, h:h + 1],
                                     start=(h == 0), stop=(h == 1))
            last.then_inc(s_mm, 1)


def convnext_blocks(nc, k, w, hT, table, ybuf2):
    NALL = L * NU
    LAG = 3
    NP = NU // 2
    with Stage(nc, "cnx") as s:
        y = s.sb("y", [P, 2, UNIT])
        ysq = s.sb("ysq", [P, 2, UNIT])
        yn = s.sb("yn", [P, 2, UNIT])
        gl = s.sb("gl", [P, 2, 2, UNIT])
        junk = s.sb("junk", [P, 2, UB, SEQ], BF16)
        w1c = s.sb("w1c", [P, 2 * C])
        w2s = s.sb("w2s", [P, 2, 2, UB, C])
        out = s.sb("out", [P, 2, UNIT])
        st = s.sb("st", [P, 2, UT])
        rs = s.sb("rs", [P, 2, UT])
        ss = s.sb("ss", [P, 2, 2, UB])
        g = s.sb("g", [P, 2, 2, UB])
        gm = s.sb("gm", [P, 2, UB])
        gs = s.sb("gs", [P, 2, 2, UB])
        ps_wide = s.pb("pswide", [P, UNIT])
        ps_inv = s.pb("psinv", [P, UNIT])
        ps_out = s.pb("psout", [P, UNIT])
        ps_c = s.pb("psc", [P, UNIT])
        ps_gm = ps_out[:, 0:UB]
        S = {n: s.sem(n) for n in ("mid", "conv", "cent", "sq", "stat", "stc", "rs", "inv", "norm", "w1", "gelu", "ss", "g",
                                   "gm", "sc", "w2s", "w2", "out", "wl")}
        s_tick = s.sem("tick")
        CE = CAP1 // P
        empty = s.sb("empty", [P, CE, ROW1])
        num = s.sb("num", [P, CE], I32)
        s_empty, s_fill = s.sem("empty"), s.sem("fill")
        block = s.block()
        mid = KC // 2

        def seqs(ap):
            return ap.rearrange("p (b t) -> p b t", t=SEQ)

        class Item:

            def __init__(self, j, u, lag):
                self.v = (u - lag) & 1
                q = j + (u - lag) // 2
                self.n = q * 2 + self.v
                self.there = not isinstance(j, int) or 0 <= self.n < NALL
                if self.there:
                    self.l = q // NP
                    self.col = (q & (NP - 1)) * (2 * UNIT) + self.v * UNIT

            def unit(self):
                return hT[:, self.col:self.col + UNIT] if isinstance(self.col, int) else hT[:, bass.ds(self.col, UNIT)]

        def one(ap, i):
            return ap[:, i:i + 1] if isinstance(i, int) else ap[:, bass.ds(i, 1)]

        def steps(eng, step):
            fill = (LAG + 1) // 2
            for j in range(fill):
                step(j, 0)
                step(j, 1)
            with eng.Fori(fill, NALL // 2) as j:
                step(j, 0)
                step(j, 1)
            for n in range(NALL, NALL + LAG):
                step(n // 2, n % 2)

        @block.sync
        def _(sp):
            sp.wait_ge(s_empty, 1)
            for e in range(E1):
                sp.dma_start(table[e * CAP1:(e + 1) * CAP1, :].rearrange("(t p) c -> p t c", p=P), empty[:, :, :])\
                    .then_inc(s_fill, 16)
            sp.dma_start(ybuf2[T:T + CAP1, :].rearrange("(t p) c -> p t c", p=P), empty[:, :, 0:C]).then_inc(s_fill, 16)
            sp.wait_ge(s_fill, 16 * (E1 + 1))

        @block.vector
        def _(dve):
            def taps(i, some):
                src, dst = seqs(i.unit()), seqs(y[:, i.v, :])
                for t in some:
                    o = t - mid
                    a, b = max(0, -o), SEQ - max(0, o)
                    last = dve.scalar_tensor_tensor(dst[:, :, a:b], src[:, :, a + o:b + o],
                                                    w["cw"][:, i.l, t:t + 1], dst[:, :, a:b], ALU.mult, ALU.add)
                    if t < KC - 1:
                        dve.drain()
                return last

            def step(j, u):
                this, norm, last = Item(j, u, 0), Item(j, u, 1), Item(j, u, 3)
                if last.there:
                    v = last.v
                    dve.wait_ge(S["gm"], last.n + 1)
                    dve.tensor_scalar(gm[:, v, :], ps_gm, 1e-6, None, ALU.add)
                    dve.drain()
                    dve.reciprocal(gm[:, v, :], gm[:, v, :])
                    dve.drain()
                    dve.tensor_tensor(gs[:, v, :, :], g[:, v, :, :], bc(gm[:, v, :], 1, 2), ALU.mult)
                    dve.drain()
                    for h in range(2):
                        scaled = dve.tensor_scalar(gs[:, v, h, :], gs[:, v, h, :], w["gw"][:, last.l, h:h + 1], 1.0,
                                                   ALU.mult, ALU.add)
                    scaled.then_inc(S["sc"], 1)
                if this.there:
                    dve.wait_ge(S["mid"], this.n + 1)
                    taps(this, [t for t in range(KC) if t != mid]).then_inc(S["conv"], 1)
                if norm.there:
                    dve.wait_ge(S["inv"], norm.n + 1)
                    dve.tensor_tensor(yn[:, norm.v, :], y[:, norm.v, :], ps_inv[:, :], ALU.mult)\
                        .then_inc(S["norm"], 1)

            steps(dve, step)

        @block.scalar
        def _(act):
            def middle(i):
                act.activation(y[:, i.v, :], i.unit(), ACT.Identity, bias=one(w["cb"], i.l),
                               scale=w["cw"][:, i.l, mid:mid + 1]).then_inc(S["mid"], 1)

            def squares(i, h):
                for b in range(UB):
                    last = act.activation(junk[:, h, b, :], gl[:, i.v, h, b * SEQ:(b + 1) * SEQ], ACT.Square,
                                          accum_out=ss[:, i.v, h, b:b + 1])
                return last

            middle(Item(0, 0, 0))

            def step(j, u):
                this, after, wide, small = Item(j, u, 0), Item(j, u, -1), Item(j, u, 1), Item(j, u, 2)
                if after.there:
                    if wide.there:
                        wait_alone(act, S["norm"], wide.n + 1, s_tick)
                    middle(after)
                if this.there:
                    act.wait_ge(S["cent"], this.n + 1)
                    act.activation(ysq[:, this.v, :], ps_c[:, :], ACT.Square).then_inc(S["sq"], 1)
                if wide.there:
                    wait_alone(act, S["w1"], wide.n * 2 + 1, s_tick)
                    act.activation(gl[:, wide.v, 0, :], ps_wide[:, :], ACT.Gelu, bias=w["b1"][:, wide.l, 0:1])\
                        .then_inc(S["gelu"], 1)
                if this.there:
                    act.wait_ge(S["stat"], this.n + 1)
                    act.activation(st[:, this.v, :], ps_c[:, 0:UT], ACT.Copy)\
                        .then_inc(S["stc"], 1)
                if wide.there:
                    act.drain()
                    squares(wide, 0)
                    wait_alone(act, S["w1"], wide.n * 2 + 2, s_tick)
                    act.activation(gl[:, wide.v, 1, :], ps_wide[:, :], ACT.Gelu, bias=w["b1"][:, wide.l, 1:2])\
                        .then_inc(S["gelu"], 1)
                    act.drain()
                    squares(wide, 1).then_inc(S["ss"], 1)
                if small.there:
                    wait_alone(act, S["w2"], small.n + 1, s_tick)
                    act.activation(out[:, small.v, :], ps_out[:, :], ACT.Identity, bias=one(w["b2"], small.l))\
                        .then_inc(S["out"], 1)

            steps(act, step)

        @block.gpsimd
        def _(pool):
            pool.memset(empty[:, :, :], 0.0)
            pool.iota(num[:, :], pattern=[[P, CE]], base=T, channel_multiplier=1)
            pool.drain()
            pool.tensor_copy(empty[:, :, C], num[:, :]).then_inc(s_empty, 1)

            def step(j, u):
                i = Item(j, u, 2)
                if i.there:
                    wait_alone(pool, S["sc"], i.n + 1, s_tick)
                    for h in range(2):
                        last = pool.tensor_tensor(w2s[:, i.v, h, :, :], bc(w["w2"][:, i.l, h, :], 1, UB),
                                                  bc(gs[:, i.v, h, :], 2, C), ALU.mult)
                    last.then_inc(S["w2s"], 1)
                i = Item(j, u, 0)
                if i.there:
                    wait_alone(pool, S["stc"], i.n + 1, s_tick)
                    pool.tensor_scalar(rs[:, i.v, :], st[:, i.v, :], 1e-6, None, ALU.add)
                    pool.drain()
                    pool.tensor_tensor(rs[:, i.v, :], rs[:, i.v, :], k["nhalf"][:, 0:UT], ALU.pow)\
                        .then_inc(S["rs"], 1)
                    if u == 0:
                        if after_first(j):
                            wait_alone(pool, S["w1"], i.n * 2, s_tick)
                        pool.tensor_copy(w1c[:, :], w["w1"][:, i.l, :]).then_inc(S["wl"], 1)
                i = Item(j, u, 1)
                if i.there:
                    pool.wait_ge(S["ss"], i.n + 1)
                    pool.tensor_tensor(g[:, i.v, :, :], ss[:, i.v, :, :],
                                       k["half"][:, 0:2 * UB].rearrange("p (a b) -> p a b", a=2), ALU.pow)\
                        .then_inc(S["g"], 1)
                i = Item(j, u, 2)
                if i.there:
                    wait_alone(pool, S["out"], i.n + 1, s_tick)
                    pool.tensor_tensor(i.unit(), i.unit(), out[:, i.v, :], ALU.add)

            steps(pool, step)

        @block.tensor
        def _(pe):
            def widen(i, h):
                for c in range(2):
                    last = pe.matmul(ps_wide[:, c * 512:(c + 1) * 512], w1c[:, h * C:(h + 1) * C],
                                     yn[:, i.v, c * 512:(c + 1) * 512], start=True, stop=True)
                last.then_inc(S["w1"], 1)

            def narrow(i):
                for b in range(UB):
                    for h in range(2):
                        last = pe.matmul(ps_out[:, b * SEQ:(b + 1) * SEQ], w2s[:, i.v, h, b, :],
                                         gl[:, i.v, h, b * SEQ:(b + 1) * SEQ], start=(h == 0), stop=(h == 1))
                last.then_inc(S["w2"], 1)

            def step(j, u):
                this, wide, small = Item(j, u, 0), Item(j, u, 1), Item(j, u, 2)
                if this.there:
                    pe.wait_ge(S["conv"], this.n + 1)
                    for c in range(2):
                        last = pe.matmul(ps_c[:, c * 512:(c + 1) * 512], k["cent"][:, :],
                                         y[:, this.v, c * 512:(c + 1) * 512], start=True, stop=True)
                    last.then_inc(S["cent"], 1)
                if wide.there:
                    if u == 1:
                        pe.wait_ge(S["wl"], j + 1)
                    pe.wait_ge(S["norm"], wide.n + 1)
                    if small.there:
                        pe.wait_ge(S["gelu"], wide.n * 2)
                    widen(wide, 0)
                if this.there:
                    pe.wait_ge(S["sq"], this.n + 1)
                    for t in range(UT):
                        last = pe.matmul(ps_c[:, t:t + 1], ysq[:, this.v, t * P:(t + 1) * P], k["mean"][:, 0:1],
                                         start=True, stop=True)
                    last.then_inc(S["stat"], 1)
                if wide.there:
                    pe.wait_ge(S["gelu"], wide.n * 2 + 1)
                    widen(wide, 1)
                if small.there:
                    pe.wait_ge(S["w2s"], small.n + 1)
                    narrow(small)
                if this.there:
                    pe.wait_ge(S["rs"], this.n + 1)
                    for t in range(UT):
                        last = pe.matmul(ps_inv[:, t * P:(t + 1) * P], bc(rs[:, this.v, t:t + 1], 1, P)[:, :, 0],
                                         k["ident"][:, :], start=True, stop=True)
                    last.then_inc(S["inv"], 1)
                if wide.there:
                    pe.wait_ge(S["g"], wide.n + 1)
                    if small.there:
                        pe.wait_ge(S["out"], small.n + 1)
                    for h in range(2):
                        last = pe.matmul(ps_gm, k["half_mean"][:, :], g[:, wide.v, h, :], start=(h == 0), stop=(h == 1))
                    last.then_inc(S["gm"], 1)

            steps(pe, step)



S_ = 64
KA = 5
E0 = 16
ROW = C + E0
TWO_PI_HI, TWO_PI_LO = 6.28125, 0.0019353071795864769
PI = 3.14159265358979
ROUND = 12582912.0


def lru_weights(nc, k, w, d):
    with Stage(nc, "lwt") as s:
        wi = s.sb("wi", [P, C])
        wit = s.sb("wit", [P, C])
        lnw = s.sb("lnw", [P, 2])
        cw = s.sb("cw", [S_, S_, KA])
        cwt = s.sb("cwt", [S_, KA + 1, S_])
        cb = s.sb("cb", [S_, 1])
        par = s.sb("par", [P, 3])
        ex = s.sb("ex", [P, 3])
        lm = s.sb("lm", [P, 1])
        lam = s.sb("lam", [P, 1])
        ang = s.sb("ang", [P, 2])
        q = s.sb("q", [P, 2])
        tr = s.sb("tr", [P, 2])
        bn = s.sb("bn", [P, S_])
        bnT = s.sb("bnT", [S_, P])
        cc = s.sb("cc", [S_, 2, 2, S_])
        wo = s.sb("wo", [P, S_])
        em = s.sb("em", [P, 2])
        en = s.sb("en", [P, 2])
        mix = s.sb("mix", [P, 2, SEQ // 2])
        ps = s.pb("ps", [P, 8, 512])
        s_in, s_ex, s_lm, s_q, s_sin = s.sem("in"), s.sem("ex"), s.sem("lm"), s.sem("q"), s.sem("sin")
        s_bn, s_cc, s_t, s_bnT, s_m, s_cwt, s_wit = (s.sem(n) for n in ("bn", "cc", "t", "bnT", "m", "cwt", "wit"))
        block = s.block()
        NIN = 21

        @block.sync
        def _(sp):
            col = lambda a: a.rearrange("(p a) -> p a", a=1)
            for dst, src in (
                (wi[0:S_, :], d["W_in"][S_:2 * S_, :]), (wi[S_:P, :], d["W_in"][0:S_, :]),
                (lnw[:, 0:1], col(d["ln_w"])), (lnw[:, 1:2], col(d["ln_b"])),
                (cw[:, :, :], d["conv_w"]), (cb[:, :], col(d["conv_b"])),
                (par[0:S_, 0:1], col(d["nu_log"])), (par[S_:P, 0:1], col(d["nu_log"])),
                (par[0:S_, 1:2], col(d["theta_log"])), (par[S_:P, 1:2], col(d["theta_log"])),
                (par[0:S_, 2:3], col(d["gamma_log"])), (par[S_:P, 2:3], col(d["gamma_log"])),
                (bn[0:S_, :], d["B_re"]), (bn[S_:P, :], d["B_im"]),
                (cc[:, 0, 0, :], d["C_re"]), (cc[:, 0, 1, :], d["C_im"]),
                (cc[:, 1, 0, :], d["C_im"]), (cc[:, 1, 1, :], d["C_re"]),
                (wo[:, :], d["W_out"]), (w["gate"][:, :], d["gate_w"]), (w["wout"][S_:S_ + 1, :], d["b_out"].rearrange("(a n) -> a n", a=1)),
            ):
                sp.dma_start(dst, src, allow_slow_non_contiguous=True).then_inc(s_in, 16)

        @block.scalar
        def _(act):
            act.wait_ge(s_in, 16 * NIN)
            act.activation(ex[:, :], par[:, :], ACT.Exp).then_inc(s_ex, 1)
            act.drain()
            act.activation(lm[:, :], ex[:, 0:1], ACT.Exp, scale=-1.0).then_inc(s_lm, 1)
            act.wait_ge(s_q, 1)
            act.activation(tr[:, :], ang[:, :], ACT.Sin).then_inc(s_sin, 1)

        @block.vector
        def _(dve):
            dve.wait_ge(s_in, 16 * NIN)
            dve.wait_ge(s_ex, 1)
            dve.tensor_scalar(bn[:, :], bn[:, :], ex[:, 2:3], None, ALU.mult).then_inc(s_bn, 1)
            dve.tensor_scalar(cc[:, 0, 1, :], cc[:, 0, 1, :], -1.0, None, ALU.mult)
            dve.tensor_scalar(cc[:, 1, :, :], cc[:, 1, :, :], -1.0, None, ALU.mult).then_inc(s_cc, 1)
            dve.tensor_copy(cwt[:, 0:KA, :], cw[:, :, :].rearrange("i j k -> i k j"))
            dve.memset(cwt[:, KA, :], 0.0).then_inc(s_cwt, 1)
            dve.tensor_scalar(ang[:, 0:1], ex[:, 1:2], PI / 2, None, ALU.add)
            dve.tensor_copy(ang[:, 1:2], ex[:, 1:2])
            dve.drain()
            dve.tensor_scalar(q[:, :], ang[:, :], 1.0 / (2 * PI), ROUND, ALU.mult, ALU.add)
            dve.drain()
            dve.tensor_scalar(q[:, :], q[:, :], ROUND, None, ALU.subtract)
            dve.drain()
            for part in (TWO_PI_HI, TWO_PI_LO):
                dve.scalar_tensor_tensor(ang[:, :], q[:, :], -part, ang[:, :], ALU.mult, ALU.add)
                dve.drain()
            dve.tensor_scalar(ang[:, :], ang[:, :], PI, -PI, ALU.min, ALU.max).then_inc(s_q, 1)
            dve.wait_ge(s_lm, 1)
            dve.memset(w["decay"][:, :], 1.0)
            dve.drain()
            dve.tensor_scalar(w["decay"][:, :], w["decay"][:, :], lm[:, :], None, ALU.mult)
            dve.drain()
            dve.memset(w["decay"][:, :].rearrange("p (b t) -> p b t", t=SEQ)[:, :, 0:1], 0.0)
            dve.wait_ge(s_sin, 1)
            cs, sn = w["cos"], w["sin"]
            dve.memset(cs[:, 0:1], 1.0)
            dve.memset(sn[:, 0:1], 0.0)
            dve.tensor_copy(em[:, :], tr[:, :])
            dve.drain()
            m = 1
            while m < SEQ:
                dve.tensor_scalar(mix[:, 0, 0:m], sn[:, 0:m], em[:, 1:2], None, ALU.mult)
                dve.tensor_scalar(mix[:, 1, 0:m], cs[:, 0:m], em[:, 1:2], None, ALU.mult)
                dve.tensor_tensor(en[:, :], em[:, :], em[:, :], ALU.mult)
                dve.drain()
                dve.scalar_tensor_tensor(cs[:, m:2 * m], cs[:, 0:m], em[:, 0:1], mix[:, 0, 0:m], ALU.mult, ALU.subtract)
                dve.scalar_tensor_tensor(sn[:, m:2 * m], sn[:, 0:m], em[:, 0:1], mix[:, 1, 0:m], ALU.mult, ALU.add)
                dve.tensor_tensor(en[:, 0:1], en[:, 0:1], en[:, 1:2], ALU.subtract)
                dve.drain()
                dve.scalar_tensor_tensor(em[:, 1:2], em[:, 1:2], 2.0, em[:, 0:1], ALU.mult, ALU.mult)
                dve.drain()
                dve.tensor_copy(em[:, 0:1], en[:, 0:1])
                dve.drain()
                m *= 2
            dve.tensor_copy(w["sinr"][0:S_, :], sn[0:S_, :])
            dve.tensor_scalar(w["sinr"][S_:P, :], sn[S_:P, :], -1.0, None, ALU.mult)
            dve.wait_ge(s_t, 1)
            dve.tensor_copy(bnT[:, :], ps[0:S_, 0, 0:P]).then_inc(s_bnT, 1)
            dve.tensor_copy(w["cp"][:, :], ps[:, 1, 0:S_])
            dve.tensor_copy(w["cq"][:, :], ps[:, 1, S_:P])
            dve.tensor_copy(w["wout"][0:S_, :], ps[0:S_, 2, 0:C])
            dve.tensor_copy(wit[:, :], ps[:, 3, 0:C]).then_inc(s_wit, 1)
            dve.drain()
            dve.tensor_scalar(w["win"][:, :], wit[:, :], lnw[:, 0:1], None, ALU.mult)
            dve.wait_ge(s_m, 1)
            for n in range(3):
                dve.tensor_copy(w["bc"][:, n, :], ps[:, 4, n * P:(n + 1) * P])
            dve.tensor_copy(w["bA"][:, :], ps[:, 5, 0:1])
            dve.tensor_copy(w["bsw"][0:S_, :], ps[S_:P, 5, 0:1])
            dve.tensor_copy(w["bsw"][S_:P, :], ps[0:S_, 5, 0:1])
            dve.tensor_copy(w["bin"][:, :], ps[:, 6, 0:1])

        @block.tensor
        def _(pe):
            pe.wait_ge(s_in, 16 * NIN)
            pe.wait_ge(s_bn, 1)
            pe.wait_ge(s_cc, 1)
            pe.transpose(ps[0:S_, 0, 0:P], bn[:, :], k["ident"][:, :])
            for n in range(2):
                pe.transpose(ps[:, 1, n * S_:(n + 1) * S_], cc[:, n, :, :].rearrange("o a s -> o (a s)"),
                             k["ident"][0:S_, 0:S_])
            pe.transpose(ps[0:S_, 2, 0:C], wo[:, :], k["ident"][:, :])
            pe.transpose(ps[:, 3, 0:C], wi[:, :], k["ident"][:, :]).then_inc(s_t, 1)
            pe.wait_ge(s_bnT, 1)
            pe.wait_ge(s_cwt, 1)
            for n in range(3):
                pe.matmul(ps[:, 4, n * P:(n + 1) * P], cwt[:, 2 * n:2 * n + 2, :].rearrange("i a j -> i (a j)"),
                          bnT[:, :], start=True, stop=True)
            pe.matmul(ps[:, 5, 0:1], bnT[:, :], cb[:, :], start=True, stop=True)
            pe.wait_ge(s_wit, 1)
            pe.matmul(ps[:, 6, 0:1], wit[:, :], lnw[:, 1:2], start=True, stop=True).then_inc(s_m, 1)


def lru_block(nc, k, w, hT, x2T, lg, xrows, ybuf):
    NP = NU // 2
    W = SEQ + 4
    EPS = 1e-5
    with Stage(nc, "lru") as s:
        hx = s.sb("hx", [P, 2, UNIT])
        htk = s.sb("htk", [P, 2, UT, C])
        x1 = s.sb("x1", [P, 2, UT, C])
        z = s.sb("z", [P, 2, UT, C])
        zT = hx
        V2 = s.sb("V2", [P, 2, UB, W])
        gx = s.sb("gx", [S_, 2, UNIT])
        ta = s.sb("ta", [P, 2, UNIT])
        tb = s.sb("tb", [P, 2, UNIT])
        uu = s.sb("uu", [P, 2, UNIT])
        o = s.sb("o", [S_ + 1, 2, UNIT])
        ho = s.sb("ho", [P, 2, UT, C])
        bs = s.sb("bs", [P, 2, UT, 6])
        ba1, ba2 = s.sb("ba1", [P, 2, UT, 2]), s.sb("ba2", [P, 2, UT, 2])
        r1, rz, nb = s.sb("r1", [P, 2, UT]), s.sb("rz", [P, 2, UT]), s.sb("nb", [P, 2, UT])
        rb = s.sb("rb", [P, 2, UT])
        eps = s.sb("eps", [P, 2])
        x2 = tb
        x2c = s.sb("x2c", [P, 2, UNIT])
        ps = s.pb("ps", [P, 2, 4, 512])
        names = ("hx", "T1", "htk", "bn1", "sd1", "rs", "z", "x1", "Tz", "zT", "win", "V2", "gx", "A", "t", "u", "scan",
                 "q", "p", "y", "o", "wo", "h1", "bn", "sd", "x2", "T2", "x2T", "x2c", "lg", "lgc", "sx", "sy")
        S = {n: s.sem2(n) for n in names}
        s_pad, s_tick = s.sem("pad"), s.sem("tick")
        block = s.block()
        seqs = lambda ap: ap.rearrange("p (b t) -> p b t", t=SEQ)
        flat = lambda ap: ap.rearrange("p a b -> p (a b)")

        def bank(u, n, rows=slice(0, P)):
            return ps[rows, u, n:n + 2, :].rearrange("p a b -> p (a b)")

        @block.sync
        def _(sp):
            def step(j, more):
                for u in range(2):
                    rows = lambda t: t[bass.ds(j * 2 * UNIT + u * UNIT, UNIT), :].rearrange("(t p) c -> p t c", p=P)
                    sp.wait_ge(S["h1"][u], j + 1)
                    sp.dma_start(rows(ybuf), ho[:, u, :, :]).then_inc(S["sy"][u], 16)
                    sp.wait_ge(S["x2"][u], j + 1)
                    sp.dma_start(rows(xrows[:, 0:C]), x2[:, u, :].rearrange("p (t c) -> p t c", c=C))\
                        .then_inc(S["sx"][u], 16)

            pairs(sp, step)
            for u in range(2):
                sp.wait_ge(S["sy"][u], 16 * NP)
                sp.wait_ge(S["sx"][u], 16 * NP)

        @block.scalar
        def _(act):
            def copy_input(j):
                for u in range(2):
                    if after_first(j):
                        wait_alone(act, S["win"][u], j, s_tick)
                    act.activation(hx[:, u, :], hT[:, bass.ds(j * 2 * UNIT + u * UNIT, UNIT)], ACT.Copy)\
                        .then_inc(S["hx"][u], 1)

            def by_tokens(j):
                for u in range(2):
                    act.wait_ge(S["T1"][u], j + 1)
                    if after_first(j):
                        act.wait_ge(S["x1"][u], j)
                    act.activation(flat(htk[:, u, :, :]), bank(u, 0), ACT.Copy).then_inc(S["htk"][u], 1)

            def deviations(j):
                for u in range(2):
                    act.wait_ge(S["bn1"][u], j + 1)
                    act.activation(r1[:, u, :], ba1[:, u, :, 1], ACT.Sqrt, bias=eps[:, 0:1])
                    act.activation(rz[:, u, :], ba1[:, u, :, 1], ACT.Sqrt, bias=eps[:, 1:2], scale=1.0 + EPS)\
                        .then_inc(S["sd1"][u], 1)

            def with_norm(j, u):
                act.wait_ge(S["rs"][u], j + 1)
                if after_first(j):
                    act.wait_ge(S["h1"][u], j)
                for t in range(UT):
                    last = act.activation(x1[:, u, t, :], htk[:, u, t, :], ACT.Identity, scale=r1[:, u, t:t + 1],
                                          bias=nb[:, u, t:t + 1])
                last.then_inc(S["x1"][u], 1)

            def norm_by_channels(j):
                for u in range(2):
                    act.wait_ge(S["Tz"][u], j + 1)
                    act.activation(zT[:, u, :], bank(u, 0), ACT.Copy).then_inc(S["zT"][u], 1)

            act.wait_ge(s_pad, 3)
            copy_input(0)
            by_tokens(0)
            deviations(0)
            norm_by_channels(0)
            for u in range(2):
                with_norm(0, u)

            def step(j, more):
                for u in range(2):
                    act.wait_ge(S["win"][u], j + 1)
                    act.activation(V2[0:S_, u, :, 2:2 + SEQ], seqs(bank(u, 2, slice(0, S_))), ACT.Identity,
                                   bias=w["bin"][0:S_, 0:1])
                    act.activation(V2[S_:P, u, :, 1:1 + SEQ], seqs(bank(u, 2, slice(0, S_))), ACT.Identity,
                                   bias=w["bin"][0:S_, 0:1]).then_inc(S["V2"][u], 1)
                    act.activation(gx[:, u, :], bank(u, 2, slice(S_, P)), ACT.Gelu,
                                   bias=w["bin"][S_:P, 0:1]).then_inc(S["gx"][u], 1)
                if more:
                    copy_input(j + 1)
                    by_tokens(j + 1)
                    deviations(j + 1)
                    norm_by_channels(j + 1)
                for u in range(2):
                    act.wait_ge(S["bn"][u], j + 1)
                    act.activation(rb[:, u, :], ba2[:, u, :, 1], ACT.Sqrt, bias=eps[:, 0:1]).then_inc(S["sd"][u], 1)
                for u in range(2):
                    if more:
                        with_norm(j + 1, u)
                    act.wait_ge(S["T2"][u], j + 1)
                    act.activation(x2c[:, u, :], bank(u, 2), ACT.Copy).then_inc(S["x2c"][u], 1)
                for u in range(2):
                    act.activation(x2T[:, bass.ds(j * 2 * UNIT + u * UNIT, UNIT)], bank(u, 2), ACT.Copy)\
                        .then_inc(S["x2T"][u], 1)

            pairs(act, step)

        @block.gpsimd
        def _(pool):
            pool.memset(eps[:, 0:1], EPS)
            pool.memset(eps[:, 1:2], EPS * EPS).then_inc(s_pad, 1)
            pool.memset(V2[:, :, :, :], 0.0).then_inc(s_pad, 1)
            pool.drain()
            pool.memset(o[S_:S_ + 1, :, :], 1.0).then_inc(s_pad, 1)
            pool.drain()

            def step(j, more):
                for u in range(2):
                    pool.wait_ge(S["t"][u], j + 1)
                    pool.tensor_tensor(uu[:, u, :], ta[:, u, :], tb[:, u, :], ALU.add).then_inc(S["u"][u], 1)
                for u in range(2):
                    pool.wait_ge(S["scan"][u], j + 1)
                    pool.tensor_tensor(seqs(tb[:, u, :]), seqs(uu[:, u, :]), bc(w["sin"][:, :], 1, UB),
                                       ALU.mult).then_inc(S["q"][u], 1)

            pairs(pool, step)

        @block.vector
        def _(dve):
            def stats(src, u, ba, done):
                for t in range(UT):
                    dve.bn_stats(bs[:, u, t, :], src[:, u, t, :])
                dve.drain()
                for t in range(UT):
                    last = dve.bn_aggr(ba[:, u, t, :], bs[:, u, t, :])
                last.then_inc(done[u], 1)

            def input_stats(j, u):
                dve.wait_ge(S["htk"][u], j + 1)
                stats(htk, u, ba1, S["bn1"])

            def norm(j, u):
                dve.wait_ge(S["sd1"][u], j + 1)
                dve.reciprocal(r1[:, u, :], r1[:, u, :])
                dve.reciprocal(rz[:, u, :], rz[:, u, :])
                dve.drain()
                dve.scalar_tensor_tensor(nb[:, u, :], ba1[:, u, :, 0], -1.0, r1[:, u, :], ALU.mult, ALU.mult)
                dve.drain()
                dve.tensor_scalar(r1[:, u, :], r1[:, u, :], 1.0, None, ALU.add).then_inc(S["rs"][u], 1)
                for t in range(UT):
                    last = dve.tensor_scalar(z[:, u, t, :], htk[:, u, t, :], ba1[:, u, t, 0:1],
                                             rz[:, u, t:t + 1], ALU.subtract, ALU.mult)
                last.then_inc(S["z"][u], 1)

            for u in range(2):
                input_stats(0, u)
            for u in range(2):
                norm(0, u)

            def step(j, more):
                for u in range(2):
                    dve.wait_ge(S["A"][u], j + 1)
                    if after_first(j):
                        dve.wait_ge(S["sx"][u], j * 16)
                    dve.scalar_tensor_tensor(seqs(ta[:, u, :]), seqs(bank(u, 0)), w["bA"][:, 0:1],
                                             bc(w["cos"][:, :], 1, UB), ALU.add, ALU.mult)
                    dve.scalar_tensor_tensor(seqs(tb[0:S_, u, :]), seqs(bank(u, 0, slice(S_, P))), w["bsw"][0:S_, 0:1],
                                             bc(w["sinr"][0:S_, :], 1, UB), ALU.add, ALU.mult)
                    dve.scalar_tensor_tensor(seqs(tb[S_:P, u, :]), seqs(bank(u, 0, slice(0, S_))), w["bsw"][S_:P, 0:1],
                                             bc(w["sinr"][S_:P, :], 1, UB), ALU.add, ALU.mult).then_inc(S["t"][u], 1)
                for u in range(2):
                    if more:
                        input_stats(j + 1, u)
                    dve.wait_ge(S["u"][u], j + 1)
                    dve.tensor_tensor_scan(uu[:, u, :], w["decay"][:, :], uu[:, u, :], 0.0,
                                           ALU.mult, ALU.add).then_inc(S["scan"][u], 1)
                    dve.drain()
                    dve.tensor_tensor(seqs(ta[:, u, :]), seqs(uu[:, u, :]), bc(w["cos"][:, :], 1, UB),
                                      ALU.mult).then_inc(S["p"][u], 1)
                if more:
                    for u in range(2):
                        norm(j + 1, u)
                for u in range(2):
                    dve.wait_ge(S["y"][u], j + 1)
                    dve.wait_ge(S["gx"][u], j + 1)
                    dve.tensor_tensor(o[0:S_, u, :], bank(u, 2, slice(0, S_)), gx[:, u, :], ALU.mult)\
                        .then_inc(S["o"][u], 1)
                for u in range(2):
                    dve.wait_ge(S["wo"][u], j + 1)
                    dve.wait_ge(S["x1"][u], j + 1)
                    if after_first(j):
                        dve.wait_ge(S["sy"][u], j * 16)
                    dve.tensor_tensor(flat(ho[:, u, :, :]), bank(u, 0), flat(x1[:, u, :, :]), ALU.add)\
                        .then_inc(S["h1"][u], 1)
                    dve.drain()
                    stats(ho, u, ba2, S["bn"])
                for u in range(2):
                    dve.wait_ge(S["sd"][u], j + 1)
                    dve.reciprocal(rb[:, u, :], rb[:, u, :])
                    dve.drain()
                    for t in range(UT):
                        last = dve.tensor_scalar(x2[:, u, t * C:(t + 1) * C], ho[:, u, t, :], ba2[:, u, t, 0:1],
                                                 rb[:, u, t:t + 1], ALU.subtract, ALU.mult)
                    last.then_inc(S["x2"][u], 1)
                for u in range(2):
                    dve.wait_ge(S["lg"][u], j + 1)
                    dve.tensor_copy(lg[:, bass.ds(j * 2 * UT + u * UT, UT), :],
                                    ps[:, u, 0, 0:UT * E0].rearrange("p (t e) -> p t e", e=E0)).then_inc(S["lgc"][u], 1)

            pairs(dve, step)

        @block.tensor
        def _(pe):
            pe.wait_ge(s_pad, 3)
            tiles = lambda ap, t: ap[:, t * P:(t + 1) * P]
            halves = lambda c: slice(c * 512, (c + 1) * 512)

            def transposes(u, n, src, done):
                for t in range(UT):
                    last = pe.transpose(ps[:, u, n + t // 4, (t % 4) * P:(t % 4 + 1) * P], src(t), k["ident"][:, :])
                last.then_inc(done, 1)

            def by_tokens(j):
                for u in range(2):
                    pe.wait_ge(S["hx"][u], j + 1)
                    if after_first(j):
                        pe.wait_ge(S["t"][u], j)
                    transposes(u, 0, lambda t: tiles(hx[:, u, :], t), S["T1"][u])

            def norm_by_channels(j):
                for u in range(2):
                    pe.wait_ge(S["z"][u], j + 1)
                    transposes(u, 0, lambda t: z[:, u, t, :], S["Tz"][u])

            by_tokens(0)
            norm_by_channels(0)

            def step(j, more):
                for u in range(2):
                    pe.wait_ge(S["zT"][u], j + 1)
                    if after_first(j):
                        pe.wait_ge(S["x2T"][u], j)
                    for c in range(2):
                        last = pe.matmul(ps[:, u, 2 + c, :], w["win"][:, :], zT[:, u, halves(c)], start=True, stop=True)
                    last.then_inc(S["win"][u], 1)
                for u in range(2):
                    pe.wait_ge(S["V2"][u], j + 1)
                    if after_first(j):
                        pe.wait_ge(S["lgc"][u], j)
                    for c in range(2):
                        for n in range(3):
                            rows = slice(0, P if n < 2 else S_)
                            last = pe.matmul(ps[:, u, c, :].rearrange("p (b t) -> p b t", t=SEQ), w["bc"][rows, n, :],
                                             V2[rows, u, 2 * c:2 * c + 2, 2 * n:2 * n + SEQ],
                                             start=(n == 0), stop=(n == 2))
                    last.then_inc(S["A"][u], 1)
                if more:
                    by_tokens(j + 1)
                for u in range(2):
                    pe.wait_ge(S["gx"][u], j + 1)
                    pe.wait_ge(S["p"][u], j + 1)
                    pe.wait_ge(S["q"][u], j + 1)
                    for c in range(2):
                        pe.matmul(ps[0:S_, u, 2 + c, :], w["cp"][:, :], ta[:, u, halves(c)], start=True, stop=False)
                        last = pe.matmul(ps[0:S_, u, 2 + c, :], w["cq"][:, :], tb[:, u, halves(c)],
                                         start=False, stop=True)
                    last.then_inc(S["y"][u], 1)
                if more:
                    norm_by_channels(j + 1)
                for u in range(2):
                    pe.wait_ge(S["o"][u], j + 1)
                    if more:
                        pe.wait_ge(S["zT"][u], j + 2)
                    for t in range(UT):
                        last = pe.matmul(ps[:, u, t // 4, (t % 4) * P:(t % 4 + 1) * P], tiles(o[:, u, :], t),
                                         w["wout"][:, :], start=True, stop=True)
                    last.then_inc(S["wo"][u], 1)
                for u in range(2):
                    pe.wait_ge(S["x2"][u], j + 1)
                    transposes(u, 2, lambda t: tiles(x2[:, u, :], t), S["T2"][u])
                for u in range(2):
                    pe.wait_ge(S["x2c"][u], j + 1)
                    for t in range(UT):
                        last = pe.matmul(ps[:, u, 0, t * E0:(t + 1) * E0], tiles(x2c[:, u, :], t), w["gate"][:, :],
                                         start=True, stop=True)
                    last.then_inc(S["lg"][u], 1)

            pairs(pe, step)


CAP0 = T // E0
H = 512
HT = H // P
CH = 512
CT = CH // P
SEG = P // E0
ST = NT // SEG


def softmax_experts(nc, k, lg, pT, xrows):
    with Stage(nc, "smx") as s:
        mx = s.sb("mx", [P, NT])
        pr = s.sb("pr", [P, ST, SEG, E0])
        ps = s.pb("ps", [P, 2, 512])
        s_sub, s_exp, s_pr, s_pc, s_t, s_x = (s.sem(n) for n in ("sub", "exp", "pr", "pc", "t", "x"))
        block = s.block()

        @block.vector
        def _(dve):
            dve.tensor_reduce(mx[:, :], lg[:, :, :], AX, ALU.max)
            dve.drain()
            dve.tensor_tensor(lg[:, :, :], lg[:, :, :], bc(mx[:, :], 2, E0), ALU.subtract).then_inc(s_sub, 1)
            dve.wait_ge(s_exp, 1)
            dve.tensor_reduce(mx[:, :], lg[:, :, :], AX, ALU.add)
            dve.drain()
            dve.reciprocal(mx[:, :], mx[:, :])
            dve.drain()
            dve.tensor_tensor(lg[:, :, :], lg[:, :, :], bc(mx[:, :], 2, E0), ALU.mult).then_inc(s_pr, 1)
            dve.drain()
            dve.tensor_copy(pr[:, :, :, :], lg[:, :, :].rearrange("p (s t) e -> p t s e", s=SEG)).then_inc(s_pc, 1)
            dve.wait_ge(s_t, 1)
            dve.tensor_copy(pT[:, :], ps[:, :, :].rearrange("p a b -> p (a b)"))

        @block.scalar
        def _(act):
            act.wait_ge(s_sub, 1)
            act.activation(lg[:, :, :], lg[:, :, :], ACT.Exp).then_inc(s_exp, 1)

        @block.tensor
        def _(pe):
            pe.wait_ge(s_pc, 1)
            for t in range(ST):
                last = pe.transpose(ps[:, t // 4, (t % 4) * P:(t % 4 + 1) * P],
                                    pr[:, t, :, :].rearrange("p s e -> p (s e)"), k["ident"][:, :])
            last.then_inc(s_t, 1)

        @block.sync
        def _(sp):
            sp.wait_ge(s_pr, 1)
            sp.dma_start(xrows[:, C:ROW].rearrange("(t p) e -> p t e", p=P), lg[:, :, :],
                         allow_slow_non_contiguous=True).then_inc(s_x, 16)
            sp.wait_ge(s_x, 16)


def select_tokens(nc, k, pT, idx):
    BITS = 30
    with Stage(nc, "sel") as s:
        same = s.sb("same", [P, P])
        lower = s.sb("lower", [P, P])
        thr = s.sb("thr", [P, 1], I32)
        cand = s.sb("cand", [P, 1], I32)
        bit = s.sb("bit", [P, 1], I32)
        keep = s.sb("keep", [P, 1], I32)
        cnt = s.sb("cnt", [P, 4])
        junk = s.sb("junk", [P, T // SEG], BF16)
        gt = s.sb("gt", [P, T // SEG])
        eq = s.sb("eq", [P, T // SEG])
        rk = s.sb("rk", [P, T // SEG])
        one = s.sb("one", [P, T // SEG])
        lim = s.sb("lim", [P, 2])
        sl = s.sb("sl", [P, SEG, ST, E0], I32)
        si = s.sb("si", [P, SEG, ST, E0], I32)
        lo = s.sb("lo", [P, NT, E0], BF16)
        hi = s.sb("hi", [P, NT, E0], BF16)
        io = s.sb("io", [P, 32, E0], I32)
        iob = s.sb("iob", [P, 32, E0], BF16)
        ioe = s.sb("ioe", [P, E0, 32], BF16)
        tok = s.sb("tok", [P, 1 + NT])
        toki = s.sb("toki", [P, 1 + NT], I32)
        oa = s.sb("oa", [P, 2, E0, 32], BF16)
        ob = s.sb("ob", [P, 2, 16, E0], BF16)
        ov = s.sb("ov", [P, 2, 2, 16, E0], BF16)
        zz = s.sb("zz", [P, P], BF16)
        ls = s.sb("ls", [P, 4, 2, 16, 4])
        psh = s.pb("psh", [P, 4, 512])
        psc = s.pb("psc", [P, 512])
        s_set, s_tick = s.sem("set"), s.sem("tick")
        s_cnt, s_sum = s.sem("cnt"), s.sem("sum")
        s_ge, s_tot, s_cs, s_off, s_v, s_vt = (s.sem(n) for n in ("ge", "tot", "cs", "off", "v", "vt"))
        s_oh, s_ob, s_ov, s_li = s.sem2("oh"), s.sem2("ob"), s.sem2("ov"), s.sem2("li")
        s_end = s.sem("end")
        block = s.block()

        @block.gpsimd
        def _(pool):
            pool.memset(lower[:, :], 0.0)
            pool.memset(one[:, :], 1.0)
            pool.memset(zz[:, :], 0.0)
            pool.iota(toki[:, 0:1], pattern=[[0, 1]], base=0, channel_multiplier=1)
            pool.iota(toki[:, 1:1 + NT], pattern=[[1, NT]], base=0, channel_multiplier=0)
            pool.iota(io[:, :, :], pattern=[[1, 32], [0, E0]], base=0, channel_multiplier=0)
            pool.drain()
            pool.tensor_copy(tok[:, :], toki[:, :])
            pool.tensor_copy(iob[:, :, :], io[:, :, :])
            pool.tensor_copy(ioe[:, :, :], io[:, :, :].rearrange("p b e -> p e b"))
            for n in range(1, SEG):
                pool.affine_select(out=lower[:, :], in_=lower[:, :], compare_op=ALU.not_equal, fill=1.0,
                                   base=E0 * n, pattern=[[-1, P]], channel_multiplier=1)
                pool.drain()
            pool.tensor_tensor(same[:, :], lower[:, :], k["ident"][:, :], ALU.add)
            pool.drain()
            for n in range(1, SEG):
                last = pool.affine_select(out=same[:, :], in_=same[:, :], compare_op=ALU.not_equal, fill=1.0,
                                          base=-E0 * n, pattern=[[-1, P]], channel_multiplier=1)
                if n == SEG - 1:
                    last.then_inc(s_set, 1)
                else:
                    pool.drain()

        @block.scalar
        def _(act):
            with act.Fori(0, NT // 2) as j:
                for u in range(2):
                    wait_alone(act, s_ob[u], j + 1, s_tick)
                    act.activation(ov[:, u, 0, :, :], ob[:, u, :, :], ACT.Copy, scale=tok[:, 0:1])
                    act.activation(ov[:, u, 1, :, :], ob[:, u, :, :], ACT.Copy, scale=tok[:, bass.ds(2 * j + u + 1, 1)])\
                        .then_inc(s_ov[u], 1)

        @block.vector
        def _(dve):
            dve.memset(thr[:, :], 0)
            dve.memset(bit[:, :], 1 << 29)
            dve.wait_ge(s_set, 1)
            dve.drain()
            with dve.Fori(0, BITS) as n:
                dve.tensor_tensor(cand[:, :], thr[:, :], bit[:, :], ALU.bitwise_or)
                dve.drain()
                dve.tensor_scalar(junk[:, :], pT[:, :], cand[:, :].bitcast(F32), None, ALU.is_ge, ALU.add,
                                  accum_out=cnt[:, 0:1]).then_inc(s_cnt, 1)
                dve.tensor_scalar(bit[:, :], bit[:, :], 1, None, ALU.logical_shift_right)
                dve.wait_ge(s_sum, n + 1)
                dve.tensor_scalar(keep[:, :], psc[:, 0:1], CAP0 - 0.5, None, ALU.is_ge)
                dve.drain()
                dve.copy_predicated(thr[:, :], keep[:, :], cand[:, :])
                dve.drain()
            thf = thr[:, :].bitcast(F32)
            dve.tensor_scalar(gt[:, :], pT[:, :], thf, None, ALU.is_gt, ALU.add, accum_out=cnt[:, 0:1])
            dve.tensor_scalar(eq[:, :], pT[:, :], thf, None, ALU.is_equal, ALU.add, accum_out=cnt[:, 1:2])\
                .then_inc(s_ge, 1)
            dve.drain()
            dve.tensor_tensor_scan(rk[:, :], one[:, :], eq[:, :], 0.0, ALU.mult, ALU.add)
            dve.wait_ge(s_tot, 1)
            dve.tensor_scalar(lim[:, 0:1], psc[:, 1:2], -1.0, float(CAP0), ALU.mult, ALU.add)
            dve.drain()
            dve.tensor_tensor(lim[:, 0:1], lim[:, 0:1], psc[:, 2:3], ALU.subtract)
            dve.drain()
            dve.scalar_tensor_tensor(eq[:, :], rk[:, :], lim[:, 0:1], eq[:, :], ALU.is_le, ALU.mult)
            dve.drain()
            dve.tensor_tensor(gt[:, :], gt[:, :], eq[:, :], ALU.add)
            dve.drain()
            dve.tensor_tensor_scan(rk[:, :], one[:, :], gt[:, :], 0.0, ALU.mult, ALU.add).then_inc(s_cs, 1)
            dve.wait_ge(s_off, 1)
            dve.tensor_copy(lim[:, 1:2], psc[:, 3:4])
            dve.drain()
            dve.scalar_tensor_tensor(rk[:, :], rk[:, :], lim[:, 1:2], gt[:, :], ALU.add, ALU.mult).then_inc(s_v, 1)
            dve.wait_ge(s_vt, 1)
            for q in range(2):
                dve.tensor_scalar(si[:, :, q * 4:(q + 1) * 4, :],
                                  psh[:, q, :].rearrange("p (t s e) -> p s t e", s=SEG, e=E0), -1.0, None, ALU.add)
            dve.drain()
            dve.tensor_scalar(sl[:, :, :, :], si[:, :, :, :], 31, None, ALU.bitwise_and)
            dve.tensor_scalar(si[:, :, :, :], si[:, :, :, :], 5, None, ALU.arith_shift_right)
            dve.drain()
            dve.tensor_copy(lo[:, :, :], sl[:, :, :, :].rearrange("p s t e -> p (s t) e"))
            dve.tensor_copy(hi[:, :, :], si[:, :, :, :].rearrange("p s t e -> p (s t) e"))
            dve.drain()

            def one_hots(j):
                for u in range(2):
                    t = 2 * j + u
                    if after_first(j):
                        dve.wait_ge(s_li[u], j)
                    dve.tensor_tensor(ob[:, u, :, :], bc(hi[:, bass.ds(t, 1), :], 1, 16)[:, :, 0, :], iob[:, 0:16, :],
                                      ALU.is_equal).then_inc(s_ob[u], 1)
                    dve.tensor_tensor(oa[:, u, :, :], bc(lo[:, bass.ds(t, 1), :], 3, 32)[:, 0, :, :], ioe[:, :, :],
                                      ALU.is_equal).then_inc(s_oh[u], 1)

            one_hots(0)
            with dve.Fori(1, NT // 2) as j:
                one_hots(j)
            dve.wait_ge(s_end, 1)
            dve.tensor_copy(ls[:, :, :, :, :].rearrange("p g v a e -> p g (v a e)"), psh[:, :, 0:P])
            dve.drain()
            for e in range(4):
                for a in range(4):
                    src = ls[32 * e:32 * e + 32, :, :, a:16:4, e]
                    dst = idx[32 * a:32 * a + 32, :, :].rearrange("p (q e) g -> p q e g", e=4)[:, :, e, :]
                    dve.scalar_tensor_tensor(dst, src[:, :, 1, :], float(P), src[:, :, 0, :], ALU.mult, ALU.add)

        @block.tensor
        def _(pe):
            pe.wait_ge(s_set, 1)
            with pe.Fori(0, BITS) as n:
                pe.wait_ge(s_cnt, n + 1)
                pe.matmul(psc[:, 0:1], same[:, :], cnt[:, 0:1], start=True, stop=True).then_inc(s_sum, 1)
            pe.wait_ge(s_ge, 1)
            pe.matmul(psc[:, 1:2], same[:, :], cnt[:, 0:1], start=True, stop=True)
            pe.matmul(psc[:, 2:3], lower[:, :], cnt[:, 1:2], start=True, stop=True).then_inc(s_tot, 1)
            pe.wait_ge(s_cs, 1)
            pe.matmul(psc[:, 3:4], lower[:, :], rk[:, T // SEG - 1:T // SEG], start=True, stop=True).then_inc(s_off, 1)
            pe.wait_ge(s_v, 1)
            for t in range(ST):
                last = pe.transpose(psh[:, t // 4, (t % 4) * P:(t % 4 + 1) * P], rk[:, t * P:(t + 1) * P],
                                    k["ident"][:, :])
            last.then_inc(s_vt, 1)
            pe.wait_ge(s_oh[0], 1)
            for g in range(4):
                pe.matmul(psh[:, g, 0:P], zz[:, :], zz[:, :], start=True, stop=False)
            with pe.Fori(0, NT // 2) as j:
                for u in range(2):
                    pe.wait_ge(s_oh[u], j + 1)
                    pe.wait_ge(s_ov[u], j + 1)
                    for g in range(4):
                        last = pe.matmul(psh[:, g, 0:P],
                                         oa[:, u, 4 * g:4 * g + 4, :].rearrange("p e b -> p (e b)"),
                                         ov[:, u, :, :, 4 * g:4 * g + 4].rearrange("p v a e -> p (v a) e"),
                                         start=False, stop=False)
                    last.then_inc(s_li[u], 1)
            for g in range(4):
                last = pe.matmul(psh[:, g, 0:P], zz[:, :], zz[:, :], start=False, stop=True)
            last.then_inc(s_end, 1)


def experts_choice(nc, k, d, idx, xrows, x2T, ybuf, shared):
    NE2 = E0 // 2
    NW, NS = 4, 4
    with Stage(nc, "moe") as s:
        w1 = s.sb("w1", [P, 2, H])
        w2 = s.sb("w2", [P, 2, HT, C])
        b1 = s.sb("b1", [P, 2, HT])
        b2 = s.sb("b2", [P, 2, C])
        w1s = s.sb("w1s", [P, H])
        w2s = s.sb("w2s", [P, HT, C])
        b1s = s.sb("b1s", [P, HT])
        b2s = s.sb("b2s", [P, C])
        idg = s.sb("idg", [P, 2, CT], I32)
        ids = s.sb("ids", [P, 2, CT], I32)
        xg = s.sb("xg", [P, 2, CT, ROW])
        gw = s.sb("gw", [P, 2, CT])
        xT = s.sb("xT", [P, 2, CH])
        hs = s.sb("hs", [P, 2, HT, CH])
        yo = s.sb("yo", [P, 2, CT, C])
        psx = s.pb("psx", [P, 512])
        psh = s.pb("psh", [P, 4, 512])
        pso = s.pb("pso", [P, 2, 512])
        S = {n: s.sem2(n) for n in ("w", "x", "add")}
        s_ws, s_T, s_xT, s_out, s_y, s_outs, s_ev, s_tick = (
            s.sem(n) for n in ("ws", "T", "xT", "out", "y", "outs", "ev", "tick"))
        s_hid = [s.sem(f"hid{n}") for n in range(HT)]
        s_gel = [s.sem(f"gel{n}") for n in range(HT)]
        block = s.block()

        @block.sync
        def _(sp):
            def load(e, u):
                for dst, src in (
                    (w1[:, u, :], d["w1"][e, :, :].rearrange("a c h -> (a c) h")),
                    (w2[:, u, :, :], d["w2"][e, :, :].rearrange("a (k p) c -> p (a k) c", p=P)),
                    (b1[:, u, :], d["b1"][e, :].rearrange("a (k p) -> p (a k)", p=P)),
                    (b2[:, u, :], bc(d["b2"][e, :], 0, P).rearrange("q a c -> q (a c)")),
                ):
                    sp.dma_start(dst, src, allow_slow_non_contiguous=True).then_inc(S["w"][u], 16)

            load(slice(0, 1), 0)
            for dst, src in ((w1s[:, :], d["sw1"]), (w2s[:, :, :], d["sw2"].rearrange("(k p) c -> p k c", p=P)),
                             (b1s[:, :], d["sb1"].rearrange("(k p) -> p k", p=P)), (b2s[:, :], bc(d["sb2"], 0, P))):
                sp.dma_start(dst, src, allow_slow_non_contiguous=True).then_inc(s_ws, 16)
            load(slice(1, 2), 1)
            with sp.Fori(0, NE2 - 1) as j:
                for u in range(2):
                    sp.wait_ge(s_y, 2 * j + u + 1)
                    load(bass.ds(2 * j + 2 + u, 1), u)

        @block.gpsimd
        def _(pool):
            def gather(i, u):
                pool.tensor_copy(idg[:, u, :], idx[:, bass.ds(i, 1), :].rearrange("p a g -> p (a g)"))
                pool.drain()
                for t in range(CT):
                    pool.indirect_dma_start(xg[:, u, t, :], None, xrows,
                                            bass.IndirectOffsetOnAxis(ap=idg[:, u, t:t + 1], axis=0))\
                        .then_inc(S["x"][u], 16)

            for u in range(2):
                gather(u, u)

            def step(j, more):
                for u in range(2):
                    i = 2 * j + u
                    if more:
                        wait_alone(pool, s_xT, i + 1, s_tick)
                        gather(i + 2, u)
                    wait_alone(pool, s_y, i + 1, s_tick)
                    if u == 1 or after_first(j):
                        wait_alone(pool, S["add"][1 - u], (j + u) * 16 * CT, s_tick)
                    pool.tensor_copy(ids[:, u, :], idx[:, bass.ds(i, 1), :].rearrange("p a g -> p (a g)"))
                    pool.drain()
                    for t in range(CT):
                        pool.indirect_dma_start(ybuf, bass.IndirectOffsetOnAxis(ap=ids[:, u, t:t + 1], axis=0),
                                                yo[:, u, t, :], None, compute_op=ALU.add).then_inc(S["add"][u], 16)

            pairs(pool, step, NE2)
            for u in range(2):
                pool.wait_ge(S["add"][u], NE2 * 16 * CT)

        @block.scalar
        def _(act):
            act.wait_ge(s_ws, 16 * NS)
            with act.Fori(0, NE2) as j:
                for u in range(2):
                    i = 2 * j + u
                    act.wait_ge(S["w"][u], (j + 1) * 16 * NW)
                    for q, bias in enumerate((b1[:, u, :], b1s)):
                        for m in range(HT):
                            act.wait_ge(s_hid[m], 2 * i + q + 1)
                            act.activation(hs[:, q, m, :], psh[:, m, :], ACT.Gelu_apprx_tanh, bias=bias[:, m:m + 1])\
                                .then_inc(s_gel[m], 1)

        @block.vector
        def _(dve):
            def evacuate(i, u):
                dve.wait_ge(s_T, i + 1)
                dve.tensor_copy(xT[:, u, :], psx[:, :])
                dve.drain()
                dve.tensor_copy(gw[:, u, :], xg[:, u, :, bass.ds(C + i, 1)].rearrange("p t a -> p (t a)"))\
                    .then_inc(s_xT, 1)

            dve.wait_ge(s_ws, 16 * NS)
            evacuate(0, 0)

            def step(j, more):
                for u in range(2):
                    i = 2 * j + u
                    if more or u == 0:
                        evacuate(i + 1, 1 - u)
                    dve.wait_ge(s_out, i + 1)
                    if after_first(j):
                        dve.wait_ge(S["add"][u], j * 16 * CT)
                    dve.tensor_tensor(yo[:, u, :, :], pso[:, 0, :].rearrange("p (t c) -> p t c", c=C),
                                      bc(b2[:, u, :], 1, CT), ALU.add)
                    dve.drain()
                    for t in range(CT):
                        last = dve.tensor_scalar(yo[:, u, t, :], yo[:, u, t, :], gw[:, u, t:t + 1], None, ALU.mult)
                    last.then_inc(s_y, 1)
                    dve.wait_ge(s_outs, i + 1)
                    dve.tensor_tensor(shared[:, bass.ds(i * CT, CT), :],
                                      pso[:, 1, :].rearrange("p (t c) -> p t c", c=C), bc(b2s[:, :], 1, CT),
                                      ALU.add).then_inc(s_ev, 1)

            pairs(dve, step, NE2)

        @block.tensor
        def _(pe):
            def gathered(i, j, u):
                pe.wait_ge(S["x"][u], (j + 1) * 16 * CT)
                for t in range(CT):
                    last = pe.transpose(psx[:, t * P:(t + 1) * P], xg[:, u, t, 0:C], k["ident"][:, :])
                last.then_inc(s_T, 1)

            def up(q, w, x, i):
                for m in range(HT):
                    if not isinstance(i, int) or i + q > 0:
                        pe.wait_ge(s_gel[m], 2 * i + q)
                    pe.matmul(psh[:, m, :], w[:, m * P:(m + 1) * P], x, start=True, stop=True).then_inc(s_hid[m], 1)

            def down(q, w, i, free, done):
                for m in range(HT):
                    pe.wait_ge(s_gel[m], 2 * i + q + 1)
                if not isinstance(i, int) or i > 0:
                    pe.wait_ge(free, i)
                for t in range(CT):
                    for m in range(HT):
                        last = pe.matmul(pso[:, q, t * P:(t + 1) * P], hs[:, q, m, t * P:(t + 1) * P], w[:, m, :],
                                         start=(m == 0), stop=(m == HT - 1))
                last.then_inc(done, 1)

            gathered(0, 0, 0)
            pe.wait_ge(s_ws, 16 * NS)

            def step(j, more):
                for u in range(2):
                    i = 2 * j + u
                    pe.wait_ge(S["w"][u], (j + 1) * 16 * NW)
                    pe.wait_ge(s_xT, i + 1)
                    up(0, w1[:, u, :], xT[:, u, :], i)
                    up(1, w1s, x2T[:, bass.ds(i * CH, CH)], i)
                    if more or u == 0:
                        gathered(i + 1, j + u, 1 - u)
                    down(0, w2[:, u, :, :], i, s_y, s_out)
                    down(1, w2s, i, s_ev, s_outs)

            pairs(pe, step, NE2)




NH, HD = 8, C // 8
KD = 9
E1 = 8
CAP1 = 2560
ROW1 = C + 1 + E1
DUMP = E1 * CAP1


def attention_block(nc, k, d, shared, ybuf, table, ybuf2):
    PT = 2 * UT
    NP = NU // 2
    BAND = 3 * P
    with Stage(nc, "att") as s:
        wq = s.sb("wq", [P, 3 * C])
        bq = s.sb("bq", [P, 3 * C])
        wd = s.sb("wd", [P, NH, KD])
        band = s.sb("band", [P, NH, BAND])
        wp = s.sb("wp", [P, C])
        bp = s.sb("bp", [P, C])
        wr = s.sb("wr", [P, E1])
        br = s.sb("br", [P, E1])
        eps = s.sb("eps", [P, 1])
        mask = s.sb("mask", [P, P])
        h3 = s.sb("h3", [P, 2, UT, C])
        ht = s.sb("ht", [P, 2, UT, C])
        xa = s.sb("xa", [P, 2, UT, C])
        xb = s.sb("xb", [P, 2, UT, C])
        xT = s.sb("xT", [P, 2, UNIT])
        qk = s.sb("qk", [P, 2, UT, 2 * C])
        sq = s.sb("sq", [P, 2, UT, 2 * C])
        rr = s.sb("rr", [P, 2, UT, 2 * NH])
        v = s.sb("v", [P, 2, UT, C])
        qT = s.sb("qT", [P, 2, UNIT])
        am = s.sb("am", [P, 2, UB, P])
        on = s.sb("on", [P, 2, UT, C])
        ro = s.sb("ro", [P, 2, UT, NH])
        bs = s.sb("bs", [P, 2, UT, 6])
        ba1, ba2 = s.sb("ba1", [P, 2, UT, 2]), s.sb("ba2", [P, 2, UT, 2])
        rb1, rb2 = s.sb("rb1", [P, 2, UT]), s.sb("rb2", [P, 2, UT])
        nb1, nb2 = s.sb("nb1", [P, 2, UT]), s.sb("nb2", [P, 2, UT])
        cT, x4T = xT, qT
        lg = s.sb("lg", [P, PT, E1])
        pr, one1, one2, tmp = (s.sb(n, [P, PT, E1]) for n in ("prb", "one1", "one2", "tmp"))
        both, run, reset = (s.sb(n, [P, E1, PT]) for n in ("both", "run", "reset"))
        carry, more8 = s.sb("carry", [P, E1]), s.sb("more8", [P, E1])
        rank, base = s.sb("rank", [P, E1]), s.sb("base", [P, E1])
        ranki, basei = s.sb("ranki", [P, E1], I32), s.sb("basei", [P, E1], I32)
        top = s.sb("top", [P, 2, PT])
        f = s.sb("f", [P, PT])
        kp, slot, num, dump = (s.sb(n, [P, 2, PT]) for n in ("kp", "slot", "num", "dump"))
        numi, sloti = s.sb("numi", [P, 2, PT], I32), s.sb("sloti", [P, 2, PT], I32)
        before = s.sb("before", [P, P])
        rows_out = s.sb("rows", [P, PT, ROW1])
        ps = s.pb("ps", [P, 2, 4, 512])
        names = ("ld", "h3", "bn", "sd", "rb", "xn", "Tx", "xT", "QK", "qk", "sq", "ssq", "rt", "kn", "V", "v",
                 "Tq", "qT", "at", "am", "dc", "o", "o2", "osq", "oss", "ro", "on", "To", "cT", "pr", "h4", "hb", "bn2",
                 "sd2", "rb2", "x4", "x4c", "T4", "x4T", "lg", "lgc", "sy")
        S = {n: s.sem2(n) for n in names}
        s_in, s_tick, s_mask, s_zero, s_band = (s.sem(n) for n in ("in", "tick", "mask", "zero", "band"))
        s_sub, s_exp, s_run, s_pos, s_posr, s_row, s_put = (
            s.sem(n) for n in ("sub", "exp", "run", "pos", "posr", "row", "put"))
        ps_pos = ps[:, 1, 3, 0:E1 * PT]
        block = s.block()
        flat = lambda ap: ap.rearrange("p a b -> p (a b)")
        bank = lambda u, n, m=2: ps[:, u, n:n + m, :].rearrange("p a b -> p (a b)")
        NIN = 8

        def rows(t, j, u):
            return t[bass.ds(j * 2 * UNIT + u * UNIT, UNIT), :].rearrange("(t p) c -> p t c", p=P)

        @block.sync
        def _(sp):
            for dst, src in (
                (wq[:, :], d["w_qkv"]), (bq[:, :], bc(d["b_qkv"], 0, P)),
                (wd[:, :, :], bc(d["w_dconv"].rearrange("h a k b -> h (a k b)"), 0, P)),
                (wp[:, :], d["w_proj"]), (bp[:, :], bc(d["b_proj"], 0, P)), (wr[:, :], d["Wr"]),
                (br[:, :], bc(d["br"], 0, P)),
            ):
                sp.dma_start(dst, src, allow_slow_non_contiguous=True).then_inc(s_in, 16)
            for u in range(2):
                sp.dma_start(h3[:, u, :, :], rows(ybuf, 0, u)).then_inc(S["ld"][u], 16)

            def step(j, more):
                if more:
                    for u in range(2):
                        sp.wait_ge(S["hb"][u], j + 1)
                        sp.dma_start(h3[:, u, :, :], rows(ybuf, j + 1, u)).then_inc(S["ld"][u], 16)
                for u in range(2):
                    sp.wait_ge(S["h4"][u], j + 1)
                    sp.dma_start(rows(ybuf2, j, u), ht[:, u, :, :]).then_inc(S["sy"][u], 16)

            pairs(sp, step)
            for u in range(2):
                sp.wait_ge(S["sy"][u], 16 * NP)

        @block.scalar
        def _(act):
            act.wait_ge(s_in, 16 * (NIN - 1))

            def deviations(ready, j, ba, rb, done):
                for u in range(2):
                    act.wait_ge(ready[u], j + 1)
                    act.activation(rb[:, u, :], ba[:, u, :, 1], ACT.Sqrt, bias=eps[:, 0:1]).then_inc(done[u], 1)

            def normalize(ready, j, dst, src, rb, nb, done):
                act.wait_ge(ready[0], j + 1)
                for t in range(UT):
                    last = act.activation(dst[:, 0, t, :], src[:, 0, t, :], ACT.Identity, scale=rb[:, 0, t:t + 1],
                                          bias=nb[:, 0, t:t + 1])
                last.then_inc(done[0], 1)

            def copies(ready, j, dst, done):
                for u in range(2):
                    act.wait_ge(ready[u], j + 1)
                    act.activation(dst[:, u, :], bank(u, 0), ACT.Copy).then_inc(done[u], 1)

            act.wait_ge(s_zero, 1)
            deviations(S["bn"], 0, ba1, rb1, S["sd"])
            normalize(S["rb"], 0, xa, h3, rb1, nb1, S["xn"])
            copies(S["Tx"], 0, xT, S["xT"])

            def step(j, more):
                for u in range(2):
                    act.wait_ge(S["qk"][u], j + 1)
                    act.activation(sq[:, u, :, :], qk[:, u, :, :], ACT.Square).then_inc(S["sq"][u], 1)
                for u in range(2):
                    act.wait_ge(S["ssq"][u], j + 1)
                    act.activation(rr[:, u, :, :], rr[:, u, :, :], ACT.Sqrt).then_inc(S["rt"][u], 1)
                for u in range(2):
                    act.wait_ge(S["Tq"][u], j + 1)
                    act.activation(qT[:, u, :], bank(u, 0), ACT.Copy).then_inc(S["qT"][u], 1)
                for u in range(2):
                    act.wait_ge(S["o2"][u], j + 1)
                    act.activation(sq[:, u, :, 0:C], on[:, u, :, :], ACT.Square).then_inc(S["osq"][u], 1)
                for u in range(2):
                    act.wait_ge(S["oss"][u], j + 1)
                    act.activation(ro[:, u, :, :], ro[:, u, :, :], ACT.Sqrt).then_inc(S["ro"][u], 1)
                for u in range(2):
                    act.wait_ge(S["To"][u], j + 1)
                    act.activation(cT[:, u, :], bank(u, 0), ACT.Copy).then_inc(S["cT"][u], 1)
                deviations(S["bn2"], j, ba2, rb2, S["sd2"])
                if more:
                    deviations(S["bn"], j + 1, ba1, rb1, S["sd"])
                if after_first(j):
                    act.wait_ge(S["x4c"][0], j)
                normalize(S["rb2"], j, xb, ht, rb2, nb2, S["x4"])
                if more:
                    normalize(S["rb"], j + 1, xa, h3, rb1, nb1, S["xn"])
                copies(S["T4"], j, x4T, S["x4T"])
                if more:
                    copies(S["Tx"], j + 1, xT, S["xT"])
                act.wait_ge(s_sub, j + 1)
                act.activation(pr[:, :, :], pr[:, :, :], ACT.Exp).then_inc(s_exp, 1)

            pairs(act, step)

        @block.gpsimd
        def _(pool):
            pool.memset(before[:, :], 1.0)
            pool.memset(reset[:, :, :], 1.0)
            pool.memset(carry[:, :], 0.0)
            pool.iota(ranki[:, :], pattern=[[-1, E1]], base=E1, channel_multiplier=0)
            pool.iota(basei[:, :], pattern=[[CAP1, E1]], base=0, channel_multiplier=0)
            pool.iota(numi[:, :, :], pattern=[[T, 2], [P, PT]], base=0, channel_multiplier=1)
            pool.drain()
            pool.memset(reset[:, :, 0:1], 0.0)
            pool.affine_select(out=before[:, :], in_=before[:, :], compare_op=ALU.is_gt, fill=0.0, base=0,
                               pattern=[[1, P]], channel_multiplier=-1)
            pool.tensor_copy(rank[:, :], ranki[:, :])
            pool.tensor_copy(base[:, :], basei[:, :])
            pool.tensor_copy(num[:, :, :], numi[:, :, :])
            pool.memset(band[:, :, :], 0.0)
            pool.memset(eps[:, :], 1e-5)
            pool.memset(mask[:, :], 1.0 / PI).then_inc(s_zero, 1)
            pool.drain()
            blocks = mask[:, :].rearrange("p (h e) -> p h e", e=HD)
            pool.affine_select(out=blocks, in_=blocks, compare_op=ALU.is_ge, fill=0.0, base=0,
                               pattern=[[-HD, NH], [0, HD]], channel_multiplier=1)
            pool.drain()
            pool.affine_select(out=blocks, in_=blocks, compare_op=ALU.is_ge, fill=0.0, base=HD - 1,
                               pattern=[[HD, NH], [0, HD]], channel_multiplier=-1).then_inc(s_mask, 1)
            pool.wait_ge(s_in, 16 * (NIN - 1))

            def residual(j, u):
                wait_alone(pool, S["ld"][u], (j + 1) * 16, s_tick)
                pool.tensor_tensor(h3[:, u, :, :], h3[:, u, :, :],
                                   shared[:, bass.ds(j * 2 * UT + u * UT, UT), :], ALU.add).then_inc(S["h3"][u], 1)

            for u in range(2):
                residual(0, u)

            def step(j, more):
                for u in range(2):
                    wait_alone(pool, S["xn"][u], j + 1, s_tick)
                    if after_first(j):
                        wait_alone(pool, S["sy"][u], j * 16, s_tick)
                    pool.tensor_tensor(ht[:, u, :, :], h3[:, u, :, :], bc(bp[:, :], 1, UT), ALU.add)\
                        .then_inc(S["hb"][u], 1)
                if more:
                    for u in range(2):
                        residual(j + 1, u)
                if after_first(j):
                    scatter(j - 1)
                for u in range(2):
                    wait_alone(pool, S["x4"][u], j + 1, s_tick)
                    if u == 0 and after_first(j):
                        wait_alone(pool, s_put, j * 16 * 2 * PT, s_tick)
                    pool.tensor_copy(rows_out[:, u * UT:(u + 1) * UT, 0:C], xb[:, u, :, :]).then_inc(S["x4c"][u], 1)

            def scatter(j):
                wait_alone(pool, s_row, j + 1, s_tick)
                for t in range(PT):
                    for q in range(2):
                        pool.indirect_dma_start(table, bass.IndirectOffsetOnAxis(ap=sloti[:, q, t:t + 1], axis=0),
                                                rows_out[:, t, :], None).then_inc(s_put, 16)

            pairs(pool, step)
            scatter(NP - 1)
            pool.wait_ge(s_put, NP * 16 * 2 * PT)

        @block.vector
        def _(dve):
            def norm_stats(src, u, ba, done):
                for t in range(UT):
                    dve.bn_stats(bs[:, u, t, :], src[:, u, t, :])
                dve.drain()
                for t in range(UT):
                    last = dve.bn_aggr(ba[:, u, t, :], bs[:, u, t, :])
                last.then_inc(done[u], 1)

            def input_stats(j):
                for u in range(2):
                    dve.wait_ge(S["h3"][u], j + 1)
                    norm_stats(h3, u, ba1, S["bn"])

            def norm_factors(ready, j, ba, rb, nb, done):
                for u in range(2):
                    dve.wait_ge(ready[u], j + 1)
                    dve.reciprocal(rb[:, u, :], rb[:, u, :])
                    dve.drain()
                    dve.scalar_tensor_tensor(nb[:, u, :], ba[:, u, :, 0], -1.0, rb[:, u, :], ALU.mult, ALU.mult)\
                        .then_inc(done[u], 1)

            def normalize(dst, src, ba, rb, done):
                for t in range(UT):
                    last = dve.tensor_scalar(dst[:, 1, t, :], src[:, 1, t, :], ba[:, 1, t, 0:1], rb[:, 1, t:t + 1],
                                             ALU.subtract, ALU.mult)
                last.then_inc(done[1], 1)

            heads = lambda ap: ap.rearrange("p t (h e) -> p (t h) e", e=HD)
            dve.wait_ge(s_in, 16 * (NIN - 1))
            dve.wait_ge(s_mask, 1)
            for n in range(KD):
                o = P + KD // 2 - n
                for h in range(NH):
                    last = dve.scalar_tensor_tensor(band[:, h, o:o + P], k["ident"][:, :], wd[:, h, n:n + 1],
                                                    band[:, h, o:o + P], ALU.mult, ALU.add)
                dve.drain()
            last.then_inc(s_band, 1)
            input_stats(0)
            norm_factors(S["sd"], 0, ba1, rb1, nb1, S["rb"])
            normalize(xa, h3, ba1, rb1, S["xn"])

            def step(j, more):
                for u in range(2):
                    dve.wait_ge(S["QK"][u], j + 1)
                    dve.tensor_tensor(qk[:, u, :, :], bank(u, 0, 4).rearrange("p (t n) -> p t n", n=2 * C),
                                      bc(bq[:, 0:2 * C], 1, UT), ALU.add).then_inc(S["qk"][u], 1)
                for u in range(2):
                    dve.wait_ge(S["V"][u], j + 1)
                    dve.tensor_tensor(v[:, u, :, :], bank(u, 0).rearrange("p (t n) -> p t n", n=C),
                                      bc(bq[:, 2 * C:3 * C], 1, UT), ALU.add).then_inc(S["v"][u], 1)
                    dve.wait_ge(S["sq"][u], j + 1)
                    dve.tensor_reduce(rr[:, u, :, :].rearrange("p t h -> p (t h)"), heads(sq[:, u, :, :]), AX,
                                      ALU.add).then_inc(S["ssq"][u], 1)
                for u in range(2):
                    dve.wait_ge(S["rt"][u], j + 1)
                    dve.reciprocal(rr[:, u, :, :], rr[:, u, :, :])
                    dve.drain()
                    kk = qk[:, u, :, C:2 * C].rearrange("p t (h e) -> p t h e", e=HD)
                    dve.tensor_tensor(kk, kk, bc(rr[:, u, :, NH:2 * NH], 3, HD), ALU.mult).then_inc(S["kn"][u], 1)
                for u in range(2):
                    dve.wait_ge(S["at"][u], j + 1)
                    dve.tensor_tensor(am[:, u, :, :], bank(u, 2, 1).rearrange("p (b n) -> p b n", n=P),
                                      bc(mask[:, :], 1, UB), ALU.mult).then_inc(S["am"][u], 1)
                for u in range(2):
                    dve.wait_ge(S["o"][u], j + 1)
                    dve.tensor_tensor(on[:, u, :, :].rearrange("p t (h e) -> p t h e", e=HD),
                                      bank(u, 0).rearrange("p (t h e) -> p t h e", e=HD, h=NH),
                                      bc(rr[:, u, :, 0:NH], 3, HD), ALU.mult)
                    dve.drain()
                    dve.scalar_tensor_tensor(on[:, u, :, :], v[:, u, :, :], 0.5, on[:, u, :, :], ALU.mult,
                                             ALU.add).then_inc(S["o2"][u], 1)
                for u in range(2):
                    dve.wait_ge(S["osq"][u], j + 1)
                    dve.tensor_reduce(ro[:, u, :, :], sq[:, u, :, 0:C].rearrange("p t (h e) -> p t h e", e=HD), AX,
                                      ALU.add).then_inc(S["oss"][u], 1)
                for u in range(2):
                    dve.wait_ge(S["ro"][u], j + 1)
                    oo = on[:, u, :, :].rearrange("p t (h e) -> p (t h) e", e=HD)
                    dve.reciprocal(ro[:, u, :, :], ro[:, u, :, :])
                    dve.drain()
                    dve.tensor_tensor(oo, oo, bc(ro[:, u, :, :].rearrange("p t h -> p (t h)"), 2, HD), ALU.mult)
                    dve.drain()
                    dve.wait_ge(S["dc"][u], j + 1)
                    oo = on[:, u, :, :].rearrange("p t (h e) -> p t h e", e=HD)
                    dve.tensor_tensor(oo, oo, bank(u, 2).rearrange("p (h t e) -> p t h e", e=HD, h=NH), ALU.add)\
                        .then_inc(S["on"][u], 1)
                for u in range(2):
                    dve.wait_ge(S["pr"][u], j + 1)
                    dve.wait_ge(S["hb"][u], j + 1)
                    dve.tensor_tensor(flat(ht[:, u, :, :]), bank(u, 2), flat(ht[:, u, :, :]), ALU.add)\
                        .then_inc(S["h4"][u], 1)
                    dve.drain()
                    norm_stats(ht, u, ba2, S["bn2"])
                if more:
                    input_stats(j + 1)
                norm_factors(S["sd2"], j, ba2, rb2, nb2, S["rb2"])
                if after_first(j):
                    dve.wait_ge(S["x4c"][1], j)
                normalize(xb, ht, ba2, rb2, S["x4"])
                if more:
                    norm_factors(S["sd"], j + 1, ba1, rb1, nb1, S["rb"])
                    normalize(xa, h3, ba1, rb1, S["xn"])
                for u in range(2):
                    dve.wait_ge(S["lg"][u], j + 1)
                    dve.tensor_tensor(lg[:, u * UT:(u + 1) * UT, :],
                                      ps[:, u, 2, 0:UT * E1].rearrange("p (t e) -> p t e", e=E1),
                                      bc(br[:, :], 1, UT), ALU.add).then_inc(S["lgc"][u], 1)
                dve.drain()
                route(j)

            te = lambda ap: ap.rearrange("p e t -> p t e")
            fl = lambda ap: ap.rearrange("p a b -> p (a b)")

            def route(j):
                def tt(out, a, b, op):
                    dve.tensor_tensor(out, a, b, op)
                    dve.drain()

                dve.tensor_reduce(f[:, :], lg[:, :, :], AX, ALU.max)
                dve.drain()
                dve.tensor_tensor(pr[:, :, :], lg[:, :, :], bc(f[:, :], 2, E1), ALU.subtract).then_inc(s_sub, 1)
                dve.wait_ge(s_exp, j + 1)
                dve.tensor_reduce(f[:, :], pr[:, :, :], AX, ALU.add)
                dve.drain()
                dve.reciprocal(f[:, :], f[:, :])
                dve.drain()
                tt(pr[:, :, :], pr[:, :, :], bc(f[:, :], 2, E1), ALU.mult)
                for q, hot in enumerate((one1, one2)):
                    dve.tensor_reduce(top[:, q, :], pr[:, :, :], AX, ALU.max)
                    dve.drain()
                    tt(tmp[:, :, :], pr[:, :, :], bc(top[:, q, :], 2, E1), ALU.is_equal)
                    tt(tmp[:, :, :], tmp[:, :, :], bc(rank[:, :], 1, PT), ALU.mult)
                    dve.tensor_reduce(f[:, :], tmp[:, :, :], AX, ALU.max)
                    dve.drain()
                    tt(hot[:, :, :], tmp[:, :, :], bc(f[:, :], 2, E1), ALU.is_equal)
                    if q == 0:
                        dve.scalar_tensor_tensor(pr[:, :, :], hot[:, :, :], -2.0, pr[:, :, :], ALU.mult, ALU.add)
                        dve.drain()
                tt(te(both[:, :, :]), one1[:, :, :], one2[:, :, :], ALU.add)
                dve.tensor_reduce(more8[:, :], both[:, :, :], AX, ALU.add)
                dve.tensor_tensor_scan(fl(run[:, :, :]), fl(reset[:, :, :]), fl(both[:, :, :]), 0.0, ALU.mult, ALU.add)
                dve.drain()
                tt(run[:, :, :], run[:, :, :], both[:, :, :], ALU.subtract)
                dve.tensor_tensor(run[:, :, :], run[:, :, :], bc(carry[:, :], 2, PT), ALU.add).then_inc(s_run, 1)
                dve.drain()
                dve.tensor_tensor(carry[:, :], carry[:, :], more8[:, :], ALU.add)
                dve.wait_ge(s_pos, j + 1)
                dve.tensor_copy(run[:, :, :], ps_pos.rearrange("p (e t) -> p e t", t=PT)).then_inc(s_posr, 1)
                dve.drain()
                dve.tensor_scalar(both[:, :, :], run[:, :, :], float(CAP1), None, ALU.is_lt)
                dve.tensor_tensor(run[:, :, :], run[:, :, :], bc(base[:, :], 2, PT), ALU.add)
                tt(f[:, :], top[:, 0, :], top[:, 1, :], ALU.add)
                dve.tensor_scalar(f[:, :], f[:, :], 1e-9, None, ALU.add)
                dve.drain()
                dve.reciprocal(f[:, :], f[:, :])
                dve.drain()
                dve.tensor_tensor(top[:, :, :], top[:, :, :], bc(f[:, :], 1, 2), ALU.mult)
                for q, hot in enumerate((one1, one2)):
                    tt(tmp[:, :, :], hot[:, :, :], te(both[:, :, :]), ALU.mult)
                    dve.tensor_reduce(kp[:, q, :], tmp[:, :, :], AX, ALU.add)
                    dve.drain()
                    tt(tmp[:, :, :], hot[:, :, :], te(run[:, :, :]), ALU.mult)
                    dve.tensor_reduce(slot[:, q, :], tmp[:, :, :], AX, ALU.add)
                    dve.drain()
                dve.tensor_tensor(top[:, :, :], top[:, :, :], kp[:, :, :], ALU.mult)
                dve.tensor_scalar(dump[:, :, :], num[:, :, :], float(DUMP), None, ALU.add)
                dve.drain()
                tt(slot[:, :, :], slot[:, :, :], dump[:, :, :], ALU.subtract)
                tt(slot[:, :, :], slot[:, :, :], kp[:, :, :], ALU.mult)
                tt(slot[:, :, :], slot[:, :, :], dump[:, :, :], ALU.add)
                tt(f[:, :], top[:, 0, :], top[:, 1, :], ALU.add)
                dve.tensor_scalar(f[:, :], f[:, :], 1e-9, None, ALU.add)
                dve.drain()
                dve.reciprocal(f[:, :], f[:, :])
                dve.drain()
                tt(top[:, :, :], top[:, :, :], bc(f[:, :], 1, 2), ALU.mult)
                for q, hot in enumerate((one1, one2)):
                    dve.tensor_tensor(hot[:, :, :], hot[:, :, :], bc(top[:, q, :], 2, E1), ALU.mult)
                dve.drain()
                for u in range(2):
                    dve.wait_ge(S["x4c"][u], j + 1)
                dve.tensor_copy(sloti[:, :, :], slot[:, :, :])
                dve.tensor_copy(rows_out[:, :, C], num[:, 0, :])
                dve.tensor_tensor(rows_out[:, :, C + 1:ROW1], one1[:, :, :], one2[:, :, :], ALU.add).then_inc(s_row, 1)
                dve.drain()
                dve.tensor_scalar(num[:, :, :], num[:, :, :], float(2 * UNIT), None, ALU.add)

            pairs(dve, step)

        @block.tensor
        def _(pe):
            pe.wait_ge(s_in, 16 * (NIN - 1))
            pe.wait_ge(s_band, 1)
            tile = lambda u, n, t: ps[:, u, n + t // 4, (t % 4) * P:(t % 4 + 1) * P]
            cols = lambda ap, t: ap[:, t * P:(t + 1) * P]

            def transposes(u, n, src, done):
                for t in range(UT):
                    last = pe.transpose(tile(u, n, t), src(t), k["ident"][:, :])
                last.then_inc(done, 1)

            def transpose_input(j):
                for u in range(2):
                    pe.wait_ge(S["xn"][u], j + 1)
                    transposes(u, 0, lambda t: xa[:, u, t, :], S["Tx"][u])

            transpose_input(0)

            def places(j):
                pe.wait_ge(s_run, j + 1)
                pe.matmul(ps_pos, before[:, :], both[:, :, :].rearrange("p e t -> p (e t)"), start=True, stop=False)
                pe.matmul(ps_pos, k["ones"][:, :], run[:, :, :].rearrange("p e t -> p (e t)"), start=False,
                          stop=True).then_inc(s_pos, 1)

            def step(j, more):
                for u in range(2):
                    if u == 1 and after_first(j):
                        places(j - 1)
                        pe.wait_ge(s_posr, j)
                    pe.wait_ge(S["xT"][u], j + 1)
                    if after_first(j):
                        pe.wait_ge(S["lgc"][u], j)
                    for t in range(UT):
                        last = pe.matmul(ps[:, u, t // 2, (t % 2) * 2 * C:(t % 2 + 1) * 2 * C], cols(xT[:, u, :], t),
                                         wq[:, 0:2 * C], start=True, stop=True)
                    last.then_inc(S["QK"][u], 1)
                for u in range(2):
                    pe.wait_ge(S["qk"][u], j + 1)
                    for t in range(UT):
                        last = pe.matmul(tile(u, 0, t), cols(xT[:, u, :], t), wq[:, 2 * C:3 * C], start=True, stop=True)
                    last.then_inc(S["V"][u], 1)
                for u in range(2):
                    pe.wait_ge(S["v"][u], j + 1)
                    transposes(u, 0, lambda t: qk[:, u, t, 0:C], S["Tq"][u])
                for u in range(2):
                    pe.wait_ge(S["kn"][u], j + 1)
                    for b in range(UB):
                        for t in range(2):
                            last = pe.matmul(ps[:, u, 2, b * P:(b + 1) * P], qk[:, u, 2 * b + t, C:2 * C],
                                             v[:, u, 2 * b + t, :], start=(t == 0), stop=(t == 1))
                    last.then_inc(S["at"][u], 1)
                for u in range(2):
                    pe.wait_ge(S["am"][u], j + 1)
                    pe.wait_ge(S["qT"][u], j + 1)
                    for t in range(UT):
                        last = pe.matmul(tile(u, 0, t), cols(qT[:, u, :], t), am[:, u, t // 2, :], start=True, stop=True)
                    last.then_inc(S["o"][u], 1)
                for u in range(2):
                    for h in range(NH):
                        vh = v[:, u, :, h * HD:(h + 1) * HD]
                        vs = vh.rearrange("p (b s) e -> p b s e", s=2)
                        out = bank(u, 2)[:, h * P:(h + 1) * P].rearrange("p (t e) -> p t e", e=HD)
                        outs = out.rearrange("p (b s) e -> p b s e", s=2)
                        pe.matmul(out, band[:, h, P:2 * P], vh, start=True, stop=False)
                        pe.matmul(outs[:, :, 0, :], band[:, h, 0:P], vs[:, :, 1, :], start=False, stop=False)
                        last = pe.matmul(outs[:, :, 1, :], band[:, h, 2 * P:3 * P], vs[:, :, 0, :],
                                         start=False, stop=True)
                    last.then_inc(S["dc"][u], 1)
                for u in range(2):
                    pe.wait_ge(S["on"][u], j + 1)
                    transposes(u, 0, lambda t: on[:, u, t, :], S["To"][u])
                for u in range(2):
                    pe.wait_ge(S["cT"][u], j + 1)
                    for t in range(UT):
                        last = pe.matmul(tile(u, 2, t), cols(cT[:, u, :], t), wp[:, :], start=True, stop=True)
                    last.then_inc(S["pr"][u], 1)
                for u in range(2):
                    pe.wait_ge(S["x4"][u], j + 1)
                    transposes(u, 0, lambda t: xb[:, u, t, :], S["T4"][u])
                for u in range(2):
                    pe.wait_ge(S["x4T"][u], j + 1)
                    for t in range(UT):
                        last = pe.matmul(ps[:, u, 2, t * E1:(t + 1) * E1], cols(x4T[:, u, :], t), wr[:, :],
                                         start=True, stop=True)
                    last.then_inc(S["lg"][u], 1)
                if more:
                    transpose_input(j + 1)

            pairs(pe, step)
            places(NP - 1)


def top2_experts(nc, k, d, table, ybuf2, out):
    NC1 = CAP1 // CH
    NE2 = E1 // 2
    BODY = 2 * NC1
    HALF = BODY // 2
    NW = 4
    with Stage(nc, "mo2") as s:
        w1 = s.sb("w1", [P, 2, H])
        w2 = s.sb("w2", [P, 2, HT, C])
        b1 = s.sb("b1", [P, 2, HT])
        b2 = s.sb("b2", [P, 2, C])
        xg = s.sb("xg", [P, 2, CT, ROW1])
        ids = s.sb("ids", [P, BODY, CT], I32)
        gw = s.sb("gw", [P, BODY, CT])
        xT = s.sb("xT", [P, 2, CH])
        hs = s.sb("hs", [P, 2, HT, CH])
        yo = s.sb("yo", [P, 2, CT, C])
        psx = s.pb("psx", [P, 512])
        psh = s.pb("psh", [P, 4, 512])
        pso = s.pb("pso", [P, 2, 512])
        S = {n: s.sem2(n) for n in ("w", "x", "add")}
        s_T, s_xT, s_out, s_y, s_tick, s_o = (s.sem(n) for n in ("T", "xT", "out", "y", "tick", "o"))
        s_hid = [s.sem(f"hid{n}") for n in range(HT)]
        s_gel = [s.sem(f"gel{n}") for n in range(HT)]
        block = s.block()

        class Piece:

            def __init__(self, j, i):
                j, i = j + i // BODY, i % BODY
                self.i, self.u, self.e, self.first = i, i % 2, i // NC1, i % NC1 == 0
                self.n, self.before, self.expert = j * BODY + i, j * HALF + i // 2, 2 * j + i // NC1
                self.there = not isinstance(j, int) or 0 <= j < NE2
                self.nth = not isinstance(j, int) or self.n > 0
                self.reuse = not isinstance(j, int) or self.n > 1

        @block.sync
        def _(sp):
            def rows(p):
                src = table[bass.ds(p.n * CH, CH), :] if not isinstance(p.n, int) else table[p.n * CH:(p.n + 1) * CH, :]
                sp.dma_start(xg[:, p.u, :, :], src.rearrange("(t p) c -> p t c", p=P)).then_inc(S["x"][p.u], 16)

            def load(expert, e):
                for dst, src in (
                    (w1[:, e, :], d["W1"][bass.ds(expert, 1), :, :].rearrange("a c h -> (a c) h")),
                    (w2[:, e, :, :], d["W2"][bass.ds(expert, 1), :, :].rearrange("a (k p) c -> p (a k) c", p=P)),
                    (b1[:, e, :], d["b1"][bass.ds(expert, 1), :].rearrange("a (k p) -> p (a k)", p=P)),
                    (b2[:, e, :], bc(d["b2"][bass.ds(expert, 1), :], 0, P).rearrange("q a c -> q (a c)")),
                ):
                    sp.dma_start(dst, src, allow_slow_non_contiguous=True).then_inc(S["w"][e], 16)

            rows(Piece(0, 0))
            load(0, 0)
            rows(Piece(0, 1))

            def step(j, more):
                for i in range(BODY):
                    p, later = Piece(j, i), Piece(j, i + 2)
                    if later.there:
                        sp.wait_ge(s_xT, p.n + 1)
                        rows(later)
                    if i % NC1 == 1 and (more or i < NC1):
                        if p.expert > 0 if isinstance(j, int) else True:
                            sp.wait_ge(s_y, p.n - 1)
                        load(p.expert + 1, 1 - p.e)

            pairs(sp, step, NE2)
            for u in range(2):
                sp.wait_ge(S["add"][u], NE2 * HALF * 16 * CT)
            sp.dma_start(out.rearrange("a b c -> (a b) c"), ybuf2[0:T, :]).then_inc(s_o, 16)
            sp.wait_ge(s_o, 16)

        @block.gpsimd
        def _(pool):
            def step(j, more):
                for i in range(BODY):
                    p = Piece(j, i)
                    wait_alone(pool, s_y, p.n + 1, s_tick)
                    if p.first and p.nth:
                        for q in range(2):
                            wait_alone(pool, S["add"][q], (j * HALF + (i + 1 - q) // 2) * 16 * CT, s_tick)
                    for t in range(CT):
                        pool.indirect_dma_start(ybuf2, bass.IndirectOffsetOnAxis(ap=ids[:, i, t:t + 1], axis=0),
                                                yo[:, p.u, t, :], None, compute_op=ALU.add).then_inc(S["add"][p.u], 16)

            pairs(pool, step, NE2)

        @block.scalar
        def _(act):
            with act.Fori(0, NE2) as j:
                for i in range(BODY):
                    p = Piece(j, i)
                    if p.first:
                        act.wait_ge(S["w"][p.e], (j + 1) * 16 * NW)
                    for m in range(HT):
                        act.wait_ge(s_hid[m], p.n + 1)
                        act.activation(hs[:, p.u, m, :], psh[:, m, :], ACT.Gelu, bias=b1[:, p.e, m:m + 1])\
                            .then_inc(s_gel[m], 1)

        @block.vector
        def _(dve):
            def evacuate(p):
                dve.wait_ge(s_T, p.n + 1)
                dve.tensor_copy(xT[:, p.u, :], psx[:, :])
                dve.tensor_copy(ids[:, p.i, :], xg[:, p.u, :, C])
                dve.tensor_copy(gw[:, p.i, :], xg[:, p.u, :, bass.ds(p.expert + C + 1, 1)]
                                .rearrange("p t a -> p (t a)")).then_inc(s_xT, 1)

            def finish(p):
                dve.wait_ge(s_out, p.n + 1)
                if p.reuse:
                    dve.wait_ge(S["add"][p.u], p.before * 16 * CT)
                dve.tensor_tensor(yo[:, p.u, :, :], pso[:, p.u, :].rearrange("p (t c) -> p t c", c=C),
                                  bc(b2[:, p.e, :], 1, CT), ALU.add)
                dve.drain()
                for t in range(CT):
                    last = dve.tensor_scalar(yo[:, p.u, t, :], yo[:, p.u, t, :], gw[:, p.i, t:t + 1], None, ALU.mult)
                last.then_inc(s_y, 1)

            evacuate(Piece(0, 0))

            def step(j, more):
                for i in range(BODY):
                    last, after = Piece(j, i - 1), Piece(j, i + 1)
                    if after.there:
                        evacuate(after)
                    if last.there:
                        finish(last)

            pairs(dve, step, NE2)
            finish(Piece(NE2 - 1, BODY - 1))

        @block.tensor
        def _(pe):
            def gathered(p):
                pe.wait_ge(S["x"][p.u], (p.before + 1) * 16)
                for t in range(CT):
                    last = pe.transpose(psx[:, t * P:(t + 1) * P], xg[:, p.u, t, 0:C], k["ident"][:, :])
                last.then_inc(s_T, 1)

            def up(p, j):
                if p.first:
                    pe.wait_ge(S["w"][p.e], (j + 1) * 16 * NW)
                pe.wait_ge(s_xT, p.n + 1)
                for m in range(HT):
                    if p.nth:
                        pe.wait_ge(s_gel[m], p.n)
                    pe.matmul(psh[:, m, :], w1[:, p.e, m * P:(m + 1) * P], xT[:, p.u, :], start=True,
                              stop=True).then_inc(s_hid[m], 1)

            def down(p):
                if p.reuse:
                    pe.wait_ge(s_y, p.n - 1)
                for m in range(HT):
                    pe.wait_ge(s_gel[m], p.n + 1)
                for t in range(CT):
                    for m in range(HT):
                        last = pe.matmul(pso[:, p.u, t * P:(t + 1) * P], hs[:, p.u, m, t * P:(t + 1) * P],
                                         w2[:, p.e, m, :], start=(m == 0), stop=(m == HT - 1))
                last.then_inc(s_out, 1)

            gathered(Piece(0, 0))

            def step(j, more):
                for i in range(BODY):
                    last, this, after = (Piece(j, i + o) for o in (-1, 0, 1))
                    up(this, j)
                    if after.there:
                        gathered(after)
                    if last.there:
                        down(last)

            pairs(pe, step, NE2)
            down(Piece(NE2 - 1, BODY - 1))


def tower(nc, d, out):
    xrows = nc.dram_tensor("xrows", [T, ROW], F32, kind="Internal").ap()
    ybuf = nc.dram_tensor("ybuf", [T, C], F32, kind="Internal").ap()
    ybuf2 = nc.dram_tensor("ybuf2", [T + CAP1, C], F32, kind="Internal").ap()
    table = nc.dram_tensor("table", [DUMP + 2 * T, ROW1], F32, kind="Internal").ap()
    part = lambda tag: {n[len(tag):]: a for n, a in d.items() if n.startswith(tag)}
    with Stage(nc, "top") as s:
        k = {n: s.sb(n, [P, P]) for n in ("ident", "cent", "mean", "ones", "half_mean")}
        k["nhalf"] = s.sb("nhalf", [P, 64])
        k["half"] = s.sb("half", [P, 64])
        hT = s.sb("hT", [P, T])
        constants(nc, k)
        with Stage(nc, "tok") as st:
            w = {"w1": st.sb("w1", [P, L, 2 * C]), "w2": st.sb("w2", [P, L, 2, C]), "cw": st.sb("cw", [P, L + 1, KC]),
                 "cb": st.sb("cb", [P, L + 1]), "gw": st.sb("gw", [P, L, 2]), "b1": st.sb("b1", [P, L, 2]),
                 "b2": st.sb("b2", [P, L])}
            block_weights(nc, k, w, part("L0_tok_"))
            token_embedding(nc, k, d["x"], d["L0_tok_emb_table"], d["L0_tok_pos_emb"], hT)
            convnext_blocks(nc, k, w, hT, table, ybuf2)
        x2T = s.sb("x2T", [P, T])
        lg = s.sb("lg", [P, NT, E0])
        with Stage(nc, "rec") as st:
            w = {"win": st.sb("win", [P, C]), "bin": st.sb("bin", [P, 1]), "bc": st.sb("bcw", [P, 3, P]),
                 "bA": st.sb("bA", [P, 1]), "bsw": st.sb("bsw", [P, 1]), "decay": st.sb("decay", [P, UNIT]),
                 "cos": st.sb("cos", [P, SEQ]), "sin": st.sb("sin", [P, SEQ]), "sinr": st.sb("sinr", [P, SEQ]),
                 "cp": st.sb("cp", [P, S_]), "cq": st.sb("cq", [P, S_]), "wout": st.sb("wout", [S_ + 1, C]),
                 "gate": st.sb("gate", [P, E0])}
            lru_weights(nc, k, w, {**part("L0_attn_"), "gate_w": d["L0_ffn_gate_w"]})
            lru_block(nc, k, w, hT, x2T, lg, xrows, ybuf)
        shared = hT[:, :].rearrange("p (t c) -> p t c", c=C)
        idx = s.sb("idx", [P, E0, CAP0 // P], I32)
        with Stage(nc, "exp") as st:
            pT = st.sb("pT", [P, T // SEG])
            softmax_experts(nc, k, lg, pT, xrows)
            select_tokens(nc, k, pT, idx)
        experts_choice(nc, k, part("L0_ffn_"), idx, xrows, x2T, ybuf, shared)
        attention_block(nc, k, {**part("L1_attn_"), **part("L1_ffn_")}, shared, ybuf, table, ybuf2)
        top2_experts(nc, k, part("L1_ffn_"), table, ybuf2, out)


_INS = ["x"] + ["L0_tok_" + n for n in ("emb_table", "pos_emb", "conv_w", "conv_b", "ln_g", "ln_b", "w1", "b1", "grn_w", "grn_b",
                                        "w2", "b2")] \
    + ["L0_attn_" + n for n in ("ln_w", "ln_b", "W_in", "conv_w", "conv_b", "nu_log", "theta_log", "gamma_log", "B_re",
                                "B_im", "C_re", "C_im", "W_out", "b_out")] \
    + ["L0_ffn_" + n for n in ("gate_w", "w1", "b1", "w2", "b2", "sw1", "sb1", "sw2", "sb2")] \
    + ["L1_attn_" + n for n in ("w_qkv", "b_qkv", "w_dconv", "w_proj", "b_proj")] \
    + ["L1_ffn_" + n for n in ("Wr", "br", "W1", "b1", "W2", "b2")]


def kernel(**inputs):
    import numpy as _np
    import concourse.bacc as _bacc
    from concourse import mybir as _mybir
    from concourse.bass_utils import run_bass_kernel_spmd as _run

    nc = _bacc.Bacc("TRN2", target_bir_lowering=False, num_devices=1)
    arrays, d = {}, {}
    for name in _INS:
        a = _np.ascontiguousarray(inputs[name])
        arrays[f"{name}_dram"] = a
        d[name] = nc.dram_tensor(f"{name}_dram", a.shape, _mybir.dt.from_np(a.dtype), kind="ExternalInput").ap()
    out = nc.dram_tensor("out_dram", (32, SEQ, C), _mybir.dt.from_np(_np.dtype("float32")), kind="ExternalOutput").ap()
    tower(nc, d, out)
    r = _run(nc, [arrays], core_ids=[0])
    return r.results[0]["out_dram"]
```

```python
from contextlib import ExitStack

import concourse.bass as bass
from concourse import mybir

F32 = mybir.dt.float32
BF16 = mybir.dt.bfloat16
I32 = mybir.dt.int32
ALU = mybir.AluOpType
ACT = mybir.ActivationFunctionType
AX = mybir.AxisListType.X

P = 128
C = 128
T = 8192
SEQ = 256
UNIT = 1024
NU = T // UNIT
UB = UNIT // SEQ
UT = UNIT // P
NT = T // P
L = 4
KC = 7
VOCAB_ROWS = 8001


class Stage:

    def __init__(self, nc, tag):
        self.nc, self.tag, self.ctx, self.sems = nc, tag, ExitStack(), []

    def __enter__(self):
        self.ctx.__enter__()
        return self

    def __exit__(self, *a):
        self.ctx.__exit__(*a)
        if self.sems and a[0] is None:
            self.nc.clear_and_free_semaphores(self.sems)
            self.nc.all_engine_barrier()

    def sb(self, name, shape, dt=F32):
        return self.ctx.enter_context(self.nc.sbuf_tensor(f"{self.tag}_{name}", shape, dt))

    def pb(self, name, shape, dt=F32):
        return self.ctx.enter_context(self.nc.psum_tensor(f"{self.tag}_{name}", shape, dt))

    def sem(self, name):
        self.sems.append(self.nc.alloc_semaphore(f"{self.tag}_{name}"))
        return self.sems[-1]

    def sem2(self, name):
        return [self.sem(f"{name}{u}") for u in range(2)]

    def block(self):
        return self.ctx.enter_context(self.nc.Block())


def bc(ap, at, n):
    pat = [list(x) for x in ap.ap]
    pat.insert(at, [0, n])
    return bass.AP(tensor=ap.tensor, offset=ap.offset, ap=pat)


def wait_alone(eng, sem, value, tick):
    eng.wait_ge(sem, value)
    eng.sem_inc(tick, 1)


def pairs(eng, step, n=NU // 2):
    step(0, True)
    with eng.Fori(1, n - 1) as j:
        step(j, True)
    step(n - 1, False)


def after_first(j):
    return not isinstance(j, int) or j > 0


def constants(nc, k):
    with Stage(nc, "cst") as s:
        s_m, s_i, s_d = s.sem("memset"), s.sem("ident"), s.sem("done")
        block = s.block()

        @block.gpsimd
        def _(pool):
            pool.memset(k["ident"][:, :], 0.0)
            pool.memset(k["mean"][:, :], 1.0 / C)
            pool.memset(k["ones"][:, :], 1.0)
            pool.memset(k["nhalf"][:, :], -0.5)
            pool.memset(k["half"][:, :], 0.5)
            pool.memset(k["half_mean"][:, :], 0.5 / C)
            pool.drain()
            pool.affine_select(out=k["ident"][:, :], in_=k["ident"][:, :], compare_op=ALU.not_equal, fill=1.0,
                               base=0, pattern=[[-1, P]], channel_multiplier=1)
            pool.drain()
            pool.tensor_tensor(k["cent"][:, :], k["ident"][:, :], k["mean"][:, :], ALU.subtract)


def prepare(nc, k, x, emb, pos, hT, w, d, rec, dr):
    with Stage(nc, "emb") as s:
        ids = s.sb("ids", [NT, P], I32)
        idf = s.sb("idf", [NT, P])
        idx = s.sb("idx", [P, NT], I32)
        idc = s.sb("idc", [P, 2, UT], I32)
        rows = s.sb("rows", [P, 2, UT, C])
        posr = s.sb("posr", [P, 2, C])
        posT = s.sb("posT", [P, SEQ])
        ps = s.pb("ps", [P, 2, UNIT])
        ps_small = s.pb("small", [P, 4, 512])
        ps_pos = ps_small[:, 0, 0:SEQ]
        ps_ids = ps_small[:, 0, SEQ:SEQ + NT]
        s_in, s_idf, s_tr, s_idx = s.sem("in"), s.sem("idf"), s.sem("tr"), s.sem("idx")
        s_rows, s_free, s_hT, s_ps = s.sem2("rows"), s.sem2("free"), s.sem2("hT"), s.sem2("ps")
        blocks = block_weights(s, k, w, d, ps_small)
        recurrent = lru_weights(s, k, rec, dr, ps_small)
        block = s.block()

        @block.sync
        def _(sp):
            sp.dma_start(ids[:, :], x.rearrange("a (b p) -> (a b) p", p=P)).then_inc(s_in, 16)
            sp.dma_start(posr[:, :, :], pos[0:SEQ, :].rearrange("(a p) c -> p a c", p=P)).then_inc(s_in, 16)
            blocks["sync"](sp)
            recurrent["sync"](sp)

        @block.scalar
        def _(act):
            recurrent["scalar"](act)

        @block.vector
        def _(dve):
            dve.wait_ge(s_in, 32)
            dve.tensor_scalar(idf[:, :], ids[:, :], float(VOCAB_ROWS - 1), None, ALU.min).then_inc(s_idf, 1)
            dve.wait_ge(s_tr, 1)
            dve.tensor_copy(idx[:, :], ps_ids)
            dve.tensor_copy(posT[:, :], ps_pos).then_inc(s_idx, 1)
            dve.drain()
            blocks["vector"](dve)
            recurrent["vector"](dve)
            with dve.Fori(0, NU // 2) as j:
                for u in range(2):
                    dve.wait_ge(s_ps[u], j + 1)
                    dst = hT[:, bass.ds(j * 2 * UNIT + u * UNIT, UNIT)].rearrange("p (b t) -> p b t", t=SEQ)
                    dve.tensor_tensor(dst, ps[:, u, :].rearrange("p (b t) -> p b t", t=SEQ),
                                      bc(posT[:, :], 1, UB), ALU.add).then_inc(s_hT[u], 1)

        @block.gpsimd
        def _(pool):
            pool.wait_ge(s_idx, 1)
            with pool.Fori(0, NU // 2) as j:
                for u in range(2):
                    pool.wait_ge(s_free[u], j + 1)
                    pool.tensor_copy(idc[:, u, :], idx[:, bass.ds(j * 2 * UT + u * UT, UT)])
                    pool.drain()
                    for t in range(UT):
                        pool.indirect_dma_start(rows[:, u, t, :], None, emb,
                                                bass.IndirectOffsetOnAxis(ap=idc[:, u, t:t + 1], axis=0))\
                            .then_inc(s_rows[u], 16)

        @block.tensor
        def _(pe):
            pe.sem_inc(s_free[0], 1)
            pe.sem_inc(s_free[1], 1)
            pe.wait_ge(s_idf, 1)
            pe.transpose(ps_ids, idf[:, :], k["ident"][0:NT, 0:NT])
            pe.transpose(ps_pos[:, 0:P], posr[:, 0, :], k["ident"][:, :])
            pe.transpose(ps_pos[:, P:SEQ], posr[:, 1, :], k["ident"][:, :]).then_inc(s_tr, 1)
            pe.wait_ge(s_idx, 1)
            blocks["tensor"](pe)
            recurrent["tensor"](pe)
            with pe.Fori(0, NU // 2) as j:
                for u in range(2):
                    pe.wait_ge(s_rows[u], j * 16 * UT + 16 * UT)
                    for t in range(UT):
                        last = pe.transpose(ps[:, u, t * P:(t + 1) * P], rows[:, u, t, :], k["ident"][:, :])
                    last.then_inc(s_ps[u], 1)
                    pe.wait_ge(s_hT[u], j + 1)
                    pe.sem_inc(s_free[u], 1)


def block_weights(s, k, w, d, ps):
    w1r = s.sb("bw_w1r", [P, L, 2 * C])
    w1g = s.sb("bw_w1g", [P, L, 2 * C])
    b1 = s.sb("bw_b1", [P, L, 2])
    b2 = s.sb("bw_b2", [P, L])
    lg = s.sb("bw_lg", [P, L])
    lb = s.sb("bw_lb", [P, L])
    gb = s.sb("bw_gb", [P, L, 2])
    ps_w = ps[:, 0:2, :].rearrange("p a (b n) -> p (a b) n", n=2 * C)
    ps_b = ps[:, 2, 0:32]
    s_in, s_g, s_mm, s_read = s.sem("bwin"), s.sem("g"), s.sem("mm"), s.sem("bwread")
    NIN = 10

    def sync(sp):
        for dst, src in (
            (w1r[:, :, :], d["w1"].rearrange("l c n -> c l n")),
            (w["w2"][:, :, :, :], d["w2"].rearrange("l (h p) c -> p l h c", p=P)),
            (w["cw"][:, 0:L, :], d["conv_w"].rearrange("l c o k -> c l (o k)")),
            (w["cb"][:, 0:L], d["conv_b"].rearrange("l c -> c l")),
            (lg[:, :], d["ln_g"].rearrange("l c -> c l")),
            (lb[:, :], d["ln_b"].rearrange("l c -> c l")),
            (b1[:, :, :], d["b1"].rearrange("l (h p) -> p l h", p=P)),
            (w["gw"][:, :, :], d["grn_w"].rearrange("l (h p) -> p l h", p=P)),
            (gb[:, :, :], d["grn_b"].rearrange("l (h p) -> p l h", p=P)),
            (b2[:, :], d["b2"].rearrange("l c -> c l")),
        ):
            sp.dma_start(dst, src, allow_slow_non_contiguous=True).then_inc(s_in, 16)

    def vector(dve):
        dve.wait_ge(s_in, 16 * NIN)
        dve.memset(w["cw"][:, L, :], 0.0)
        dve.memset(w["cb"][:, L:L + 1], 0.0)
        dve.tensor_tensor(w1g[:, :, :], w1r[:, :, :], bc(lg[:, :], 2, 2 * C), ALU.mult).then_inc(s_g, 1)
        dve.wait_ge(s_mm, 1)
        dve.tensor_copy(w["w1"][:, :, :], ps_w)
        dve.tensor_tensor(w["b1"][:, :, :], b1[:, :, :],
                          ps_b[:, 0:2 * L].rearrange("p (l h) -> p l h", h=2), ALU.add)
        dve.tensor_tensor(w["b2"][:, :], b2[:, :], ps_b[:, 2 * L:3 * L], ALU.add).then_inc(s_read, 1)

    def tensor(pe):
        pe.wait_ge(s_in, 16 * NIN)
        pe.wait_ge(s_g, 1)
        for l in range(L):
            pe.matmul(ps_w[:, l, :], k["cent"][:, :], w1g[:, l, :], start=True, stop=True)
            for h in range(2):
                pe.matmul(ps_b[:, 2 * l + h:2 * l + h + 1], w1r[:, l, h * C:(h + 1) * C], lb[:, l:l + 1],
                          start=True, stop=True)
            for h in range(2):
                last = pe.matmul(ps_b[:, 2 * L + l:2 * L + l + 1], w["w2"][:, l, h, :], gb[:, l, h:h + 1],
                                 start=(h == 0), stop=(h == 1))
        last.then_inc(s_mm, 1)
        pe.wait_ge(s_read, 1)

    return {"sync": sync, "vector": vector, "tensor": tensor}


def convnext_blocks(nc, k, w, hT, table, ybuf2):
    NALL = L * NU
    LAG = 3
    NP = NU // 2
    with Stage(nc, "cnx") as s:
        y = s.sb("y", [P, 2, UNIT])
        ysq = s.sb("ysq", [P, 2, UNIT])
        yn = s.sb("yn", [P, 2, UNIT])
        gl = s.sb("gl", [P, 2, 2, UNIT])
        junk = s.sb("junk", [P, 2, UB, SEQ], BF16)
        w1c = s.sb("w1c", [P, 2 * C])
        w2s = s.sb("w2s", [P, 2, 2, UB, C])
        out = s.sb("out", [P, 2, UNIT])
        st = s.sb("st", [P, 2, UT])
        rs = s.sb("rs", [P, 2, UT])
        ss = s.sb("ss", [P, 2, 2, UB])
        g = s.sb("g", [P, 2, 2, UB])
        gm = s.sb("gm", [P, 2, UB])
        gs = s.sb("gs", [P, 2, 2, UB])
        ps_wide = s.pb("pswide", [P, UNIT])
        ps_inv = s.pb("psinv", [P, UNIT])
        ps_out = s.pb("psout", [P, UNIT])
        ps_c = s.pb("psc", [P, UNIT])
        ps_gm = ps_out[:, 0:UB]
        S = {n: s.sem(n) for n in ("mid", "conv", "cent", "sq", "stat", "stc", "rs", "inv", "norm", "w1", "gelu", "ss", "g",
                                   "gm", "sc", "w2s", "w2", "out", "wl")}
        s_tick = s.sem("tick")
        CE = CAP1 // P
        empty = s.sb("empty", [P, CE, ROW1])
        num = s.sb("num", [P, CE], I32)
        s_empty, s_fill = s.sem("empty"), s.sem("fill")
        block = s.block()
        mid = KC // 2

        def seqs(ap):
            return ap.rearrange("p (b t) -> p b t", t=SEQ)

        class Item:

            def __init__(self, j, u, lag):
                self.v = (u - lag) & 1
                q = j + (u - lag) // 2
                self.n = q * 2 + self.v
                self.there = not isinstance(j, int) or 0 <= self.n < NALL
                if self.there:
                    self.l = q // NP
                    self.col = (q & (NP - 1)) * (2 * UNIT) + self.v * UNIT

            def unit(self):
                return hT[:, self.col:self.col + UNIT] if isinstance(self.col, int) else hT[:, bass.ds(self.col, UNIT)]

        def one(ap, i):
            return ap[:, i:i + 1] if isinstance(i, int) else ap[:, bass.ds(i, 1)]

        def steps(eng, step):
            fill = (LAG + 1) // 2
            for j in range(fill):
                step(j, 0)
                step(j, 1)
            with eng.Fori(fill, NALL // 2) as j:
                step(j, 0)
                step(j, 1)
            for n in range(NALL, NALL + LAG):
                step(n // 2, n % 2)

        @block.sync
        def _(sp):
            sp.wait_ge(s_empty, 1)
            for e in range(E1):
                sp.dma_start(table[e * CAP1:(e + 1) * CAP1, :].rearrange("(t p) c -> p t c", p=P), empty[:, :, :])\
                    .then_inc(s_fill, 16)
            sp.dma_start(ybuf2[T:T + CAP1, :].rearrange("(t p) c -> p t c", p=P), empty[:, :, 0:C]).then_inc(s_fill, 16)
            sp.wait_ge(s_fill, 16 * (E1 + 1))

        @block.vector
        def _(dve):
            def taps(i, some):
                src, dst = seqs(i.unit()), seqs(y[:, i.v, :])
                for t in some:
                    o = t - mid
                    a, b = max(0, -o), SEQ - max(0, o)
                    last = dve.scalar_tensor_tensor(dst[:, :, a:b], src[:, :, a + o:b + o],
                                                    w["cw"][:, i.l, t:t + 1], dst[:, :, a:b], ALU.mult, ALU.add)
                    if t < KC - 1:
                        dve.drain()
                return last

            def step(j, u):
                this, norm, last = Item(j, u, 0), Item(j, u, 1), Item(j, u, 3)
                if last.there:
                    v = last.v
                    dve.wait_ge(S["gm"], last.n + 1)
                    dve.tensor_scalar(gm[:, v, :], ps_gm, 1e-6, None, ALU.add)
                    dve.drain()
                    dve.reciprocal(gm[:, v, :], gm[:, v, :])
                    dve.drain()
                    dve.tensor_tensor(gs[:, v, :, :], g[:, v, :, :], bc(gm[:, v, :], 1, 2), ALU.mult)
                    dve.drain()
                    for h in range(2):
                        scaled = dve.tensor_scalar(gs[:, v, h, :], gs[:, v, h, :], w["gw"][:, last.l, h:h + 1], 1.0,
                                                   ALU.mult, ALU.add)
                    scaled.then_inc(S["sc"], 1)
                if this.there:
                    dve.wait_ge(S["mid"], this.n + 1)
                    taps(this, [t for t in range(KC) if t != mid]).then_inc(S["conv"], 1)
                if norm.there:
                    dve.wait_ge(S["inv"], norm.n + 1)
                    dve.tensor_tensor(yn[:, norm.v, :], y[:, norm.v, :], ps_inv[:, :], ALU.mult)\
                        .then_inc(S["norm"], 1)

            steps(dve, step)

        @block.scalar
        def _(act):
            def middle(i):
                act.activation(y[:, i.v, :], i.unit(), ACT.Identity, bias=one(w["cb"], i.l),
                               scale=w["cw"][:, i.l, mid:mid + 1]).then_inc(S["mid"], 1)

            def squares(i, h):
                for b in range(UB):
                    last = act.activation(junk[:, h, b, :], gl[:, i.v, h, b * SEQ:(b + 1) * SEQ], ACT.Square,
                                          accum_out=ss[:, i.v, h, b:b + 1])
                return last

            middle(Item(0, 0, 0))

            def step(j, u):
                this, after, wide, small = Item(j, u, 0), Item(j, u, -1), Item(j, u, 1), Item(j, u, 2)
                if after.there:
                    if wide.there:
                        wait_alone(act, S["norm"], wide.n + 1, s_tick)
                    middle(after)
                if this.there:
                    act.wait_ge(S["cent"], this.n + 1)
                    act.activation(ysq[:, this.v, :], ps_c[:, :], ACT.Square).then_inc(S["sq"], 1)
                if wide.there:
                    wait_alone(act, S["w1"], wide.n * 2 + 1, s_tick)
                    act.activation(gl[:, wide.v, 0, :], ps_wide[:, :], ACT.Gelu, bias=w["b1"][:, wide.l, 0:1])\
                        .then_inc(S["gelu"], 1)
                if this.there:
                    act.wait_ge(S["stat"], this.n + 1)
                    act.activation(st[:, this.v, :], ps_c[:, 0:UT], ACT.Copy)\
                        .then_inc(S["stc"], 1)
                if wide.there:
                    act.drain()
                    squares(wide, 0)
                    wait_alone(act, S["w1"], wide.n * 2 + 2, s_tick)
                    act.activation(gl[:, wide.v, 1, :], ps_wide[:, :], ACT.Gelu, bias=w["b1"][:, wide.l, 1:2])\
                        .then_inc(S["gelu"], 1)
                    act.drain()
                    squares(wide, 1).then_inc(S["ss"], 1)
                if small.there:
                    wait_alone(act, S["w2"], small.n + 1, s_tick)
                    act.activation(out[:, small.v, :], ps_out[:, :], ACT.Identity, bias=one(w["b2"], small.l))\
                        .then_inc(S["out"], 1)

            steps(act, step)

        @block.gpsimd
        def _(pool):
            pool.memset(empty[:, :, :], 0.0)
            pool.iota(num[:, :], pattern=[[P, CE]], base=T, channel_multiplier=1)
            pool.drain()
            pool.tensor_copy(empty[:, :, C], num[:, :]).then_inc(s_empty, 1)

            def step(j, u):
                i = Item(j, u, 2)
                if i.there:
                    wait_alone(pool, S["sc"], i.n + 1, s_tick)
                    for h in range(2):
                        last = pool.tensor_tensor(w2s[:, i.v, h, :, :], bc(w["w2"][:, i.l, h, :], 1, UB),
                                                  bc(gs[:, i.v, h, :], 2, C), ALU.mult)
                    last.then_inc(S["w2s"], 1)
                i = Item(j, u, 0)
                if i.there:
                    wait_alone(pool, S["stc"], i.n + 1, s_tick)
                    pool.tensor_scalar(rs[:, i.v, :], st[:, i.v, :], 1e-6, None, ALU.add)
                    pool.drain()
                    pool.tensor_tensor(rs[:, i.v, :], rs[:, i.v, :], k["nhalf"][:, 0:UT], ALU.pow)\
                        .then_inc(S["rs"], 1)
                    if u == 0:
                        if after_first(j):
                            wait_alone(pool, S["w1"], i.n * 2, s_tick)
                        pool.tensor_copy(w1c[:, :], w["w1"][:, i.l, :]).then_inc(S["wl"], 1)
                i = Item(j, u, 1)
                if i.there:
                    pool.wait_ge(S["ss"], i.n + 1)
                    pool.tensor_tensor(g[:, i.v, :, :], ss[:, i.v, :, :],
                                       k["half"][:, 0:2 * UB].rearrange("p (a b) -> p a b", a=2), ALU.pow)\
                        .then_inc(S["g"], 1)
                i = Item(j, u, 2)
                if i.there:
                    wait_alone(pool, S["out"], i.n + 1, s_tick)
                    pool.tensor_tensor(i.unit(), i.unit(), out[:, i.v, :], ALU.add)

            steps(pool, step)

        @block.tensor
        def _(pe):
            def widen(i, h):
                for c in range(2):
                    last = pe.matmul(ps_wide[:, c * 512:(c + 1) * 512], w1c[:, h * C:(h + 1) * C],
                                     yn[:, i.v, c * 512:(c + 1) * 512], start=True, stop=True)
                last.then_inc(S["w1"], 1)

            def narrow(i):
                for b in range(UB):
                    for h in range(2):
                        last = pe.matmul(ps_out[:, b * SEQ:(b + 1) * SEQ], w2s[:, i.v, h, b, :],
                                         gl[:, i.v, h, b * SEQ:(b + 1) * SEQ], start=(h == 0), stop=(h == 1))
                last.then_inc(S["w2"], 1)

            def step(j, u):
                this, wide, small = Item(j, u, 0), Item(j, u, 1), Item(j, u, 2)
                if this.there:
                    pe.wait_ge(S["conv"], this.n + 1)
                    for c in range(2):
                        last = pe.matmul(ps_c[:, c * 512:(c + 1) * 512], k["cent"][:, :],
                                         y[:, this.v, c * 512:(c + 1) * 512], start=True, stop=True)
                    last.then_inc(S["cent"], 1)
                if wide.there:
                    if u == 1:
                        pe.wait_ge(S["wl"], j + 1)
                    pe.wait_ge(S["norm"], wide.n + 1)
                    if small.there:
                        pe.wait_ge(S["gelu"], wide.n * 2)
                    widen(wide, 0)
                if this.there:
                    pe.wait_ge(S["sq"], this.n + 1)
                    for t in range(UT):
                        last = pe.matmul(ps_c[:, t:t + 1], ysq[:, this.v, t * P:(t + 1) * P], k["mean"][:, 0:1],
                                         start=True, stop=True)
                    last.then_inc(S["stat"], 1)
                if wide.there:
                    pe.wait_ge(S["gelu"], wide.n * 2 + 1)
                    widen(wide, 1)
                if small.there:
                    pe.wait_ge(S["w2s"], small.n + 1)
                    narrow(small)
                if this.there:
                    pe.wait_ge(S["rs"], this.n + 1)
                    for t in range(UT):
                        last = pe.matmul(ps_inv[:, t * P:(t + 1) * P], bc(rs[:, this.v, t:t + 1], 1, P)[:, :, 0],
                                         k["ident"][:, :], start=True, stop=True)
                    last.then_inc(S["inv"], 1)
                if wide.there:
                    pe.wait_ge(S["g"], wide.n + 1)
                    if small.there:
                        pe.wait_ge(S["out"], small.n + 1)
                    for h in range(2):
                        last = pe.matmul(ps_gm, k["half_mean"][:, :], g[:, wide.v, h, :], start=(h == 0), stop=(h == 1))
                    last.then_inc(S["gm"], 1)

            steps(pe, step)



S_ = 64
KA = 5
E0 = 16
ROW = C + E0
TWO_PI_HI, TWO_PI_LO = 6.28125, 0.0019353071795864769
PI = 3.14159265358979
ROUND = 12582912.0


def lru_weights(s, k, w, d, ps):
    wi = s.sb("lw_wi", [P, C])
    wit = s.sb("lw_wit", [P, C])
    lnw = s.sb("lw_lnw", [P, 2])
    cw = s.sb("lw_cw", [S_, S_, KA])
    cwt = s.sb("lw_cwt", [S_, KA + 1, S_])
    cb = s.sb("lw_cb", [S_, 1])
    par = s.sb("lw_par", [P, 3])
    ex = s.sb("lw_ex", [P, 3])
    lm = s.sb("lw_lm", [P, 1])
    lam = s.sb("lw_lam", [P, 1])
    ang = s.sb("lw_ang", [P, 2])
    q = s.sb("lw_q", [P, 2])
    tr = s.sb("lw_tr", [P, 2])
    bn = s.sb("lw_bn", [P, S_])
    bnT = s.sb("lw_bnT", [S_, P])
    cc = s.sb("lw_cc", [S_, 2, 2, S_])
    wo = s.sb("lw_wo", [P, S_])
    em = s.sb("lw_em", [P, 2])
    en = s.sb("lw_en", [P, 2])
    mix = s.sb("lw_mix", [P, 2, SEQ // 2])
    s_in, s_ex, s_lm, s_q, s_sin = s.sem("lwin"), s.sem("ex"), s.sem("lm"), s.sem("q"), s.sem("sin")
    s_bn, s_cc, s_t, s_bnT, s_m, s_cwt, s_wit = (s.sem(n) for n in ("bn", "cc", "t", "bnT", "m", "cwt", "wit"))
    NIN = 21
    ps_bn, ps_wo = ps[0:S_, 0, 0:P], ps[0:S_, 0, P:P + C]
    ps_c, ps_wi = ps[:, 1, 0:P], ps[:, 1, P:P + C]

    def sync(sp):
        col = lambda a: a.rearrange("(p a) -> p a", a=1)
        for dst, src in (
            (wi[0:S_, :], d["W_in"][S_:2 * S_, :]), (wi[S_:P, :], d["W_in"][0:S_, :]),
            (lnw[:, 0:1], col(d["ln_w"])), (lnw[:, 1:2], col(d["ln_b"])),
            (cw[:, :, :], d["conv_w"]), (cb[:, :], col(d["conv_b"])),
            (par[0:S_, 0:1], col(d["nu_log"])), (par[S_:P, 0:1], col(d["nu_log"])),
            (par[0:S_, 1:2], col(d["theta_log"])), (par[S_:P, 1:2], col(d["theta_log"])),
            (par[0:S_, 2:3], col(d["gamma_log"])), (par[S_:P, 2:3], col(d["gamma_log"])),
            (bn[0:S_, :], d["B_re"]), (bn[S_:P, :], d["B_im"]),
            (cc[:, 0, 0, :], d["C_re"]), (cc[:, 0, 1, :], d["C_im"]),
            (cc[:, 1, 0, :], d["C_im"]), (cc[:, 1, 1, :], d["C_re"]),
            (wo[:, :], d["W_out"]), (w["gate"][:, :], d["gate_w"]), (w["wout"][S_:S_ + 1, :], d["b_out"].rearrange("(a n) -> a n", a=1)),
        ):
            sp.dma_start(dst, src, allow_slow_non_contiguous=True).then_inc(s_in, 16)

    def scalar(act):
        act.wait_ge(s_in, 16 * NIN)
        act.activation(ex[:, :], par[:, :], ACT.Exp).then_inc(s_ex, 1)
        act.drain()
        act.activation(lm[:, :], ex[:, 0:1], ACT.Exp, scale=-1.0).then_inc(s_lm, 1)
        act.wait_ge(s_q, 1)
        act.activation(tr[:, :], ang[:, :], ACT.Sin).then_inc(s_sin, 1)

    def vector(dve):
        dve.wait_ge(s_in, 16 * NIN)
        dve.wait_ge(s_ex, 1)
        dve.tensor_scalar(bn[:, :], bn[:, :], ex[:, 2:3], None, ALU.mult).then_inc(s_bn, 1)
        dve.tensor_scalar(cc[:, 0, 1, :], cc[:, 0, 1, :], -1.0, None, ALU.mult)
        dve.tensor_scalar(cc[:, 1, :, :], cc[:, 1, :, :], -1.0, None, ALU.mult).then_inc(s_cc, 1)
        dve.tensor_copy(cwt[:, 0:KA, :], cw[:, :, :].rearrange("i j k -> i k j"))
        dve.memset(cwt[:, KA, :], 0.0).then_inc(s_cwt, 1)
        dve.tensor_scalar(ang[:, 0:1], ex[:, 1:2], PI / 2, None, ALU.add)
        dve.tensor_copy(ang[:, 1:2], ex[:, 1:2])
        dve.drain()
        dve.tensor_scalar(q[:, :], ang[:, :], 1.0 / (2 * PI), ROUND, ALU.mult, ALU.add)
        dve.drain()
        dve.tensor_scalar(q[:, :], q[:, :], ROUND, None, ALU.subtract)
        dve.drain()
        for part in (TWO_PI_HI, TWO_PI_LO):
            dve.scalar_tensor_tensor(ang[:, :], q[:, :], -part, ang[:, :], ALU.mult, ALU.add)
            dve.drain()
        dve.tensor_scalar(ang[:, :], ang[:, :], PI, -PI, ALU.min, ALU.max).then_inc(s_q, 1)
        dve.wait_ge(s_lm, 1)
        dve.memset(w["decay"][:, :], 1.0)
        dve.drain()
        dve.tensor_scalar(w["decay"][:, :], w["decay"][:, :], lm[:, :], None, ALU.mult)
        dve.drain()
        dve.memset(w["decay"][:, :].rearrange("p (b t) -> p b t", t=SEQ)[:, :, 0:1], 0.0)
        dve.wait_ge(s_sin, 1)
        cs, sn = w["cos"], w["sin"]
        dve.memset(cs[:, 0:1], 1.0)
        dve.memset(sn[:, 0:1], 0.0)
        dve.tensor_copy(em[:, :], tr[:, :])
        dve.drain()
        m = 1
        while m < SEQ:
            dve.tensor_scalar(mix[:, 0, 0:m], sn[:, 0:m], em[:, 1:2], None, ALU.mult)
            dve.tensor_scalar(mix[:, 1, 0:m], cs[:, 0:m], em[:, 1:2], None, ALU.mult)
            dve.tensor_tensor(en[:, :], em[:, :], em[:, :], ALU.mult)
            dve.drain()
            dve.scalar_tensor_tensor(cs[:, m:2 * m], cs[:, 0:m], em[:, 0:1], mix[:, 0, 0:m], ALU.mult, ALU.subtract)
            dve.scalar_tensor_tensor(sn[:, m:2 * m], sn[:, 0:m], em[:, 0:1], mix[:, 1, 0:m], ALU.mult, ALU.add)
            dve.tensor_tensor(en[:, 0:1], en[:, 0:1], en[:, 1:2], ALU.subtract)
            dve.drain()
            dve.scalar_tensor_tensor(em[:, 1:2], em[:, 1:2], 2.0, em[:, 0:1], ALU.mult, ALU.mult)
            dve.drain()
            dve.tensor_copy(em[:, 0:1], en[:, 0:1])
            dve.drain()
            m *= 2
        dve.tensor_copy(w["sinr"][0:S_, :], sn[0:S_, :])
        dve.tensor_scalar(w["sinr"][S_:P, :], sn[S_:P, :], -1.0, None, ALU.mult)
        dve.wait_ge(s_t, 1)
        dve.tensor_copy(bnT[:, :], ps_bn).then_inc(s_bnT, 1)
        dve.tensor_copy(w["cp"][:, :], ps_c[:, 0:S_])
        dve.tensor_copy(w["cq"][:, :], ps_c[:, S_:P])
        dve.tensor_copy(w["wout"][0:S_, :], ps_wo)
        dve.tensor_copy(wit[:, :], ps_wi).then_inc(s_wit, 1)
        dve.drain()
        dve.tensor_scalar(w["win"][:, :], wit[:, :], lnw[:, 0:1], None, ALU.mult)
        dve.wait_ge(s_m, 1)
        for n in range(3):
            dve.tensor_copy(w["bc"][:, n, :], ps[:, 2, n * P:(n + 1) * P])
        dve.tensor_copy(w["bA"][:, :], ps[:, 3, 0:1])
        dve.tensor_copy(w["bsw"][0:S_, :], ps[S_:P, 3, 0:1])
        dve.tensor_copy(w["bsw"][S_:P, :], ps[0:S_, 3, 0:1])
        dve.tensor_copy(w["bin"][:, :], ps[:, 3, 1:2])

    def tensor(pe):
        pe.wait_ge(s_in, 16 * NIN)
        pe.wait_ge(s_bn, 1)
        pe.wait_ge(s_cc, 1)
        pe.transpose(ps_bn, bn[:, :], k["ident"][:, :])
        for n in range(2):
            pe.transpose(ps_c[:, n * S_:(n + 1) * S_], cc[:, n, :, :].rearrange("o a s -> o (a s)"),
                         k["ident"][0:S_, 0:S_])
        pe.transpose(ps_wo, wo[:, :], k["ident"][:, :])
        pe.transpose(ps_wi, wi[:, :], k["ident"][:, :]).then_inc(s_t, 1)
        pe.wait_ge(s_bnT, 1)
        pe.wait_ge(s_cwt, 1)
        for n in range(3):
            pe.matmul(ps[:, 2, n * P:(n + 1) * P], cwt[:, 2 * n:2 * n + 2, :].rearrange("i a j -> i (a j)"),
                      bnT[:, :], start=True, stop=True)
        pe.matmul(ps[:, 3, 0:1], bnT[:, :], cb[:, :], start=True, stop=True)
        pe.wait_ge(s_wit, 1)
        pe.matmul(ps[:, 3, 1:2], wit[:, :], lnw[:, 1:2], start=True, stop=True).then_inc(s_m, 1)

    return {"sync": sync, "vector": vector, "scalar": scalar, "tensor": tensor}


def lru_block(nc, k, w, hT, x2T, lg, xrows, ybuf):
    NP = NU // 2
    W = SEQ + 4
    EPS = 1e-5
    with Stage(nc, "lru") as s:
        hx = s.sb("hx", [P, 2, UNIT])
        htk = s.sb("htk", [P, 2, UT, C])
        x1 = s.sb("x1", [P, 2, UT, C])
        z = s.sb("z", [P, 2, UT, C])
        zT = hx
        V2 = s.sb("V2", [P, 2, UB, W])
        gx = s.sb("gx", [S_, 2, UNIT])
        ta = s.sb("ta", [P, 2, UNIT])
        tb = s.sb("tb", [P, 2, UNIT])
        uu = s.sb("uu", [P, 2, UNIT])
        o = s.sb("o", [S_ + 1, 2, UNIT])
        ho = s.sb("ho", [P, 2, UT, C])
        bs = s.sb("bs", [P, 2, UT, 6])
        ba1, ba2 = s.sb("ba1", [P, 2, UT, 2]), s.sb("ba2", [P, 2, UT, 2])
        r1, rz, nb = s.sb("r1", [P, 2, UT]), s.sb("rz", [P, 2, UT]), s.sb("nb", [P, 2, UT])
        rb = s.sb("rb", [P, 2, UT])
        eps = s.sb("eps", [P, 2])
        x2 = tb
        x2c = s.sb("x2c", [P, 2, UNIT])
        ps = s.pb("ps", [P, 2, 4, 512])
        names = ("hx", "T1", "htk", "bn1", "sd1", "rs", "z", "x1", "Tz", "zT", "win", "V2", "gx", "A", "t", "u", "scan",
                 "q", "p", "y", "o", "wo", "h1", "bn", "sd", "x2", "T2", "x2T", "x2c", "lg", "lgc", "sx", "sy")
        S = {n: s.sem2(n) for n in names}
        s_pad, s_tick = s.sem("pad"), s.sem("tick")
        block = s.block()
        seqs = lambda ap: ap.rearrange("p (b t) -> p b t", t=SEQ)
        flat = lambda ap: ap.rearrange("p a b -> p (a b)")

        def bank(u, n, rows=slice(0, P)):
            return ps[rows, u, n:n + 2, :].rearrange("p a b -> p (a b)")

        @block.sync
        def _(sp):
            def step(j, more):
                for u in range(2):
                    rows = lambda t: t[bass.ds(j * 2 * UNIT + u * UNIT, UNIT), :].rearrange("(t p) c -> p t c", p=P)
                    sp.wait_ge(S["h1"][u], j + 1)
                    sp.dma_start(rows(ybuf), ho[:, u, :, :]).then_inc(S["sy"][u], 16)
                    sp.wait_ge(S["x2"][u], j + 1)
                    sp.dma_start(rows(xrows[:, 0:C]), x2[:, u, :].rearrange("p (t c) -> p t c", c=C))\
                        .then_inc(S["sx"][u], 16)

            pairs(sp, step)
            for u in range(2):
                sp.wait_ge(S["sy"][u], 16 * NP)
                sp.wait_ge(S["sx"][u], 16 * NP)

        @block.scalar
        def _(act):
            def copy_input(j):
                for u in range(2):
                    if after_first(j):
                        wait_alone(act, S["win"][u], j, s_tick)
                    act.activation(hx[:, u, :], hT[:, bass.ds(j * 2 * UNIT + u * UNIT, UNIT)], ACT.Copy)\
                        .then_inc(S["hx"][u], 1)

            def by_tokens(j):
                for u in range(2):
                    act.wait_ge(S["T1"][u], j + 1)
                    if after_first(j):
                        act.wait_ge(S["x1"][u], j)
                    act.activation(flat(htk[:, u, :, :]), bank(u, 0), ACT.Copy).then_inc(S["htk"][u], 1)

            def deviations(j):
                for u in range(2):
                    act.wait_ge(S["bn1"][u], j + 1)
                    act.activation(r1[:, u, :], ba1[:, u, :, 1], ACT.Sqrt, bias=eps[:, 0:1])
                    act.activation(rz[:, u, :], ba1[:, u, :, 1], ACT.Sqrt, bias=eps[:, 1:2], scale=1.0 + EPS)\
                        .then_inc(S["sd1"][u], 1)

            def with_norm(j, u):
                act.wait_ge(S["rs"][u], j + 1)
                if after_first(j):
                    act.wait_ge(S["h1"][u], j)
                for t in range(UT):
                    last = act.activation(x1[:, u, t, :], htk[:, u, t, :], ACT.Identity, scale=r1[:, u, t:t + 1],
                                          bias=nb[:, u, t:t + 1])
                last.then_inc(S["x1"][u], 1)

            def norm_by_channels(j):
                for u in range(2):
                    act.wait_ge(S["Tz"][u], j + 1)
                    act.activation(zT[:, u, :], bank(u, 0), ACT.Copy).then_inc(S["zT"][u], 1)

            def widened(j):
                for u in range(2):
                    act.wait_ge(S["win"][u], j + 1)
                    act.activation(V2[0:S_, u, :, 2:2 + SEQ], seqs(bank(u, 2, slice(0, S_))), ACT.Identity,
                                   bias=w["bin"][0:S_, 0:1])
                    act.activation(V2[S_:P, u, :, 1:1 + SEQ], seqs(bank(u, 2, slice(0, S_))), ACT.Identity,
                                   bias=w["bin"][0:S_, 0:1]).then_inc(S["V2"][u], 1)
                    act.activation(gx[:, u, :], bank(u, 2, slice(S_, P)), ACT.Gelu,
                                   bias=w["bin"][S_:P, 0:1]).then_inc(S["gx"][u], 1)

            act.wait_ge(s_pad, 3)
            copy_input(0)
            by_tokens(0)
            deviations(0)
            norm_by_channels(0)
            widened(0)
            for u in range(2):
                with_norm(0, u)

            def step(j, more):
                if more:
                    copy_input(j + 1)
                    by_tokens(j + 1)
                    deviations(j + 1)
                    norm_by_channels(j + 1)
                for u in range(2):
                    act.wait_ge(S["bn"][u], j + 1)
                    act.activation(rb[:, u, :], ba2[:, u, :, 1], ACT.Sqrt, bias=eps[:, 0:1]).then_inc(S["sd"][u], 1)
                if more:
                    widened(j + 1)
                for u in range(2):
                    act.wait_ge(S["T2"][u], j + 1)
                    act.activation(x2c[:, u, :], bank(u, 0), ACT.Copy).then_inc(S["x2c"][u], 1)
                    act.activation(x2T[:, bass.ds(j * 2 * UNIT + u * UNIT, UNIT)], bank(u, 0), ACT.Copy)\
                        .then_inc(S["x2T"][u], 1)
                if more:
                    for u in range(2):
                        with_norm(j + 1, u)

            pairs(act, step)

        @block.gpsimd
        def _(pool):
            pool.memset(eps[:, 0:1], EPS)
            pool.memset(eps[:, 1:2], EPS * EPS).then_inc(s_pad, 1)
            pool.memset(V2[:, :, :, :], 0.0).then_inc(s_pad, 1)
            pool.drain()
            pool.memset(o[S_:S_ + 1, :, :], 1.0).then_inc(s_pad, 1)
            pool.drain()

            def step(j, more):
                for u in range(2):
                    pool.wait_ge(S["t"][u], j + 1)
                    pool.tensor_tensor(uu[:, u, :], ta[:, u, :], tb[:, u, :], ALU.add).then_inc(S["u"][u], 1)
                for u in range(2):
                    pool.wait_ge(S["scan"][u], j + 1)
                    pool.tensor_tensor(seqs(tb[:, u, :]), seqs(uu[:, u, :]), bc(w["sin"][:, :], 1, UB),
                                       ALU.mult).then_inc(S["q"][u], 1)

            pairs(pool, step)

        @block.vector
        def _(dve):
            def stats(src, u, ba, done):
                for t in range(UT):
                    dve.bn_stats(bs[:, u, t, :], src[:, u, t, :])
                dve.drain()
                for t in range(UT):
                    last = dve.bn_aggr(ba[:, u, t, :], bs[:, u, t, :])
                last.then_inc(done[u], 1)

            def input_stats(j, u):
                dve.wait_ge(S["htk"][u], j + 1)
                stats(htk, u, ba1, S["bn1"])

            def norm(j, u):
                dve.wait_ge(S["sd1"][u], j + 1)
                dve.reciprocal(r1[:, u, :], r1[:, u, :])
                dve.reciprocal(rz[:, u, :], rz[:, u, :])
                dve.drain()
                dve.scalar_tensor_tensor(nb[:, u, :], ba1[:, u, :, 0], -1.0, r1[:, u, :], ALU.mult, ALU.mult)
                dve.drain()
                dve.tensor_scalar(r1[:, u, :], r1[:, u, :], 1.0, None, ALU.add).then_inc(S["rs"][u], 1)
                for t in range(UT):
                    last = dve.tensor_scalar(z[:, u, t, :], htk[:, u, t, :], ba1[:, u, t, 0:1],
                                             rz[:, u, t:t + 1], ALU.subtract, ALU.mult)
                last.then_inc(S["z"][u], 1)

            def logits(j):
                for u in range(2):
                    dve.wait_ge(S["lg"][u], j + 1)
                    dve.tensor_copy(lg[:, bass.ds(j * 2 * UT + u * UT, UT), :],
                                    ps[:, u, 2, 0:UT * E0].rearrange("p (t e) -> p t e", e=E0)).then_inc(S["lgc"][u], 1)

            for u in range(2):
                input_stats(0, u)
            for u in range(2):
                norm(0, u)

            def step(j, more):
                for u in range(2):
                    dve.wait_ge(S["A"][u], j + 1)
                    if after_first(j):
                        dve.wait_ge(S["sx"][u], j * 16)
                    dve.scalar_tensor_tensor(seqs(ta[:, u, :]), seqs(bank(u, 0)), w["bA"][:, 0:1],
                                             bc(w["cos"][:, :], 1, UB), ALU.add, ALU.mult)
                    dve.scalar_tensor_tensor(seqs(tb[0:S_, u, :]), seqs(bank(u, 0, slice(S_, P))), w["bsw"][0:S_, 0:1],
                                             bc(w["sinr"][0:S_, :], 1, UB), ALU.add, ALU.mult)
                    dve.scalar_tensor_tensor(seqs(tb[S_:P, u, :]), seqs(bank(u, 0, slice(0, S_))), w["bsw"][S_:P, 0:1],
                                             bc(w["sinr"][S_:P, :], 1, UB), ALU.add, ALU.mult).then_inc(S["t"][u], 1)
                if after_first(j):
                    logits(j - 1)
                for u in range(2):
                    if more:
                        input_stats(j + 1, u)
                    dve.wait_ge(S["u"][u], j + 1)
                    dve.tensor_tensor_scan(uu[:, u, :], w["decay"][:, :], uu[:, u, :], 0.0,
                                           ALU.mult, ALU.add).then_inc(S["scan"][u], 1)
                    dve.drain()
                    dve.tensor_tensor(seqs(ta[:, u, :]), seqs(uu[:, u, :]), bc(w["cos"][:, :], 1, UB),
                                      ALU.mult).then_inc(S["p"][u], 1)
                if more:
                    for u in range(2):
                        norm(j + 1, u)
                for u in range(2):
                    dve.wait_ge(S["y"][u], j + 1)
                    dve.wait_ge(S["gx"][u], j + 1)
                    dve.tensor_tensor(o[0:S_, u, :], bank(u, 2, slice(0, S_)), gx[:, u, :], ALU.mult)\
                        .then_inc(S["o"][u], 1)
                for u in range(2):
                    dve.wait_ge(S["wo"][u], j + 1)
                    dve.wait_ge(S["x1"][u], j + 1)
                    if after_first(j):
                        dve.wait_ge(S["sy"][u], j * 16)
                    dve.tensor_tensor(flat(ho[:, u, :, :]), bank(u, 0), flat(x1[:, u, :, :]), ALU.add)\
                        .then_inc(S["h1"][u], 1)
                    dve.drain()
                    stats(ho, u, ba2, S["bn"])
                for u in range(2):
                    dve.wait_ge(S["sd"][u], j + 1)
                    dve.reciprocal(rb[:, u, :], rb[:, u, :])
                    dve.drain()
                    for t in range(UT):
                        last = dve.tensor_scalar(x2[:, u, t * C:(t + 1) * C], ho[:, u, t, :], ba2[:, u, t, 0:1],
                                                 rb[:, u, t:t + 1], ALU.subtract, ALU.mult)
                    last.then_inc(S["x2"][u], 1)

            pairs(dve, step)
            logits(NP - 1)

        @block.tensor
        def _(pe):
            pe.wait_ge(s_pad, 3)
            tiles = lambda ap, t: ap[:, t * P:(t + 1) * P]
            halves = lambda c: slice(c * 512, (c + 1) * 512)

            def transposes(u, n, src, done):
                for t in range(UT):
                    last = pe.transpose(ps[:, u, n + t // 4, (t % 4) * P:(t % 4 + 1) * P], src(t), k["ident"][:, :])
                last.then_inc(done, 1)

            def by_tokens(j):
                for u in range(2):
                    pe.wait_ge(S["hx"][u], j + 1)
                    if after_first(j):
                        pe.wait_ge(S["t"][u], j)
                    transposes(u, 0, lambda t: tiles(hx[:, u, :], t), S["T1"][u])

            def norm_by_channels(j):
                for u in range(2):
                    pe.wait_ge(S["z"][u], j + 1)
                    transposes(u, 0, lambda t: z[:, u, t, :], S["Tz"][u])

            def widen(j):
                for u in range(2):
                    pe.wait_ge(S["zT"][u], j + 1)
                    for c in range(2):
                        last = pe.matmul(ps[:, u, 2 + c, :], w["win"][:, :], zT[:, u, halves(c)], start=True, stop=True)
                    last.then_inc(S["win"][u], 1)

            def inputs(j):
                for u in range(2):
                    pe.wait_ge(S["V2"][u], j + 1)
                    if after_first(j):
                        pe.wait_ge(S["x2T"][u], j)
                    for c in range(2):
                        for n in range(3):
                            rows = slice(0, P if n < 2 else S_)
                            last = pe.matmul(ps[:, u, c, :].rearrange("p (b t) -> p b t", t=SEQ), w["bc"][rows, n, :],
                                             V2[rows, u, 2 * c:2 * c + 2, 2 * n:2 * n + SEQ],
                                             start=(n == 0), stop=(n == 2))
                    last.then_inc(S["A"][u], 1)

            by_tokens(0)
            norm_by_channels(0)
            widen(0)
            inputs(0)

            def step(j, more):
                if more:
                    by_tokens(j + 1)
                for u in range(2):
                    pe.wait_ge(S["gx"][u], j + 1)
                    if after_first(j):
                        pe.wait_ge(S["lgc"][u], j)
                    pe.wait_ge(S["p"][u], j + 1)
                    pe.wait_ge(S["q"][u], j + 1)
                    for c in range(2):
                        pe.matmul(ps[0:S_, u, 2 + c, :], w["cp"][:, :], ta[:, u, halves(c)], start=True, stop=False)
                        last = pe.matmul(ps[0:S_, u, 2 + c, :], w["cq"][:, :], tb[:, u, halves(c)],
                                         start=False, stop=True)
                    last.then_inc(S["y"][u], 1)
                if more:
                    norm_by_channels(j + 1)
                for u in range(2):
                    pe.wait_ge(S["o"][u], j + 1)
                    if more:
                        pe.wait_ge(S["zT"][u], j + 2)
                    for t in range(UT):
                        last = pe.matmul(ps[:, u, t // 4, (t % 4) * P:(t % 4 + 1) * P], tiles(o[:, u, :], t),
                                         w["wout"][:, :], start=True, stop=True)
                    last.then_inc(S["wo"][u], 1)
                if more:
                    widen(j + 1)
                for u in range(2):
                    pe.wait_ge(S["x2"][u], j + 1)
                    transposes(u, 0, lambda t: tiles(x2[:, u, :], t), S["T2"][u])
                if more:
                    inputs(j + 1)
                for u in range(2):
                    pe.wait_ge(S["x2c"][u], j + 1)
                    if more:
                        pe.wait_ge(S["gx"][u], j + 2)
                    for t in range(UT):
                        last = pe.matmul(ps[:, u, 2, t * E0:(t + 1) * E0], tiles(x2c[:, u, :], t), w["gate"][:, :],
                                         start=True, stop=True)
                    last.then_inc(S["lg"][u], 1)

            pairs(pe, step)


CAP0 = T // E0
H = 512
HT = H // P
CH = 512
CT = CH // P
SEG = P // E0
ST = NT // SEG


def softmax_experts(nc, k, lg, pT, xrows):
    with Stage(nc, "smx") as s:
        mx = s.sb("mx", [P, NT])
        pr = s.sb("pr", [P, ST, SEG, E0])
        ps = s.pb("ps", [P, 2, 512])
        s_sub, s_exp, s_pr, s_pc, s_t, s_x = (s.sem(n) for n in ("sub", "exp", "pr", "pc", "t", "x"))
        block = s.block()

        @block.vector
        def _(dve):
            dve.tensor_reduce(mx[:, :], lg[:, :, :], AX, ALU.max)
            dve.drain()
            dve.tensor_tensor(lg[:, :, :], lg[:, :, :], bc(mx[:, :], 2, E0), ALU.subtract).then_inc(s_sub, 1)
            dve.wait_ge(s_exp, 1)
            dve.tensor_reduce(mx[:, :], lg[:, :, :], AX, ALU.add)
            dve.drain()
            dve.reciprocal(mx[:, :], mx[:, :])
            dve.drain()
            dve.tensor_tensor(lg[:, :, :], lg[:, :, :], bc(mx[:, :], 2, E0), ALU.mult).then_inc(s_pr, 1)
            dve.drain()
            dve.tensor_copy(pr[:, :, :, :], lg[:, :, :].rearrange("p (s t) e -> p t s e", s=SEG)).then_inc(s_pc, 1)
            dve.wait_ge(s_t, 1)
            dve.tensor_copy(pT[:, :], ps[:, :, :].rearrange("p a b -> p (a b)"))

        @block.scalar
        def _(act):
            act.wait_ge(s_sub, 1)
            act.activation(lg[:, :, :], lg[:, :, :], ACT.Exp).then_inc(s_exp, 1)

        @block.tensor
        def _(pe):
            pe.wait_ge(s_pc, 1)
            for t in range(ST):
                last = pe.transpose(ps[:, t // 4, (t % 4) * P:(t % 4 + 1) * P],
                                    pr[:, t, :, :].rearrange("p s e -> p (s e)"), k["ident"][:, :])
            last.then_inc(s_t, 1)

        @block.sync
        def _(sp):
            sp.wait_ge(s_pr, 1)
            sp.dma_start(xrows[:, C:ROW].rearrange("(t p) e -> p t e", p=P), lg[:, :, :],
                         allow_slow_non_contiguous=True).then_inc(s_x, 16)
            sp.wait_ge(s_x, 16)


def select_tokens(nc, k, d, x2T, pT, idx, shared):
    BITS = 30
    STEPS = 5
    TILES = 2 * HT
    BUFS = 4
    with Stage(nc, "sel") as s:
        same = s.sb("same", [P, P])
        lower = s.sb("lower", [P, P])
        thr = s.sb("thr", [P, 1], I32)
        cand = s.sb("cand", [P, 1], I32)
        bit = s.sb("bit", [P, 1], I32)
        keep = s.sb("keep", [P, 1], I32)
        cnt = s.sb("cnt", [P, 4])
        junk = s.sb("junk", [P, T // SEG], BF16)
        gt = s.sb("gt", [P, T // SEG])
        eq = s.sb("eq", [P, T // SEG])
        rk = s.sb("rk", [P, T // SEG])
        one = s.sb("one", [P, T // SEG])
        lim = s.sb("lim", [P, 2])
        sl = s.sb("sl", [P, SEG, ST, E0], I32)
        si = s.sb("si", [P, SEG, ST, E0], I32)
        lo = s.sb("lo", [P, NT, E0], BF16)
        hi = s.sb("hi", [P, NT, E0], BF16)
        io = s.sb("io", [P, 32, E0], I32)
        iob = s.sb("iob", [P, 32, E0], BF16)
        ioe = s.sb("ioe", [P, E0, 32], BF16)
        tok = s.sb("tok", [P, 1 + NT])
        toki = s.sb("toki", [P, 1 + NT], I32)
        oa = s.sb("oa", [P, BUFS, E0, 32], BF16)
        ob = s.sb("ob", [P, BUFS, 16, E0], BF16)
        ov = s.sb("ov", [P, BUFS, 2, 16, E0], BF16)
        zz = s.sb("zz", [P, P], BF16)
        ls = s.sb("ls", [P, 4, 2, 16, 4])
        psh = s.pb("psh", [P, 4, 512])
        psc = s.pb("psc", [P, 512])
        w1 = s.sb("w1", [P, H])
        w2 = s.sb("w2", [P, HT, C])
        b1 = s.sb("b1", [P, HT])
        b2 = s.sb("b2", [P, C])
        hs = s.sb("hs", [P, HT, CH])
        psu = s.pb("psu", [P, 2, 512])
        pso = s.pb("pso", [P, 512])
        s_w, s_hid, s_gel, s_out, s_ev = (s.sem(n) for n in ("w", "hid", "gel", "out", "ev"))
        s_set, s_tick = s.sem("set"), s.sem("tick")
        s_cnt, s_sum = s.sem("cnt"), s.sem("sum")
        s_ge, s_tot, s_cs, s_off, s_v, s_vt = (s.sem(n) for n in ("ge", "tot", "cs", "off", "v", "vt"))
        s_oh, s_ob, s_ov, s_li = ([s.sem(f"{n}{u}") for u in range(BUFS)] for n in ("oh", "ob", "ov", "li"))
        s_end = s.sem("end")
        block = s.block()

        @block.sync
        def _(sp):
            for dst, src in ((w1[:, :], d["sw1"]), (w2[:, :, :], d["sw2"].rearrange("(k p) c -> p k c", p=P)),
                             (b1[:, :], d["sb1"].rearrange("(k p) -> p k", p=P)), (b2[:, :], bc(d["sb2"], 0, P))):
                sp.dma_start(dst, src, allow_slow_non_contiguous=True).then_inc(s_w, 16)

        @block.gpsimd
        def _(pool):
            pool.memset(lower[:, :], 0.0)
            pool.drain()
            for n in range(1, SEG):
                pool.affine_select(out=lower[:, :], in_=lower[:, :], compare_op=ALU.not_equal, fill=1.0,
                                   base=E0 * n, pattern=[[-1, P]], channel_multiplier=1)
                pool.drain()
            pool.tensor_tensor(same[:, :], lower[:, :], k["ident"][:, :], ALU.add)
            pool.drain()
            for n in range(1, SEG):
                last = pool.affine_select(out=same[:, :], in_=same[:, :], compare_op=ALU.not_equal, fill=1.0,
                                          base=-E0 * n, pattern=[[-1, P]], channel_multiplier=1)
                if n == SEG - 1:
                    last.then_inc(s_set, 1)
                else:
                    pool.drain()
            pool.memset(one[:, :], 1.0)
            pool.memset(zz[:, :], 0.0)
            pool.iota(toki[:, 0:1], pattern=[[0, 1]], base=0, channel_multiplier=1)
            pool.iota(toki[:, 1:1 + NT], pattern=[[1, NT]], base=0, channel_multiplier=0)
            pool.iota(io[:, :, :], pattern=[[1, 32], [0, E0]], base=0, channel_multiplier=0)
            pool.drain()
            pool.tensor_copy(tok[:, :], toki[:, :])
            pool.tensor_copy(iob[:, :, :], io[:, :, :])
            pool.tensor_copy(ioe[:, :, :], io[:, :, :].rearrange("p b e -> p e b")).then_inc(s_set, 1)

        @block.scalar
        def _(act):
            act.wait_ge(s_set, 2)
            act.wait_ge(s_w, 64)
            with act.Fori(0, NT // TILES) as j:
                for n in range(TILES):
                    u = n % BUFS
                    wait_alone(act, s_ob[u], j * (TILES // BUFS) + n // BUFS + 1, s_tick)
                    act.activation(ov[:, u, 0, :, :], ob[:, u, :, :], ACT.Copy, scale=tok[:, 0:1])
                    act.activation(ov[:, u, 1, :, :], ob[:, u, :, :], ACT.Copy, scale=tok[:, bass.ds(TILES * j + n + 1, 1)])\
                        .then_inc(s_ov[u], 1)
                    if 1 <= n <= HT:
                        m = n - 1
                        act.wait_ge(s_hid, HT * j + m + 1)
                        act.activation(hs[:, m, :], psu[:, m % 2, :], ACT.Gelu_apprx_tanh, bias=b1[:, m:m + 1])\
                            .then_inc(s_gel, 1)

        @block.vector
        def _(dve):
            dve.memset(thr[:, :], 0)
            dve.memset(bit[:, :], 1 << 29)
            dve.wait_ge(s_set, 1)
            dve.drain()

            def settle(n):
                dve.tensor_tensor(cand[:, :], thr[:, :], bit[:, :], ALU.bitwise_or)
                dve.drain()
                dve.tensor_scalar(junk[:, :], pT[:, :], cand[:, :].bitcast(F32), None, ALU.is_ge, ALU.add,
                                  accum_out=cnt[:, 0:1]).then_inc(s_cnt, 1)
                dve.tensor_scalar(bit[:, :], bit[:, :], 1, None, ALU.logical_shift_right)
                dve.wait_ge(s_sum, n + 1)
                dve.tensor_scalar(keep[:, :], psc[:, 0:1], CAP0 - 0.5, None, ALU.is_ge)
                dve.drain()
                dve.copy_predicated(thr[:, :], keep[:, :], cand[:, :])
                dve.drain()

            with dve.Fori(0, BITS // STEPS) as j:
                for n in range(STEPS):
                    settle(j * STEPS + n)
            dve.wait_ge(s_set, 2)
            thf = thr[:, :].bitcast(F32)
            dve.tensor_scalar(gt[:, :], pT[:, :], thf, None, ALU.is_gt, ALU.add, accum_out=cnt[:, 0:1])
            dve.tensor_scalar(eq[:, :], pT[:, :], thf, None, ALU.is_equal, ALU.add, accum_out=cnt[:, 1:2])\
                .then_inc(s_ge, 1)
            dve.drain()
            dve.tensor_tensor_scan(rk[:, :], one[:, :], eq[:, :], 0.0, ALU.mult, ALU.add)
            dve.wait_ge(s_tot, 1)
            dve.tensor_scalar(lim[:, 0:1], psc[:, 1:2], -1.0, float(CAP0), ALU.mult, ALU.add)
            dve.drain()
            dve.tensor_tensor(lim[:, 0:1], lim[:, 0:1], psc[:, 2:3], ALU.subtract)
            dve.drain()
            dve.scalar_tensor_tensor(eq[:, :], rk[:, :], lim[:, 0:1], eq[:, :], ALU.is_le, ALU.mult)
            dve.drain()
            dve.tensor_tensor(gt[:, :], gt[:, :], eq[:, :], ALU.add)
            dve.drain()
            dve.tensor_tensor_scan(rk[:, :], one[:, :], gt[:, :], 0.0, ALU.mult, ALU.add).then_inc(s_cs, 1)
            dve.wait_ge(s_off, 1)
            dve.tensor_copy(lim[:, 1:2], psc[:, 3:4])
            dve.drain()
            dve.scalar_tensor_tensor(rk[:, :], rk[:, :], lim[:, 1:2], gt[:, :], ALU.add, ALU.mult).then_inc(s_v, 1)
            dve.wait_ge(s_vt, 1)
            for q in range(2):
                dve.tensor_scalar(si[:, :, q * 4:(q + 1) * 4, :],
                                  psh[:, q, :].rearrange("p (t s e) -> p s t e", s=SEG, e=E0), -1.0, None, ALU.add)
            dve.drain()
            dve.tensor_scalar(sl[:, :, :, :], si[:, :, :, :], 31, None, ALU.bitwise_and)
            dve.tensor_scalar(si[:, :, :, :], si[:, :, :, :], 5, None, ALU.arith_shift_right)
            dve.drain()
            dve.tensor_copy(lo[:, :, :], sl[:, :, :, :].rearrange("p s t e -> p (s t) e"))
            dve.tensor_copy(hi[:, :, :], si[:, :, :, :].rearrange("p s t e -> p (s t) e"))
            dve.drain()

            def one_hots(j):
                for n in range(TILES):
                    t, u, before = TILES * j + n, n % BUFS, j * (TILES // BUFS) + n // BUFS
                    if after_first(j) or n >= BUFS:
                        dve.wait_ge(s_li[u], before)
                    dve.tensor_tensor(ob[:, u, :, :], bc(hi[:, bass.ds(t, 1), :], 1, 16)[:, :, 0, :], iob[:, 0:16, :],
                                      ALU.is_equal).then_inc(s_ob[u], 1)
                    dve.tensor_tensor(oa[:, u, :, :], bc(lo[:, bass.ds(t, 1), :], 3, 32)[:, 0, :, :], ioe[:, :, :],
                                      ALU.is_equal).then_inc(s_oh[u], 1)
                    if n == 2 and after_first(j):
                        shared_piece(j - 1)

            def shared_piece(j):
                dve.wait_ge(s_out, j + 1)
                dve.tensor_tensor(shared[:, bass.ds(j * CT, CT), :], pso[:, :].rearrange("p (t c) -> p t c", c=C),
                                  bc(b2[:, :], 1, CT), ALU.add).then_inc(s_ev, 1)

            dve.wait_ge(s_w, 64)
            one_hots(0)
            with dve.Fori(1, NT // TILES) as j:
                one_hots(j)
            shared_piece(NT // TILES - 1)
            dve.wait_ge(s_end, 1)
            dve.tensor_copy(ls[:, :, :, :, :].rearrange("p g v a e -> p g (v a e)"), psh[:, :, 0:P])
            dve.drain()
            for e in range(4):
                for a in range(4):
                    src = ls[32 * e:32 * e + 32, :, :, a:16:4, e]
                    dst = idx[32 * a:32 * a + 32, :, :].rearrange("p (q e) g -> p q e g", e=4)[:, :, e, :]
                    dve.scalar_tensor_tensor(dst, src[:, :, 1, :], float(P), src[:, :, 0, :], ALU.mult, ALU.add)

        @block.tensor
        def _(pe):
            pe.wait_ge(s_set, 1)
            with pe.Fori(0, BITS // STEPS) as j:
                for n in range(STEPS):
                    pe.wait_ge(s_cnt, j * STEPS + n + 1)
                    pe.matmul(psc[:, 0:1], same[:, :], cnt[:, 0:1], start=True, stop=True).then_inc(s_sum, 1)
            pe.wait_ge(s_set, 2)
            pe.wait_ge(s_ge, 1)
            pe.matmul(psc[:, 1:2], same[:, :], cnt[:, 0:1], start=True, stop=True)
            pe.matmul(psc[:, 2:3], lower[:, :], cnt[:, 1:2], start=True, stop=True).then_inc(s_tot, 1)
            pe.wait_ge(s_cs, 1)
            pe.matmul(psc[:, 3:4], lower[:, :], rk[:, T // SEG - 1:T // SEG], start=True, stop=True).then_inc(s_off, 1)
            pe.wait_ge(s_v, 1)
            for t in range(ST):
                last = pe.transpose(psh[:, t // 4, (t % 4) * P:(t % 4 + 1) * P], rk[:, t * P:(t + 1) * P],
                                    k["ident"][:, :])
            last.then_inc(s_vt, 1)
            pe.wait_ge(s_oh[0], 1)
            for g in range(4):
                pe.matmul(psh[:, g, 0:P], zz[:, :], zz[:, :], start=True, stop=False)
            pe.wait_ge(s_w, 64)

            def add_tiles(j):
                for n in range(TILES):
                    u, before = n % BUFS, j * (TILES // BUFS) + n // BUFS
                    pe.wait_ge(s_oh[u], before + 1)
                    pe.wait_ge(s_ov[u], before + 1)
                    for g in range(4):
                        last = pe.matmul(psh[:, g, 0:P],
                                         oa[:, u, 4 * g:4 * g + 4, :].rearrange("p e b -> p (e b)"),
                                         ov[:, u, :, :, 4 * g:4 * g + 4].rearrange("p v a e -> p (v a) e"),
                                         start=False, stop=False)
                    last.then_inc(s_li[u], 1)
                    if n < HT:
                        if after_first(j) or n > 1:
                            pe.wait_ge(s_gel, HT * j + n - 1)
                        pe.matmul(psu[:, n % 2, :], w1[:, n * P:(n + 1) * P], x2T[:, bass.ds(j * CH, CH)],
                                  start=True, stop=True).then_inc(s_hid, 1)
                    for t in {HT + 1: (0,), HT + 2: (1,), HT + 3: (2, 3)}.get(n, ()):
                        if t == 0:
                            pe.wait_ge(s_gel, HT * (j + 1))
                            if after_first(j):
                                pe.wait_ge(s_ev, j)
                        for m in range(HT):
                            last = pe.matmul(pso[:, t * P:(t + 1) * P], hs[:, m, t * P:(t + 1) * P], w2[:, m, :],
                                             start=(m == 0), stop=(m == HT - 1))
                        if t == CT - 1:
                            last.then_inc(s_out, 1)

            add_tiles(0)
            with pe.Fori(1, NT // TILES) as j:
                add_tiles(j)
            for g in range(4):
                last = pe.matmul(psh[:, g, 0:P], zz[:, :], zz[:, :], start=False, stop=True)
            last.then_inc(s_end, 1)


def experts_choice(nc, k, d, idx, xrows, x2T, ybuf, shared):
    NE2 = E0 // 2
    NW, NS = 4, 4
    with Stage(nc, "moe") as s:
        w1 = s.sb("w1", [P, 2, H])
        w2 = s.sb("w2", [P, 2, HT, C])
        b1 = s.sb("b1", [P, 2, HT])
        b2 = s.sb("b2", [P, 2, C])
        w1s = s.sb("w1s", [P, H])
        w2s = s.sb("w2s", [P, HT, C])
        b1s = s.sb("b1s", [P, HT])
        b2s = s.sb("b2s", [P, C])
        idg = s.sb("idg", [P, 2, CT], I32)
        ids = s.sb("ids", [P, 2, CT], I32)
        xg = s.sb("xg", [P, 2, CT, ROW])
        gw = s.sb("gw", [P, 2, CT])
        xT = s.sb("xT", [P, 2, CH])
        hs = s.sb("hs", [P, 2, HT, CH])
        yo = s.sb("yo", [P, 2, CT, C])
        psx = s.pb("psx", [P, 512])
        psh = s.pb("psh", [P, 4, 512])
        pso = s.pb("pso", [P, 2, 512])
        S = {n: s.sem2(n) for n in ("w", "x", "add")}
        s_ws, s_T, s_xT, s_out, s_y, s_outs, s_ev, s_tick = (
            s.sem(n) for n in ("ws", "T", "xT", "out", "y", "outs", "ev", "tick"))
        s_hid = [s.sem(f"hid{n}") for n in range(HT)]
        s_gel = [s.sem(f"gel{n}") for n in range(HT)]
        block = s.block()

        @block.sync
        def _(sp):
            def load(e, u):
                for dst, src in (
                    (w1[:, u, :], d["w1"][e, :, :].rearrange("a c h -> (a c) h")),
                    (w2[:, u, :, :], d["w2"][e, :, :].rearrange("a (k p) c -> p (a k) c", p=P)),
                    (b1[:, u, :], d["b1"][e, :].rearrange("a (k p) -> p (a k)", p=P)),
                    (b2[:, u, :], bc(d["b2"][e, :], 0, P).rearrange("q a c -> q (a c)")),
                ):
                    sp.dma_start(dst, src, allow_slow_non_contiguous=True).then_inc(S["w"][u], 16)

            load(slice(0, 1), 0)
            for dst, src in ((w1s[:, :], d["sw1"]), (w2s[:, :, :], d["sw2"].rearrange("(k p) c -> p k c", p=P)),
                             (b1s[:, :], d["sb1"].rearrange("(k p) -> p k", p=P)), (b2s[:, :], bc(d["sb2"], 0, P))):
                sp.dma_start(dst, src, allow_slow_non_contiguous=True).then_inc(s_ws, 16)
            load(slice(1, 2), 1)
            with sp.Fori(0, NE2 - 1) as j:
                for u in range(2):
                    sp.wait_ge(s_y, 2 * j + u + 1)
                    load(bass.ds(2 * j + 2 + u, 1), u)

        @block.gpsimd
        def _(pool):
            def gather(i, u):
                pool.tensor_copy(idg[:, u, :], idx[:, bass.ds(i, 1), :].rearrange("p a g -> p (a g)"))
                pool.drain()
                for t in range(CT):
                    pool.indirect_dma_start(xg[:, u, t, :], None, xrows,
                                            bass.IndirectOffsetOnAxis(ap=idg[:, u, t:t + 1], axis=0))\
                        .then_inc(S["x"][u], 16)

            for u in range(2):
                gather(u, u)

            def step(j, more):
                for u in range(2):
                    i = 2 * j + u
                    if more:
                        wait_alone(pool, s_xT, i + 1, s_tick)
                        gather(i + 2, u)
                    wait_alone(pool, s_y, i + 1, s_tick)
                    if u == 1 or after_first(j):
                        wait_alone(pool, S["add"][1 - u], (j + u) * 16 * CT, s_tick)
                    pool.tensor_copy(ids[:, u, :], idx[:, bass.ds(i, 1), :].rearrange("p a g -> p (a g)"))
                    pool.drain()
                    for t in range(CT):
                        pool.indirect_dma_start(ybuf, bass.IndirectOffsetOnAxis(ap=ids[:, u, t:t + 1], axis=0),
                                                yo[:, u, t, :], None, compute_op=ALU.add).then_inc(S["add"][u], 16)

            pairs(pool, step, NE2)
            for u in range(2):
                pool.wait_ge(S["add"][u], NE2 * 16 * CT)

        @block.scalar
        def _(act):
            act.wait_ge(s_ws, 16 * NS)
            with act.Fori(0, NE2) as j:
                for u in range(2):
                    act.wait_ge(S["w"][u], (j + 1) * 16 * NW)
                    for use, q, bias in ((0, 0, b1[:, 0, :]), (1, 1, b1s)) if u == 0 else ((2, 0, b1[:, 1, :]),):
                        for m in range(HT):
                            act.wait_ge(s_hid[m], 3 * j + use + 1)
                            act.activation(hs[:, q, m, :], psh[:, m, :], ACT.Gelu_apprx_tanh, bias=bias[:, m:m + 1])\
                                .then_inc(s_gel[m], 1)

        @block.vector
        def _(dve):
            def evacuate(i, u):
                dve.wait_ge(s_T, i + 1)
                dve.tensor_copy(xT[:, u, :], psx[:, :])
                dve.drain()
                dve.tensor_copy(gw[:, u, :], xg[:, u, :, bass.ds(C + i, 1)].rearrange("p t a -> p (t a)"))\
                    .then_inc(s_xT, 1)

            dve.wait_ge(s_ws, 16 * NS)
            evacuate(0, 0)

            def step(j, more):
                for u in range(2):
                    i = 2 * j + u
                    if more or u == 0:
                        evacuate(i + 1, 1 - u)
                    dve.wait_ge(s_out, i + 1)
                    if after_first(j):
                        dve.wait_ge(S["add"][u], j * 16 * CT)
                    dve.tensor_tensor(yo[:, u, :, :], pso[:, 0, :].rearrange("p (t c) -> p t c", c=C),
                                      bc(b2[:, u, :], 1, CT), ALU.add)
                    dve.drain()
                    for t in range(CT):
                        last = dve.tensor_scalar(yo[:, u, t, :], yo[:, u, t, :], gw[:, u, t:t + 1], None, ALU.mult)
                    last.then_inc(s_y, 1)
                    if u == 0:
                        dve.wait_ge(s_outs, j + 1)
                        dve.tensor_tensor(shared[:, bass.ds((NE2 + j) * CT, CT), :],
                                          pso[:, 1, :].rearrange("p (t c) -> p t c", c=C), bc(b2s[:, :], 1, CT),
                                          ALU.add).then_inc(s_ev, 1)

            pairs(dve, step, NE2)

        @block.tensor
        def _(pe):
            def gathered(i, j, u):
                pe.wait_ge(S["x"][u], (j + 1) * 16 * CT)
                for t in range(CT):
                    last = pe.transpose(psx[:, t * P:(t + 1) * P], xg[:, u, t, 0:C], k["ident"][:, :])
                last.then_inc(s_T, 1)

            def up(w, x, j, use):
                for m in range(HT):
                    if use > 0 or after_first(j):
                        pe.wait_ge(s_gel[m], 3 * j + use)
                    pe.matmul(psh[:, m, :], w[:, m * P:(m + 1) * P], x, start=True, stop=True).then_inc(s_hid[m], 1)

            def down(q, w, j, use, done):
                for m in range(HT):
                    pe.wait_ge(s_gel[m], 3 * j + use + 1)
                for t in range(CT):
                    for m in range(HT):
                        last = pe.matmul(pso[:, q, t * P:(t + 1) * P], hs[:, q, m, t * P:(t + 1) * P], w[:, m, :],
                                         start=(m == 0), stop=(m == HT - 1))
                last.then_inc(done, 1)

            gathered(0, 0, 0)
            pe.wait_ge(s_ws, 16 * NS)

            def step(j, more):
                for u in range(2):
                    i = 2 * j + u
                    pe.wait_ge(S["w"][u], (j + 1) * 16 * NW)
                    pe.wait_ge(s_xT, i + 1)
                    up(w1[:, u, :], xT[:, u, :], j, 2 * u)
                    if u == 0:
                        up(w1s, x2T[:, bass.ds((NE2 + j) * CH, CH)], j, 1)
                    if more or u == 0:
                        gathered(i + 1, j + u, 1 - u)
                    if u == 1 or after_first(j):
                        pe.wait_ge(s_y, i)
                    down(0, w2[:, u, :, :], j, 2 * u, s_out)
                    if u == 0:
                        if after_first(j):
                            pe.wait_ge(s_ev, j)
                        down(1, w2s, j, 1, s_outs)

            pairs(pe, step, NE2)




NH, HD = 8, C // 8
KD = 9
E1 = 8
CAP1 = 2560
ROW1 = C + 1 + E1
DUMP = E1 * CAP1


def attention_block(nc, k, d, shared, ybuf, table, ybuf2):
    PT = 2 * UT
    NP = NU // 2
    BAND = 3 * P
    with Stage(nc, "att") as s:
        wq = s.sb("wq", [P, 3 * C])
        bq = s.sb("bq", [P, 3 * C])
        wd = s.sb("wd", [P, NH, KD])
        band = s.sb("band", [P, NH, BAND])
        wp = s.sb("wp", [P, C])
        bp = s.sb("bp", [P, C])
        wr = s.sb("wr", [P, E1])
        br = s.sb("br", [P, E1])
        eps = s.sb("eps", [P, 1])
        mask = s.sb("mask", [P, P])
        h3 = s.sb("h3", [P, 2, UT, C])
        ht = s.sb("ht", [P, 2, UT, C])
        xa = s.sb("xa", [P, 2, UT, C])
        xb = s.sb("xb", [P, 2, UT, C])
        xT = s.sb("xT", [P, 2, UNIT])
        qk = s.sb("qk", [P, 2, UT, 2 * C])
        sq = s.sb("sq", [P, 2, UT, 2 * C])
        rr = s.sb("rr", [P, 2, UT, 2 * NH])
        v = s.sb("v", [P, 2, UT, C])
        qT = s.sb("qT", [P, 2, UNIT])
        am = s.sb("am", [P, 2, UB, P])
        on = s.sb("on", [P, 2, UT, C])
        ro = s.sb("ro", [P, 2, UT, NH])
        bs = s.sb("bs", [P, 2, UT, 6])
        ba1, ba2 = s.sb("ba1", [P, 2, UT, 2]), s.sb("ba2", [P, 2, UT, 2])
        rb1, rb2 = s.sb("rb1", [P, 2, UT]), s.sb("rb2", [P, 2, UT])
        nb1, nb2 = s.sb("nb1", [P, 2, UT]), s.sb("nb2", [P, 2, UT])
        cT, x4T = xT, qT
        lg = s.sb("lg", [P, PT, E1])
        pr, one1, one2, tmp = (s.sb(n, [P, PT, E1]) for n in ("prb", "one1", "one2", "tmp"))
        both, run, reset = (s.sb(n, [P, E1, PT]) for n in ("both", "run", "reset"))
        carry, more8 = s.sb("carry", [P, E1]), s.sb("more8", [P, E1])
        rank, base = s.sb("rank", [P, E1]), s.sb("base", [P, E1])
        ranki, basei = s.sb("ranki", [P, E1], I32), s.sb("basei", [P, E1], I32)
        top = s.sb("top", [P, 2, PT])
        f, wf = s.sb("f", [P, PT]), s.sb("wf", [P, PT])
        wtmp = s.sb("wtmp", [P, PT, E1])
        minus = s.sb("minus", [P, PT])
        kp, slot, num, dump = (s.sb(n, [P, 2, PT]) for n in ("kp", "slot", "num", "dump"))
        numi, sloti = s.sb("numi", [P, 2, PT], I32), s.sb("sloti", [P, 2, PT], I32)
        before = s.sb("before", [P, P])
        rows_out = s.sb("rows", [P, PT, ROW1])
        ps = s.pb("ps", [P, 2, 4, 512])
        names = ("ld", "h3", "bn", "sd", "rb", "xn", "Tx", "xT", "QK", "qk", "sq", "ssq", "rt", "kn", "V", "v",
                 "Tq", "qT", "at", "am", "dc", "o", "o2", "osq", "oss", "ro", "on", "To", "cT", "pr", "h4", "hb", "bn2",
                 "sd2", "rb2", "x4", "x4c", "T4", "x4T", "lg", "lgc", "sy")
        S = {n: s.sem2(n) for n in names}
        s_in, s_tick, s_mask, s_zero, s_band = (s.sem(n) for n in ("in", "tick", "mask", "zero", "band"))
        s_sub, s_exp, s_run, s_pos, s_posr, s_row, s_put = (
            s.sem(n) for n in ("sub", "exp", "run", "pos", "posr", "row", "put"))
        ps_pos = ps[:, 1, 3, 0:E1 * PT]
        block = s.block()
        flat = lambda ap: ap.rearrange("p a b -> p (a b)")
        bank = lambda u, n, m=2: ps[:, u, n:n + m, :].rearrange("p a b -> p (a b)")
        NIN = 8

        def rows(t, j, u):
            return t[bass.ds(j * 2 * UNIT + u * UNIT, UNIT), :].rearrange("(t p) c -> p t c", p=P)

        @block.sync
        def _(sp):
            for dst, src in (
                (wq[:, :], d["w_qkv"]), (bq[:, :], bc(d["b_qkv"], 0, P)),
                (wd[:, :, :], bc(d["w_dconv"].rearrange("h a k b -> h (a k b)"), 0, P)),
                (wp[:, :], d["w_proj"]), (bp[:, :], bc(d["b_proj"], 0, P)), (wr[:, :], d["Wr"]),
                (br[:, :], bc(d["br"], 0, P)),
            ):
                sp.dma_start(dst, src, allow_slow_non_contiguous=True).then_inc(s_in, 16)
            for u in range(2):
                sp.dma_start(h3[:, u, :, :], rows(ybuf, 0, u)).then_inc(S["ld"][u], 16)

            def step(j, more):
                if more:
                    for u in range(2):
                        sp.wait_ge(S["hb"][u], j + 1)
                        sp.dma_start(h3[:, u, :, :], rows(ybuf, j + 1, u)).then_inc(S["ld"][u], 16)
                for u in range(2):
                    sp.wait_ge(S["h4"][u], j + 1)
                    sp.dma_start(rows(ybuf2, j, u), ht[:, u, :, :]).then_inc(S["sy"][u], 16)

            pairs(sp, step)
            for u in range(2):
                sp.wait_ge(S["sy"][u], 16 * NP)

        @block.scalar
        def _(act):
            act.wait_ge(s_in, 16 * (NIN - 1))

            def deviations(ready, j, ba, rb, done):
                for u in range(2):
                    act.wait_ge(ready[u], j + 1)
                    act.activation(rb[:, u, :], ba[:, u, :, 1], ACT.Sqrt, bias=eps[:, 0:1]).then_inc(done[u], 1)

            def normalize(ready, j, dst, src, rb, nb, done):
                act.wait_ge(ready[0], j + 1)
                for t in range(UT):
                    last = act.activation(dst[:, 0, t, :], src[:, 0, t, :], ACT.Identity, scale=rb[:, 0, t:t + 1],
                                          bias=nb[:, 0, t:t + 1])
                last.then_inc(done[0], 1)

            def copies(ready, j, dst, done):
                for u in range(2):
                    act.wait_ge(ready[u], j + 1)
                    act.activation(dst[:, u, :], bank(u, 0), ACT.Copy).then_inc(done[u], 1)

            act.wait_ge(s_zero, 1)
            deviations(S["bn"], 0, ba1, rb1, S["sd"])
            normalize(S["rb"], 0, xa, h3, rb1, nb1, S["xn"])
            copies(S["Tx"], 0, xT, S["xT"])

            def step(j, more):
                for u in range(2):
                    act.wait_ge(S["qk"][u], j + 1)
                    act.activation(sq[:, u, :, :], qk[:, u, :, :], ACT.Square).then_inc(S["sq"][u], 1)
                for u in range(2):
                    act.wait_ge(S["ssq"][u], j + 1)
                    act.activation(rr[:, u, :, :], rr[:, u, :, :], ACT.Sqrt).then_inc(S["rt"][u], 1)
                for u in range(2):
                    act.wait_ge(S["Tq"][u], j + 1)
                    act.activation(qT[:, u, :], bank(u, 0), ACT.Copy).then_inc(S["qT"][u], 1)
                for u in range(2):
                    act.wait_ge(S["o2"][u], j + 1)
                    act.activation(sq[:, u, :, 0:C], on[:, u, :, :], ACT.Square).then_inc(S["osq"][u], 1)
                for u in range(2):
                    act.wait_ge(S["oss"][u], j + 1)
                    act.activation(ro[:, u, :, :], ro[:, u, :, :], ACT.Sqrt).then_inc(S["ro"][u], 1)
                for u in range(2):
                    act.wait_ge(S["To"][u], j + 1)
                    act.activation(cT[:, u, :], bank(u, 0), ACT.Copy).then_inc(S["cT"][u], 1)
                deviations(S["bn2"], j, ba2, rb2, S["sd2"])
                if more:
                    deviations(S["bn"], j + 1, ba1, rb1, S["sd"])
                if after_first(j):
                    act.wait_ge(S["x4c"][0], j)
                normalize(S["rb2"], j, xb, ht, rb2, nb2, S["x4"])
                if more:
                    normalize(S["rb"], j + 1, xa, h3, rb1, nb1, S["xn"])
                copies(S["T4"], j, x4T, S["x4T"])
                act.wait_ge(s_sub, j + 1)
                act.activation(pr[:, :, :], pr[:, :, :], ACT.Exp).then_inc(s_exp, 1)
                if more:
                    copies(S["Tx"], j + 1, xT, S["xT"])

            pairs(act, step)

        @block.gpsimd
        def _(pool):
            pool.memset(before[:, :], 1.0)
            pool.memset(minus[:, :], -1.0)
            pool.memset(reset[:, :, :], 1.0)
            pool.memset(carry[:, :], 0.0)
            pool.iota(ranki[:, :], pattern=[[-1, E1]], base=E1, channel_multiplier=0)
            pool.iota(basei[:, :], pattern=[[CAP1, E1]], base=0, channel_multiplier=0)
            pool.iota(numi[:, :, :], pattern=[[T, 2], [P, PT]], base=0, channel_multiplier=1)
            pool.drain()
            pool.memset(reset[:, :, 0:1], 0.0)
            pool.affine_select(out=before[:, :], in_=before[:, :], compare_op=ALU.is_gt, fill=0.0, base=0,
                               pattern=[[1, P]], channel_multiplier=-1)
            pool.tensor_copy(rank[:, :], ranki[:, :])
            pool.tensor_copy(base[:, :], basei[:, :])
            pool.tensor_copy(num[:, :, :], numi[:, :, :])
            pool.memset(band[:, :, :], 0.0)
            pool.memset(eps[:, :], 1e-5)
            pool.memset(mask[:, :], 1.0 / PI).then_inc(s_zero, 1)
            pool.drain()
            blocks = mask[:, :].rearrange("p (h e) -> p h e", e=HD)
            pool.affine_select(out=blocks, in_=blocks, compare_op=ALU.is_ge, fill=0.0, base=0,
                               pattern=[[-HD, NH], [0, HD]], channel_multiplier=1)
            pool.drain()
            pool.affine_select(out=blocks, in_=blocks, compare_op=ALU.is_ge, fill=0.0, base=HD - 1,
                               pattern=[[HD, NH], [0, HD]], channel_multiplier=-1).then_inc(s_mask, 1)
            pool.wait_ge(s_in, 16 * (NIN - 1))

            def residual(j, u):
                wait_alone(pool, S["ld"][u], (j + 1) * 16, s_tick)
                pool.tensor_tensor(h3[:, u, :, :], h3[:, u, :, :],
                                   shared[:, bass.ds(j * 2 * UT + u * UT, UT), :], ALU.add).then_inc(S["h3"][u], 1)

            for u in range(2):
                residual(0, u)

            def step(j, more):
                for u in range(2):
                    wait_alone(pool, S["xn"][u], j + 1, s_tick)
                    if after_first(j):
                        wait_alone(pool, S["sy"][u], j * 16, s_tick)
                    pool.tensor_tensor(ht[:, u, :, :], h3[:, u, :, :], bc(bp[:, :], 1, UT), ALU.add)\
                        .then_inc(S["hb"][u], 1)
                if more:
                    for u in range(2):
                        residual(j + 1, u)
                if after_first(j):
                    scatter(j - 1)
                for u in range(2):
                    wait_alone(pool, S["x4"][u], j + 1, s_tick)
                    if u == 0 and after_first(j):
                        wait_alone(pool, s_put, j * 16 * 2 * PT, s_tick)
                    pool.tensor_copy(rows_out[:, u * UT:(u + 1) * UT, 0:C], xb[:, u, :, :]).then_inc(S["x4c"][u], 1)

            te = lambda ap: ap.rearrange("p e t -> p t e")

            def tt(out, a, b, op):
                pool.tensor_tensor(out, a, b, op)
                pool.drain()

            def normed():
                tt(wf[:, :], top[:, 0, :], top[:, 1, :], ALU.add)
                pool.tensor_scalar(wf[:, :], wf[:, :], 1e-9, None, ALU.add)
                pool.drain()
                tt(wf[:, :], wf[:, :], minus[:, :], ALU.pow)
                tt(top[:, :, :], top[:, :, :], bc(wf[:, :], 1, 2), ALU.mult)

            def scatter(j):
                wait_alone(pool, s_posr, j + 1, s_tick)
                pool.tensor_tensor(run[:, :, :], run[:, :, :], bc(base[:, :], 2, PT), ALU.add)
                tt(top[:, :, :], top[:, :, :], bc(f[:, :], 1, 2), ALU.mult)
                for q, hot in enumerate((one1, one2)):
                    for dst, src in ((kp, both), (slot, run)):
                        tt(wtmp[:, :, :], hot[:, :, :], te(src[:, :, :]), ALU.mult)
                        tt(wtmp[:, :, 0:4], wtmp[:, :, 0:4], wtmp[:, :, 4:8], ALU.add)
                        tt(wtmp[:, :, 0:2], wtmp[:, :, 0:2], wtmp[:, :, 2:4], ALU.add)
                        tt(dst[:, q, :], wtmp[:, :, 0], wtmp[:, :, 1], ALU.add)
                tt(top[:, :, :], top[:, :, :], kp[:, :, :], ALU.mult)
                pool.tensor_scalar(dump[:, :, :], num[:, :, :], float(DUMP), None, ALU.add)
                pool.drain()
                tt(slot[:, :, :], slot[:, :, :], dump[:, :, :], ALU.subtract)
                tt(slot[:, :, :], slot[:, :, :], kp[:, :, :], ALU.mult)
                tt(slot[:, :, :], slot[:, :, :], dump[:, :, :], ALU.add)
                normed()
                for q, hot in enumerate((one1, one2)):
                    tt(hot[:, :, :], hot[:, :, :], bc(top[:, q, :], 2, E1), ALU.mult)
                pool.tensor_copy(sloti[:, :, :], slot[:, :, :])
                pool.tensor_copy(rows_out[:, :, C], num[:, 0, :])
                pool.tensor_tensor(rows_out[:, :, C + 1:ROW1], one1[:, :, :], one2[:, :, :], ALU.add)\
                    .then_inc(s_row, 1)
                pool.drain()
                pool.tensor_scalar(num[:, :, :], num[:, :, :], float(2 * UNIT), None, ALU.add)
                for t in range(PT):
                    for q in range(2):
                        pool.indirect_dma_start(table, bass.IndirectOffsetOnAxis(ap=sloti[:, q, t:t + 1], axis=0),
                                                rows_out[:, t, :], None).then_inc(s_put, 16)

            pairs(pool, step)
            scatter(NP - 1)
            pool.wait_ge(s_put, NP * 16 * 2 * PT)

        @block.vector
        def _(dve):
            def norm_stats(src, u, ba, done):
                for t in range(UT):
                    dve.bn_stats(bs[:, u, t, :], src[:, u, t, :])
                dve.drain()
                for t in range(UT):
                    last = dve.bn_aggr(ba[:, u, t, :], bs[:, u, t, :])
                last.then_inc(done[u], 1)

            def input_stats(j):
                for u in range(2):
                    dve.wait_ge(S["h3"][u], j + 1)
                    norm_stats(h3, u, ba1, S["bn"])

            def norm_factors(ready, j, ba, rb, nb, done):
                for u in range(2):
                    dve.wait_ge(ready[u], j + 1)
                    dve.reciprocal(rb[:, u, :], rb[:, u, :])
                    dve.drain()
                    dve.scalar_tensor_tensor(nb[:, u, :], ba[:, u, :, 0], -1.0, rb[:, u, :], ALU.mult, ALU.mult)\
                        .then_inc(done[u], 1)

            def normalize(dst, src, ba, rb, done):
                for t in range(UT):
                    last = dve.tensor_scalar(dst[:, 1, t, :], src[:, 1, t, :], ba[:, 1, t, 0:1], rb[:, 1, t:t + 1],
                                             ALU.subtract, ALU.mult)
                last.then_inc(done[1], 1)

            heads = lambda ap: ap.rearrange("p t (h e) -> p (t h) e", e=HD)
            dve.wait_ge(s_in, 16 * (NIN - 1))
            dve.wait_ge(s_mask, 1)
            for n in range(KD):
                o = P + KD // 2 - n
                for h in range(NH):
                    last = dve.scalar_tensor_tensor(band[:, h, o:o + P], k["ident"][:, :], wd[:, h, n:n + 1],
                                                    band[:, h, o:o + P], ALU.mult, ALU.add)
                dve.drain()
            last.then_inc(s_band, 1)
            input_stats(0)
            norm_factors(S["sd"], 0, ba1, rb1, nb1, S["rb"])
            normalize(xa, h3, ba1, rb1, S["xn"])

            def step(j, more):
                for u in range(2):
                    dve.wait_ge(S["QK"][u], j + 1)
                    dve.tensor_tensor(qk[:, u, :, :], bank(u, 0, 4).rearrange("p (t n) -> p t n", n=2 * C),
                                      bc(bq[:, 0:2 * C], 1, UT), ALU.add).then_inc(S["qk"][u], 1)
                for u in range(2):
                    dve.wait_ge(S["V"][u], j + 1)
                    dve.tensor_tensor(v[:, u, :, :], bank(u, 0).rearrange("p (t n) -> p t n", n=C),
                                      bc(bq[:, 2 * C:3 * C], 1, UT), ALU.add).then_inc(S["v"][u], 1)
                    dve.wait_ge(S["sq"][u], j + 1)
                    dve.tensor_reduce(rr[:, u, :, :].rearrange("p t h -> p (t h)"), heads(sq[:, u, :, :]), AX,
                                      ALU.add).then_inc(S["ssq"][u], 1)
                for u in range(2):
                    dve.wait_ge(S["rt"][u], j + 1)
                    dve.reciprocal(rr[:, u, :, :], rr[:, u, :, :])
                    dve.drain()
                    kk = qk[:, u, :, C:2 * C].rearrange("p t (h e) -> p t h e", e=HD)
                    dve.tensor_tensor(kk, kk, bc(rr[:, u, :, NH:2 * NH], 3, HD), ALU.mult).then_inc(S["kn"][u], 1)
                for u in range(2):
                    dve.wait_ge(S["at"][u], j + 1)
                    dve.tensor_tensor(am[:, u, :, :], bank(u, 2, 1).rearrange("p (b n) -> p b n", n=P),
                                      bc(mask[:, :], 1, UB), ALU.mult).then_inc(S["am"][u], 1)
                for u in range(2):
                    dve.wait_ge(S["o"][u], j + 1)
                    dve.tensor_tensor(on[:, u, :, :].rearrange("p t (h e) -> p t h e", e=HD),
                                      bank(u, 0).rearrange("p (t h e) -> p t h e", e=HD, h=NH),
                                      bc(rr[:, u, :, 0:NH], 3, HD), ALU.mult)
                    dve.drain()
                    dve.scalar_tensor_tensor(on[:, u, :, :], v[:, u, :, :], 0.5, on[:, u, :, :], ALU.mult,
                                             ALU.add).then_inc(S["o2"][u], 1)
                for u in range(2):
                    dve.wait_ge(S["osq"][u], j + 1)
                    dve.tensor_reduce(ro[:, u, :, :], sq[:, u, :, 0:C].rearrange("p t (h e) -> p t h e", e=HD), AX,
                                      ALU.add).then_inc(S["oss"][u], 1)
                for u in range(2):
                    dve.wait_ge(S["ro"][u], j + 1)
                    oo = on[:, u, :, :].rearrange("p t (h e) -> p (t h) e", e=HD)
                    dve.reciprocal(ro[:, u, :, :], ro[:, u, :, :])
                    dve.drain()
                    dve.tensor_tensor(oo, oo, bc(ro[:, u, :, :].rearrange("p t h -> p (t h)"), 2, HD), ALU.mult)
                    dve.drain()
                    dve.wait_ge(S["dc"][u], j + 1)
                    oo = on[:, u, :, :].rearrange("p t (h e) -> p t h e", e=HD)
                    dve.tensor_tensor(oo, oo, bank(u, 2).rearrange("p (h t e) -> p t h e", e=HD, h=NH), ALU.add)\
                        .then_inc(S["on"][u], 1)
                for u in range(2):
                    dve.wait_ge(S["pr"][u], j + 1)
                    dve.wait_ge(S["hb"][u], j + 1)
                    dve.tensor_tensor(flat(ht[:, u, :, :]), bank(u, 2), flat(ht[:, u, :, :]), ALU.add)\
                        .then_inc(S["h4"][u], 1)
                    dve.drain()
                    norm_stats(ht, u, ba2, S["bn2"])
                if more:
                    input_stats(j + 1)
                norm_factors(S["sd2"], j, ba2, rb2, nb2, S["rb2"])
                if after_first(j):
                    dve.wait_ge(S["x4c"][1], j)
                normalize(xb, ht, ba2, rb2, S["x4"])
                if more:
                    norm_factors(S["sd"], j + 1, ba1, rb1, nb1, S["rb"])
                    normalize(xa, h3, ba1, rb1, S["xn"])
                for u in range(2):
                    dve.wait_ge(S["lg"][u], j + 1)
                    dve.tensor_tensor(lg[:, u * UT:(u + 1) * UT, :],
                                      ps[:, u, 2, 0:UT * E1].rearrange("p (t e) -> p t e", e=E1),
                                      bc(br[:, :], 1, UT), ALU.add).then_inc(S["lgc"][u], 1)
                dve.drain()
                route(j)

            te = lambda ap: ap.rearrange("p e t -> p t e")
            fl = lambda ap: ap.rearrange("p a b -> p (a b)")

            def route(j):
                def tt(out, a, b, op):
                    dve.tensor_tensor(out, a, b, op)
                    dve.drain()

                if after_first(j):
                    dve.wait_ge(s_row, j)
                dve.tensor_reduce(f[:, :], lg[:, :, :], AX, ALU.max)
                dve.drain()
                dve.tensor_tensor(pr[:, :, :], lg[:, :, :], bc(f[:, :], 2, E1), ALU.subtract).then_inc(s_sub, 1)
                dve.wait_ge(s_exp, j + 1)
                dve.tensor_reduce(f[:, :], pr[:, :, :], AX, ALU.add)
                dve.drain()
                dve.reciprocal(f[:, :], f[:, :])
                dve.drain()
                tt(pr[:, :, :], pr[:, :, :], bc(f[:, :], 2, E1), ALU.mult)
                for q, hot in enumerate((one1, one2)):
                    dve.tensor_reduce(top[:, q, :], pr[:, :, :], AX, ALU.max)
                    dve.drain()
                    tt(tmp[:, :, :], pr[:, :, :], bc(top[:, q, :], 2, E1), ALU.is_equal)
                    tt(tmp[:, :, :], tmp[:, :, :], bc(rank[:, :], 1, PT), ALU.mult)
                    dve.tensor_reduce(f[:, :], tmp[:, :, :], AX, ALU.max)
                    dve.drain()
                    tt(hot[:, :, :], tmp[:, :, :], bc(f[:, :], 2, E1), ALU.is_equal)
                    if q == 0:
                        dve.scalar_tensor_tensor(pr[:, :, :], hot[:, :, :], -2.0, pr[:, :, :], ALU.mult, ALU.add)
                        dve.drain()
                tt(te(both[:, :, :]), one1[:, :, :], one2[:, :, :], ALU.add)
                dve.tensor_reduce(more8[:, :], both[:, :, :], AX, ALU.add)
                dve.tensor_tensor_scan(fl(run[:, :, :]), fl(reset[:, :, :]), fl(both[:, :, :]), 0.0, ALU.mult, ALU.add)
                dve.drain()
                tt(run[:, :, :], run[:, :, :], both[:, :, :], ALU.subtract)
                dve.tensor_tensor(run[:, :, :], run[:, :, :], bc(carry[:, :], 2, PT), ALU.add).then_inc(s_run, 1)
                dve.drain()
                dve.tensor_tensor(carry[:, :], carry[:, :], more8[:, :], ALU.add)
                tt(f[:, :], top[:, 0, :], top[:, 1, :], ALU.add)
                dve.tensor_scalar(f[:, :], f[:, :], 1e-9, None, ALU.add)
                dve.drain()
                dve.reciprocal(f[:, :], f[:, :])
                pos = ps_pos.rearrange("p (e t) -> p e t", t=PT)
                dve.wait_ge(s_pos, j + 1)
                dve.tensor_scalar(both[:, :, :], pos, float(CAP1), None, ALU.is_lt)
                dve.tensor_copy(run[:, :, :], pos).then_inc(s_posr, 1)

            pairs(dve, step)

        @block.tensor
        def _(pe):
            pe.wait_ge(s_in, 16 * (NIN - 1))
            pe.wait_ge(s_band, 1)
            tile = lambda u, n, t: ps[:, u, n + t // 4, (t % 4) * P:(t % 4 + 1) * P]
            cols = lambda ap, t: ap[:, t * P:(t + 1) * P]

            def transposes(u, n, src, done):
                for t in range(UT):
                    last = pe.transpose(tile(u, n, t), src(t), k["ident"][:, :])
                last.then_inc(done, 1)

            def transpose_input(j):
                for u in range(2):
                    pe.wait_ge(S["xn"][u], j + 1)
                    transposes(u, 0, lambda t: xa[:, u, t, :], S["Tx"][u])

            transpose_input(0)

            def places(j):
                pe.wait_ge(s_run, j + 1)
                pe.matmul(ps_pos, before[:, :], both[:, :, :].rearrange("p e t -> p (e t)"), start=True, stop=False)
                pe.matmul(ps_pos, k["ones"][:, :], run[:, :, :].rearrange("p e t -> p (e t)"), start=False,
                          stop=True).then_inc(s_pos, 1)

            def step(j, more):
                for u in range(2):
                    if u == 1 and after_first(j):
                        places(j - 1)
                        pe.wait_ge(s_posr, j)
                    pe.wait_ge(S["xT"][u], j + 1)
                    if after_first(j):
                        pe.wait_ge(S["lgc"][u], j)
                    for t in range(UT):
                        last = pe.matmul(ps[:, u, t // 2, (t % 2) * 2 * C:(t % 2 + 1) * 2 * C], cols(xT[:, u, :], t),
                                         wq[:, 0:2 * C], start=True, stop=True)
                    last.then_inc(S["QK"][u], 1)
                for u in range(2):
                    pe.wait_ge(S["qk"][u], j + 1)
                    for t in range(UT):
                        last = pe.matmul(tile(u, 0, t), cols(xT[:, u, :], t), wq[:, 2 * C:3 * C], start=True, stop=True)
                    last.then_inc(S["V"][u], 1)
                for u in range(2):
                    pe.wait_ge(S["v"][u], j + 1)
                    transposes(u, 0, lambda t: qk[:, u, t, 0:C], S["Tq"][u])
                for u in range(2):
                    pe.wait_ge(S["kn"][u], j + 1)
                    for b in range(UB):
                        for t in range(2):
                            last = pe.matmul(ps[:, u, 2, b * P:(b + 1) * P], qk[:, u, 2 * b + t, C:2 * C],
                                             v[:, u, 2 * b + t, :], start=(t == 0), stop=(t == 1))
                    last.then_inc(S["at"][u], 1)
                for u in range(2):
                    pe.wait_ge(S["am"][u], j + 1)
                    pe.wait_ge(S["qT"][u], j + 1)
                    for t in range(UT):
                        last = pe.matmul(tile(u, 0, t), cols(qT[:, u, :], t), am[:, u, t // 2, :], start=True, stop=True)
                    last.then_inc(S["o"][u], 1)
                for u in range(2):
                    for h in range(NH):
                        vh = v[:, u, :, h * HD:(h + 1) * HD]
                        vs = vh.rearrange("p (b s) e -> p b s e", s=2)
                        out = bank(u, 2)[:, h * P:(h + 1) * P].rearrange("p (t e) -> p t e", e=HD)
                        outs = out.rearrange("p (b s) e -> p b s e", s=2)
                        pe.matmul(out, band[:, h, P:2 * P], vh, start=True, stop=False)
                        pe.matmul(outs[:, :, 0, :], band[:, h, 0:P], vs[:, :, 1, :], start=False, stop=False)
                        last = pe.matmul(outs[:, :, 1, :], band[:, h, 2 * P:3 * P], vs[:, :, 0, :],
                                         start=False, stop=True)
                    last.then_inc(S["dc"][u], 1)
                for u in range(2):
                    pe.wait_ge(S["on"][u], j + 1)
                    transposes(u, 0, lambda t: on[:, u, t, :], S["To"][u])
                for u in range(2):
                    pe.wait_ge(S["cT"][u], j + 1)
                    for t in range(UT):
                        last = pe.matmul(tile(u, 2, t), cols(cT[:, u, :], t), wp[:, :], start=True, stop=True)
                    last.then_inc(S["pr"][u], 1)
                for u in range(2):
                    pe.wait_ge(S["x4"][u], j + 1)
                    transposes(u, 0, lambda t: xb[:, u, t, :], S["T4"][u])
                for u in range(2):
                    pe.wait_ge(S["x4T"][u], j + 1)
                    for t in range(UT):
                        last = pe.matmul(ps[:, u, 2, t * E1:(t + 1) * E1], cols(x4T[:, u, :], t), wr[:, :],
                                         start=True, stop=True)
                    last.then_inc(S["lg"][u], 1)
                if more:
                    transpose_input(j + 1)

            pairs(pe, step)
            places(NP - 1)


def top2_experts(nc, k, d, table, ybuf2, out):
    NC1 = CAP1 // CH
    NE2 = E1 // 2
    BODY = 2 * NC1
    HALF = BODY // 2
    NW = 4
    with Stage(nc, "mo2") as s:
        w1 = s.sb("w1", [P, 2, H])
        w2 = s.sb("w2", [P, 2, HT, C])
        b1 = s.sb("b1", [P, 2, HT])
        b2 = s.sb("b2", [P, 2, C])
        xg = s.sb("xg", [P, 2, CT, ROW1])
        ids = s.sb("ids", [P, BODY, CT], I32)
        gw = s.sb("gw", [P, BODY, CT])
        xT = s.sb("xT", [P, 2, CH])
        hs = s.sb("hs", [P, 2, HT, CH])
        yo = s.sb("yo", [P, 2, CT, C])
        psx = s.pb("psx", [P, 512])
        psh = s.pb("psh", [P, 4, 512])
        pso = s.pb("pso", [P, 2, 512])
        S = {n: s.sem2(n) for n in ("w", "x", "add")}
        s_T, s_xT, s_out, s_y, s_tick, s_o = (s.sem(n) for n in ("T", "xT", "out", "y", "tick", "o"))
        s_hid = [s.sem(f"hid{n}") for n in range(HT)]
        s_gel = [s.sem(f"gel{n}") for n in range(HT)]
        block = s.block()

        class Piece:

            def __init__(self, j, i):
                j, i = j + i // BODY, i % BODY
                self.i, self.u, self.e, self.first = i, i % 2, i // NC1, i % NC1 == 0
                self.n, self.before, self.expert = j * BODY + i, j * HALF + i // 2, 2 * j + i // NC1
                self.there = not isinstance(j, int) or 0 <= j < NE2
                self.nth = not isinstance(j, int) or self.n > 0
                self.reuse = not isinstance(j, int) or self.n > 1

        @block.sync
        def _(sp):
            def rows(p):
                src = table[bass.ds(p.n * CH, CH), :] if not isinstance(p.n, int) else table[p.n * CH:(p.n + 1) * CH, :]
                sp.dma_start(xg[:, p.u, :, :], src.rearrange("(t p) c -> p t c", p=P)).then_inc(S["x"][p.u], 16)

            def load(expert, e):
                for dst, src in (
                    (w1[:, e, :], d["W1"][bass.ds(expert, 1), :, :].rearrange("a c h -> (a c) h")),
                    (w2[:, e, :, :], d["W2"][bass.ds(expert, 1), :, :].rearrange("a (k p) c -> p (a k) c", p=P)),
                    (b1[:, e, :], d["b1"][bass.ds(expert, 1), :].rearrange("a (k p) -> p (a k)", p=P)),
                    (b2[:, e, :], bc(d["b2"][bass.ds(expert, 1), :], 0, P).rearrange("q a c -> q (a c)")),
                ):
                    sp.dma_start(dst, src, allow_slow_non_contiguous=True).then_inc(S["w"][e], 16)

            rows(Piece(0, 0))
            load(0, 0)
            rows(Piece(0, 1))

            def step(j, more):
                for i in range(BODY):
                    p, later = Piece(j, i), Piece(j, i + 2)
                    if later.there:
                        sp.wait_ge(s_xT, p.n + 1)
                        rows(later)
                    if i % NC1 == 1 and (more or i < NC1):
                        if p.expert > 0 if isinstance(j, int) else True:
                            sp.wait_ge(s_y, p.n - 1)
                        load(p.expert + 1, 1 - p.e)

            pairs(sp, step, NE2)
            for u in range(2):
                sp.wait_ge(S["add"][u], NE2 * HALF * 16 * CT)
            sp.dma_start(out.rearrange("a b c -> (a b) c"), ybuf2[0:T, :]).then_inc(s_o, 16)
            sp.wait_ge(s_o, 16)

        @block.gpsimd
        def _(pool):
            def step(j, more):
                for i in range(BODY):
                    p = Piece(j, i)
                    wait_alone(pool, s_y, p.n + 1, s_tick)
                    if p.first and p.nth:
                        for q in range(2):
                            wait_alone(pool, S["add"][q], (j * HALF + (i + 1 - q) // 2) * 16 * CT, s_tick)
                    for t in range(CT):
                        pool.indirect_dma_start(ybuf2, bass.IndirectOffsetOnAxis(ap=ids[:, i, t:t + 1], axis=0),
                                                yo[:, p.u, t, :], None, compute_op=ALU.add).then_inc(S["add"][p.u], 16)

            pairs(pool, step, NE2)

        @block.scalar
        def _(act):
            with act.Fori(0, NE2) as j:
                for i in range(BODY):
                    p = Piece(j, i)
                    if p.first:
                        act.wait_ge(S["w"][p.e], (j + 1) * 16 * NW)
                    for m in range(HT):
                        act.wait_ge(s_hid[m], p.n + 1)
                        act.activation(hs[:, p.u, m, :], psh[:, m, :], ACT.Gelu, bias=b1[:, p.e, m:m + 1])\
                            .then_inc(s_gel[m], 1)

        @block.vector
        def _(dve):
            def evacuate(p):
                dve.wait_ge(s_T, p.n + 1)
                dve.tensor_copy(xT[:, p.u, :], psx[:, :])
                dve.tensor_copy(ids[:, p.i, :], xg[:, p.u, :, C])
                dve.tensor_copy(gw[:, p.i, :], xg[:, p.u, :, bass.ds(p.expert + C + 1, 1)]
                                .rearrange("p t a -> p (t a)")).then_inc(s_xT, 1)

            def finish(p):
                dve.wait_ge(s_out, p.n + 1)
                if p.reuse:
                    dve.wait_ge(S["add"][p.u], p.before * 16 * CT)
                dve.tensor_tensor(yo[:, p.u, :, :], pso[:, p.u, :].rearrange("p (t c) -> p t c", c=C),
                                  bc(b2[:, p.e, :], 1, CT), ALU.add)
                dve.drain()
                for t in range(CT):
                    last = dve.tensor_scalar(yo[:, p.u, t, :], yo[:, p.u, t, :], gw[:, p.i, t:t + 1], None, ALU.mult)
                last.then_inc(s_y, 1)

            evacuate(Piece(0, 0))

            def step(j, more):
                for i in range(BODY):
                    last, after = Piece(j, i - 1), Piece(j, i + 1)
                    if after.there:
                        evacuate(after)
                    if last.there:
                        finish(last)

            pairs(dve, step, NE2)
            finish(Piece(NE2 - 1, BODY - 1))

        @block.tensor
        def _(pe):
            def gathered(p):
                pe.wait_ge(S["x"][p.u], (p.before + 1) * 16)
                for t in range(CT):
                    last = pe.transpose(psx[:, t * P:(t + 1) * P], xg[:, p.u, t, 0:C], k["ident"][:, :])
                last.then_inc(s_T, 1)

            def up(p, j):
                if p.first:
                    pe.wait_ge(S["w"][p.e], (j + 1) * 16 * NW)
                pe.wait_ge(s_xT, p.n + 1)
                for m in range(HT):
                    if p.nth:
                        pe.wait_ge(s_gel[m], p.n)
                    pe.matmul(psh[:, m, :], w1[:, p.e, m * P:(m + 1) * P], xT[:, p.u, :], start=True,
                              stop=True).then_inc(s_hid[m], 1)

            def down(p):
                if p.reuse:
                    pe.wait_ge(s_y, p.n - 1)
                for m in range(HT):
                    pe.wait_ge(s_gel[m], p.n + 1)
                for t in range(CT):
                    for m in range(HT):
                        last = pe.matmul(pso[:, p.u, t * P:(t + 1) * P], hs[:, p.u, m, t * P:(t + 1) * P],
                                         w2[:, p.e, m, :], start=(m == 0), stop=(m == HT - 1))
                last.then_inc(s_out, 1)

            gathered(Piece(0, 0))

            def step(j, more):
                for i in range(BODY):
                    last, this, after = (Piece(j, i + o) for o in (-1, 0, 1))
                    up(this, j)
                    if after.there:
                        gathered(after)
                    if last.there:
                        down(last)

            pairs(pe, step, NE2)
            down(Piece(NE2 - 1, BODY - 1))


def tower(nc, d, out):
    xrows = nc.dram_tensor("xrows", [T, ROW], F32, kind="Internal").ap()
    ybuf = nc.dram_tensor("ybuf", [T, C], F32, kind="Internal").ap()
    ybuf2 = nc.dram_tensor("ybuf2", [T + CAP1, C], F32, kind="Internal").ap()
    table = nc.dram_tensor("table", [DUMP + 2 * T, ROW1], F32, kind="Internal").ap()
    part = lambda tag: {n[len(tag):]: a for n, a in d.items() if n.startswith(tag)}
    with Stage(nc, "top") as s:
        k = {n: s.sb(n, [P, P]) for n in ("ident", "cent", "mean", "ones", "half_mean")}
        k["nhalf"] = s.sb("nhalf", [P, 64])
        k["half"] = s.sb("half", [P, 64])
        hT = s.sb("hT", [P, T])
        constants(nc, k)
        x2T = s.sb("x2T", [P, T])
        lg = s.sb("lg", [P, NT, E0])
        with Stage(nc, "rec") as rt:
            rec = {"win": rt.sb("win", [P, C]), "bin": rt.sb("bin", [P, 1]), "bc": rt.sb("bcw", [P, 3, P]),
                   "bA": rt.sb("bA", [P, 1]), "bsw": rt.sb("bsw", [P, 1]), "decay": rt.sb("decay", [P, UNIT]),
                   "cos": rt.sb("cos", [P, SEQ]), "sin": rt.sb("sin", [P, SEQ]), "sinr": rt.sb("sinr", [P, SEQ]),
                   "cp": rt.sb("cp", [P, S_]), "cq": rt.sb("cq", [P, S_]), "wout": rt.sb("wout", [S_ + 1, C]),
                   "gate": rt.sb("gate", [P, E0])}
            with Stage(nc, "tok") as st:
                w = {"w1": st.sb("w1", [P, L, 2 * C]), "w2": st.sb("w2", [P, L, 2, C]),
                     "cw": st.sb("cw", [P, L + 1, KC]), "cb": st.sb("cb", [P, L + 1]), "gw": st.sb("gw", [P, L, 2]),
                     "b1": st.sb("b1", [P, L, 2]), "b2": st.sb("b2", [P, L])}
                prepare(nc, k, d["x"], d["L0_tok_emb_table"], d["L0_tok_pos_emb"], hT, w, part("L0_tok_"), rec,
                        {**part("L0_attn_"), "gate_w": d["L0_ffn_gate_w"]})
                convnext_blocks(nc, k, w, hT, table, ybuf2)
            lru_block(nc, k, rec, hT, x2T, lg, xrows, ybuf)
        shared = hT[:, :].rearrange("p (t c) -> p t c", c=C)
        idx = s.sb("idx", [P, E0, CAP0 // P], I32)
        with Stage(nc, "exp") as st:
            pT = st.sb("pT", [P, T // SEG])
            softmax_experts(nc, k, lg, pT, xrows)
            select_tokens(nc, k, part("L0_ffn_"), x2T, pT, idx, shared)
        experts_choice(nc, k, part("L0_ffn_"), idx, xrows, x2T, ybuf, shared)
        attention_block(nc, k, {**part("L1_attn_"), **part("L1_ffn_")}, shared, ybuf, table, ybuf2)
        top2_experts(nc, k, part("L1_ffn_"), table, ybuf2, out)


_INS = ["x"] + ["L0_tok_" + n for n in ("emb_table", "pos_emb", "conv_w", "conv_b", "ln_g", "ln_b", "w1", "b1", "grn_w", "grn_b",
                                        "w2", "b2")] \
    + ["L0_attn_" + n for n in ("ln_w", "ln_b", "W_in", "conv_w", "conv_b", "nu_log", "theta_log", "gamma_log", "B_re",
                                "B_im", "C_re", "C_im", "W_out", "b_out")] \
    + ["L0_ffn_" + n for n in ("gate_w", "w1", "b1", "w2", "b2", "sw1", "sb1", "sw2", "sb2")] \
    + ["L1_attn_" + n for n in ("w_qkv", "b_qkv", "w_dconv", "w_proj", "b_proj")] \
    + ["L1_ffn_" + n for n in ("Wr", "br", "W1", "b1", "W2", "b2")]


def kernel(**inputs):
    import numpy as _np
    import concourse.bacc as _bacc
    from concourse import mybir as _mybir
    from concourse.bass_utils import run_bass_kernel_spmd as _run

    nc = _bacc.Bacc("TRN2", target_bir_lowering=False, num_devices=1)
    arrays, d = {}, {}
    for name in _INS:
        a = _np.ascontiguousarray(inputs[name])
        arrays[f"{name}_dram"] = a
        d[name] = nc.dram_tensor(f"{name}_dram", a.shape, _mybir.dt.from_np(a.dtype), kind="ExternalInput").ap()
    out = nc.dram_tensor("out_dram", (32, SEQ, C), _mybir.dt.from_np(_np.dtype("float32")), kind="ExternalOutput").ap()
    tower(nc, d, out)
    r = _run(nc, [arrays], core_ids=[0])
    return r.results[0]["out_dram"]
```
